# Optimizing a Trainium2 kernel written in Bass

```python
import numpy as np
import jax
import jax.numpy as jnp

def _softmax(x, axis=-1):
    return jax.nn.softmax(x, axis=axis)

def _gelu(x):
    return jax.nn.gelu(x, approximate=True)

def _silu(x):
    return jax.nn.silu(x)

def _sigmoid(x):
    return jax.nn.sigmoid(x)

def _layernorm(x, axis=-1, eps=1e-05):
    m = jnp.mean(x, axis=axis, keepdims=True)
    v = jnp.var(x, axis=axis, keepdims=True)
    return (x - m) / jnp.sqrt(v + eps)

def _scatter_add(tgt, idx, src, axis=0):
    return tgt.at[idx].add(src)

def _segment_sum(src, seg, n):
    return jax.ops.segment_sum(src, seg, n)
kernel_name = 'mk_adj_ffn_d1_adj_r2_de2eab'

def setup_inputs(seed: int=0):
    np.random.seed(seed)
    _w = jnp.asarray

    def _rec_inputs():
        import jax
        import jax.numpy as jnp
        _gk = jax.random.key(seed)
        x = -0.0005207 + 1.001 * jax.random.normal(jax.random.fold_in(_gk, 1), (2048, 128), jnp.float32)
        _w = (1.0 + jnp.arange(2048, dtype=jnp.float32)) ** (-0.5)
        _w = _w / _w.mean()
        _pij = jnp.clip(0.000976562 * _w[:, None] * _w[None, :], 0.0, 1.0)
        _a = jax.random.uniform(jax.random.fold_in(_gk, 2), (2048, 2048)) < _pij
        _a = jnp.logical_or(_a, jnp.swapaxes(_a, -1, -2))
        _a = jnp.logical_or(_a, jnp.eye(2048, dtype=bool))
        _af = _a.astype(jnp.float32)
        _af = _af * jax.random.uniform(jax.random.fold_in(_gk, 3), (2048, 2048), jnp.float32, 0.05, 5.41998)
        adj = _af
        return (x, adj)
    x, adj = _rec_inputs()

    def _L0_gnn_setup():
        import jax, jax.numpy as jnp
        import numpy as np
        N = 4096
        D = 128
        OUT = 128
        AVG_DEG = 32
        key = jax.random.key(seed)
        k1, k2, k3, k4, k5 = jax.random.split(key, 5)
        node_features = jax.random.normal(k1, (N, D), dtype=jnp.float32)
        edge_features = jax.random.normal(k2, (N, N), dtype=jnp.float32)
        u = jax.random.uniform(k3, (N, N), dtype=jnp.float32)
        adj = jnp.where(u < AVG_DEG / N, 1.0, 0.0).astype(jnp.float32)
        stdv = 1.0 / np.sqrt(OUT)
        weight = jax.random.uniform(k4, (2 * D + 1, OUT), minval=-stdv, maxval=stdv, dtype=jnp.float32)
        bias = jax.random.uniform(k5, (OUT,), minval=-stdv, maxval=stdv, dtype=jnp.float32)
        return {'node_features': node_features, 'edge_features': edge_features, 'adj': adj, 'weight': weight, 'bias': bias}
    _L0_gnn_all = _L0_gnn_setup()
    _L0_gnn_in = {k: v for k, v in _L0_gnn_all.items() if k in ('weight', 'bias')}
    del _L0_gnn_all

    def _L0_ffn_setup():
        import jax, jax.numpy as jnp
        import numpy as np
        B, S, H, NH, NE = (4, 512, 128, 4, 4)
        D = H // NH
        EPS = 1e-08

        def layernorm(x, g, b):
            m = jnp.mean(x, axis=-1, keepdims=True)
            v = jnp.mean((x - m) ** 2, axis=-1, keepdims=True)
            return (x - m) / jnp.sqrt(v + EPS) * g + b
        key = jax.random.key(seed)
        ks = jax.random.split(key, 18)
        sc = 0.05
        return {'x': jax.random.normal(ks[0], (B, S, H), jnp.float32), 'hl_w': jax.random.normal(ks[1], (NH, D, H), jnp.float32) * sc, 'hl_b': jax.random.normal(ks[2], (NH, D), jnp.float32) * sc, 'wq': jax.random.normal(ks[3], (NH, NE, D, D), jnp.float32) * sc, 'wk': jax.random.normal(ks[4], (NH, D, D), jnp.float32) * sc, 'wv': jax.random.normal(ks[5], (NH, D, D), jnp.float32) * sc, 'gate_w': jax.random.normal(ks[6], (NH, NE, NE * D), jnp.float32) * sc, 'gate_b': jax.random.normal(ks[7], (NH, NE), jnp.float32) * sc, 'ln_g': jnp.ones((D,), jnp.float32), 'ln_b': jnp.zeros((D,), jnp.float32), 'fc1_w': jax.random.normal(ks[8], (D, D), jnp.float32) * sc, 'fc1_b': jax.random.normal(ks[9], (D,), jnp.float32) * sc, 'fc2_w': jax.random.normal(ks[10], (D, D), jnp.float32) * sc, 'fc2_b': jax.random.normal(ks[11], (D,), jnp.float32) * sc, 'fnorm_g': jnp.ones((D,), jnp.float32), 'fnorm_b': jnp.zeros((D,), jnp.float32), 'fgate_w': jax.random.normal(ks[12], (NH, H), jnp.float32) * sc}
    _L0_ffn_all = _L0_ffn_setup()
    _L0_ffn_in = {k: v for k, v in _L0_ffn_all.items() if k in ('hl_w', 'hl_b', 'wq', 'wk', 'wv', 'gate_w', 'gate_b', 'ln_g', 'ln_b', 'fc1_w', 'fc1_b', 'fc2_w', 'fc2_b', 'fnorm_g', 'fnorm_b', 'fgate_w')}
    del _L0_ffn_all
    return {'x': x, 'adj': adj, 'L0_gnn_weight': _L0_gnn_in['weight'], 'L0_gnn_bias': _L0_gnn_in['bias'], 'L0_ffn_hl_w': _L0_ffn_in['hl_w'], 'L0_ffn_hl_b': _L0_ffn_in['hl_b'], 'L0_ffn_wq': _L0_ffn_in['wq'], 'L0_ffn_wk': _L0_ffn_in['wk'], 'L0_ffn_wv': _L0_ffn_in['wv'], 'L0_ffn_gate_w': _L0_ffn_in['gate_w'], 'L0_ffn_gate_b': _L0_ffn_in['gate_b'], 'L0_ffn_ln_g': _L0_ffn_in['ln_g'], 'L0_ffn_ln_b': _L0_ffn_in['ln_b'], 'L0_ffn_fc1_w': _L0_ffn_in['fc1_w'], 'L0_ffn_fc1_b': _L0_ffn_in['fc1_b'], 'L0_ffn_fc2_w': _L0_ffn_in['fc2_w'], 'L0_ffn_fc2_b': _L0_ffn_in['fc2_b'], 'L0_ffn_fnorm_g': _L0_ffn_in['fnorm_g'], 'L0_ffn_fnorm_b': _L0_ffn_in['fnorm_b'], 'L0_ffn_fgate_w': _L0_ffn_in['fgate_w']}

def reference(x, adj, L0_gnn_weight, L0_gnn_bias, L0_ffn_hl_w, L0_ffn_hl_b, L0_ffn_wq, L0_ffn_wk, L0_ffn_wv, L0_ffn_gate_w, L0_ffn_gate_b, L0_ffn_ln_g, L0_ffn_ln_b, L0_ffn_fc1_w, L0_ffn_fc1_b, L0_ffn_fc2_w, L0_ffn_fc2_b, L0_ffn_fnorm_g, L0_ffn_fnorm_b, L0_ffn_fgate_w):
    import jax
    import jax.numpy as jnp

    def _L0_gnn_ref(node_features, edge_features, adj, weight, bias):
        import jax, jax.numpy as jnp
        import numpy as np
        N = 4096
        D = 128
        OUT = 128
        AVG_DEG = 32
        neighbor_node_features = adj @ node_features
        neighbor_edge_features = jnp.einsum('ij,ji->i', adj, edge_features)[:, None]
        support = jnp.concatenate((node_features, neighbor_node_features, neighbor_edge_features), axis=1)
        return support @ weight + bias

    def _L0_ffn_ref(x, hl_w, hl_b, wq, wk, wv, gate_w, gate_b, ln_g, ln_b, fc1_w, fc1_b, fc2_w, fc2_b, fnorm_g, fnorm_b, fgate_w):
        import jax, jax.numpy as jnp
        import numpy as np
        B, S, H, NH, NE = (4, 512, 128, 4, 4)
        D = H // NH
        EPS = 1e-08

        def layernorm(x, g, b):
            m = jnp.mean(x, axis=-1, keepdims=True)
            v = jnp.mean((x - m) ** 2, axis=-1, keepdims=True)
            return (x - m) / jnp.sqrt(v + EPS) * g + b
        b, s, h = x.shape
        nh, d, _ = wk.shape
        ne = wq.shape[1]
        sx = jnp.einsum('bsh,ndh->bnsd', x, hl_w) + hl_b[None, :, None, :]
        pad = sx == 0
        q = jnp.einsum('bnsd,neod->bneso', sx, wq)
        k = jnp.einsum('bnsd,nod->bnso', sx, wk)
        v = jnp.einsum('bnsd,nod->bnso', sx, wv)
        causal = jnp.where(jnp.tril(jnp.ones((s, s), bool)), 0.0, -jnp.inf).astype(x.dtype)
        scores = jnp.einsum('bnesd,bntd->bnest', q, k) * d ** 0.5 + causal
        att = jax.nn.softmax(scores, axis=-1)
        qkv = jnp.einsum('bnest,bntd->bnesd', att, v)
        qkv = jnp.where(pad[:, :, None], 0.0, qkv)
        out = jnp.transpose(qkv, (0, 1, 3, 2, 4)).reshape(b, nh, s, ne * d)
        gs = jax.nn.softmax(jnp.einsum('bnsf,nef->bnse', out, gate_w) + gate_b[None, :, None, :], axis=-1)
        mixed = jnp.einsum('bnsed,bnse->bnsd', out.reshape(b, nh, s, ne, d), gs)
        resid = sx[jnp.arange(nh), jnp.arange(nh)]
        hn = layernorm(mixed + resid, ln_g, ln_b)
        f_n = jnp.transpose(hn, (0, 2, 1, 3)).reshape(b, s, h)
        fx = f_n.reshape(b, s, nh, d)
        pm = fx == 0
        hx = jnp.where(pm, 0.0, fx @ fc1_w.T + fc1_b)
        hx = jax.nn.relu(hx)
        hx = jnp.where(pm, 0.0, hx @ fc2_w.T + fc2_b)
        hx = layernorm(hx + fx, fnorm_g, fnorm_b)
        fout = hx.reshape(b, s, h)
        fg = jax.nn.softmax(fout @ fgate_w.T, axis=-1)
        return (fout.reshape(b, s, nh, d) * fg[..., None]).reshape(b, s, h)
    x = x + _L0_gnn_ref(_layernorm(x, axis=-1), adj, adj, L0_gnn_weight, L0_gnn_bias)
    x = x + _L0_ffn_ref(_layernorm(x, axis=-1)[None], L0_ffn_hl_w, L0_ffn_hl_b, L0_ffn_wq, L0_ffn_wk, L0_ffn_wv, L0_ffn_gate_w, L0_ffn_gate_b, L0_ffn_ln_g, L0_ffn_ln_b, L0_ffn_fc1_w, L0_ffn_fc1_b, L0_ffn_fc2_w, L0_ffn_fc2_b, L0_ffn_fnorm_g, L0_ffn_fnorm_b, L0_ffn_fgate_w)[0]
    return x

_drawn_inputs = setup_inputs


def setup_inputs(seed=0):
    import zlib

    import numpy as np

    out = dict(_drawn_inputs(seed))
    spreads = {'L0_ffn_ln_g': (1.0, 0.6),
     'L0_ffn_ln_b': (0.0, 0.8),
     'L0_ffn_fnorm_g': (1.0, 0.6),
     'L0_ffn_fnorm_b': (0.0, 0.8)}
    factors = {'L0_gnn_bias': 5.616,
     'L0_ffn_hl_b': 8.0,
     'L0_ffn_wq': 8.0,
     'L0_ffn_wk': 8.0,
     'L0_ffn_wv': 6.446,
     'L0_ffn_gate_w': 8.0,
     'L0_ffn_gate_b': 64.0,
     'L0_ffn_fc1_w': 8.0,
     'L0_ffn_fc1_b': 26.528,
     'L0_ffn_fc2_w': 8.0,
     'L0_ffn_fc2_b': 57.259}
    for name, (base, spread) in spreads.items():
        noise = np.random.default_rng([zlib.crc32(name.encode()), seed]).standard_normal(out[name].shape)
        drawn = base * np.exp(spread * noise) if base else spread * noise
        out[name] = jnp.asarray(drawn.astype(out[name].dtype))
    for name, factor in factors.items():
        out[name] = (out[name] * factor).astype(out[name].dtype)
    return out
```

```python
from contextlib import ExitStack

import concourse.bass as bass
from concourse import mybir

F32 = mybir.dt.float32
F32R = mybir.dt.float32r
BF16 = mybir.dt.bfloat16
ALU = mybir.AluOpType
ACT = mybir.ActivationFunctionType
AX = mybir.AxisListType.X

P = 128
S = 2048
H = 128
NH = 4
NE = 4
D = 32
NT = S // P
NG = 4
GT = NT // NG
GW = S // NG
GNN_EPS = 1e-5
FFN_EPS = 1e-8
NEG = -1e30
KR = 3 * D

SLOTS = [(g, t) for g in range(NG) for t in range(GT * (g + 1))]
NS = len(SLOTS)
STEP_END = [max(i for i, (g, _) in enumerate(SLOTS) if g == gg) for gg in range(NG)]
STEP_START = [min(i for i, (g, _) in enumerate(SLOTS) if g == gg) for gg in range(NG)]
CHUNKS = [(g, c, e, j) for g in range(NG) for c in range(g + 1) for e in range(NE) for j in range(GT)]
NC = len(CHUNKS)
CHUNK_END = [max(i for i, ch in enumerate(CHUNKS) if ch[0] == gg) for gg in range(NG)]
PER_SLOT = NC // NS
LEAD = 18 * PER_SLOT
NP_RING = 4


def chunk_width(g, c, j):
    return (j + 1) * P if c == g else GW


def slot_shift(g, t):
    return max(0, t - GT * g) * P


def build(nc, a, out):
    k_scratch = nc.dram_tensor("k_scratch", (2, NH, D, S), F32, kind="Internal").ap()
    q_scratch = nc.dram_tensor("q_scratch", (2, NH, NE, D, S), F32, kind="Internal").ap()
    sx_scratch = nc.dram_tensor("sx_scratch", (NH, D, S), F32, kind="Internal").ap()
    with ExitStack() as ctx:
        def sb(name, shape, dt=F32):
            return ctx.enter_context(nc.sbuf_tensor(name, shape, dt))

        t = {
            "ident": sb("ident", [P, P]),
            "ident_bf": sb("ident_bf", [P, P], BF16),
            "mask_qk": sb("mask_qk", [P, P], BF16),
            "mask_kq": sb("mask_kq", [P, P], BF16),
            "x1": sb("x1", [P, NT, H]),
            "xn": sb("xn", [P, NT, H]),
        }
        graph(nc, a, t)
        t["sxT"] = sb("sxT", [P, S])
        t["gate_w"] = sb("gate_w", [NH * NE, P])
        t["gate_b"] = sb("gate_b", [P, 1])
        t["fc_w"] = sb("fc_w", [D, 2, P])
        t["fc_b"] = sb("fc_b", [P, 2])
        t["fgate_w"] = sb("fgate_w", [NH, P])
        for name in ("ln_g", "ln_b", "fnorm_g", "fnorm_b"):
            t[name] = sb(name, [P, D])
        t["v_all"] = sb("v_all", [P, NH, NT, D])
        t["heads_out"] = sb("heads_out", [P, NH, S])
        project(nc, a, t, k_scratch, q_scratch, sx_scratch)
        attend(nc, t, k_scratch, q_scratch, sx_scratch)
        finish(nc, a, t, out)


def graph(nc, a, t):
    UNITS, GROUP_END = [], []
    for g in range(NG):
        for c in range(NT):
            UNITS.append((g, c, True))
            if c // GT == g:
                UNITS += [(g2, c, False) for g2 in range(g)]
        GROUP_END.append(len(UNITS) - 1)
    STRIP_RING, COPY_RING = 4, 6
    operands = [u for u, x in enumerate(UNITS) if x[2]]
    operand_no = {u: n for n, u in enumerate(operands)}
    PRODUCTS = [u for u, (g, c, op) in enumerate(UNITS) if not op or c // GT <= g]
    product_no = {u: n for n, u in enumerate(PRODUCTS)}

    with ExitStack() as ctx:
        def sb(name, shape, dt=F32):
            return ctx.enter_context(nc.sbuf_tensor(name, shape, dt))

        def sem(name):
            return ctx.enter_context(nc.semaphore(name))

        adj = sb("adj", [P, NT, S])
        x = sb("x_in", [P, NT, H])
        xn = t["xn"]
        xnT = sb("xnT", [P, S])
        y = sb("y", [P, NT, H])
        copies = sb("copies", [P, COPY_RING, GW])
        junk = sb("junk", [P, 2, GW])
        accT = sb("accT", [P, GW])
        w12 = sb("w12", [P, 2, H])
        w3 = sb("w3", [P, H])
        bias = sb("bias", [P, 1])
        stats = sb("stats", [P, NT, 6])
        mean_var = sb("mean_var", [P, NT, 2])
        var_eps = sb("var_eps", [P, NT])
        std = sb("std", [P, NT])
        rstd = sb("rstd", [P, NT])
        edge_parts = sb("edge_parts", [P, NT, NG])
        edge = sb("edge", [P, NT])
        strips = [ctx.enter_context(nc.psum_tensor(f"strip{i}", [P, GW], F32)) for i in range(STRIP_RING)]
        acc = [ctx.enter_context(nc.psum_tensor(f"acc{i}", [P, GW], F32)) for i in range(2)]
        misc = [ctx.enter_context(nc.psum_tensor(f"misc{i}", [P, GT, P], F32)) for i in range(2)]

        x_in, w_in = sem("x_in_sem"), sem("w_in")
        adj_in = [sem(f"adj_in{g}") for g in range(NG)]
        consts, const_steps = sem("consts"), sem("const_steps")
        dve_chain = sem("dve_chain")
        var_ready, std_ready, xn_ready = sem("var_ready"), sem("std_ready"), sem("xn_ready")
        xnT_full, xnT_ready = sem("xnT_full"), sem("xnT_ready")
        y_full, y_ready = sem("y_full"), sem("y_ready")
        strip_full, strip_copied = sem("strip_full"), sem("strip_copied")
        strip_used, product_done = sem("strip_used"), sem("product_done")
        acc_step, acc_copied = sem("acc_step"), sem("acc_copied")
        h_full, h_used = sem("h_full"), sem("h_used")
        x1_stats = sem("x1_stats")
        block = ctx.enter_context(nc.Block())

        adj_v = a["adj"].rearrange("(i p) j -> i p j", p=P)

        @block.sync
        def _(sp):
            sp.dma_start(x[:], a["x"].rearrange("(i p) d -> p i d", p=P)).then_inc(x_in, 16)
            sp.dma_start(w12[:], a["gnn_weight"][0:2 * H, :].rearrange("(k p) d -> p k d", p=P)).then_inc(w_in, 16)
            sp.dma_start(w3[:], a["gnn_weight"][2 * H, :].partition_broadcast(P)).then_inc(w_in, 16)
            sp.dma_start(bias[:], a["gnn_bias"].rearrange("(p o) -> p o", o=1)).then_inc(w_in, 16)
            for i in range(NT):
                sp.dma_start(adj[:, i, :], adj_v[i]).then_inc(adj_in[i // GT], 16)

        @block.gpsimd
        def _(pool):
            pool.memset(t["ident"][:], 0.0).then_inc(const_steps, 1)
            pool.memset(t["ident_bf"][:], 0.0).then_inc(const_steps, 1)
            pool.memset(t["mask_qk"][:], 0.0).then_inc(const_steps, 1)
            pool.memset(t["mask_kq"][:], 0.0).then_inc(const_steps, 1)
            pool.wait_ge(const_steps, 4)
            for m in (t["ident"], t["ident_bf"]):
                pool.affine_select(out=m[:], in_=m[:], compare_op=ALU.not_equal, fill=1.0, base=0,
                                   pattern=[[-1, P]], channel_multiplier=1).then_inc(consts, 1)
            pool.affine_select(out=t["mask_qk"][:], in_=t["mask_qk"][:], compare_op=ALU.is_ge, fill=NEG, base=0,
                               pattern=[[-1, P]], channel_multiplier=1).then_inc(consts, 1)
            pool.affine_select(out=t["mask_kq"][:], in_=t["mask_kq"][:], compare_op=ALU.is_ge, fill=NEG, base=0,
                               pattern=[[1, P]], channel_multiplier=-1).then_inc(consts, 1)

        @block.vector
        def _(dve):
            chain = [0]

            def link(ins):
                chain[0] += 1
                ins.then_inc(dve_chain, 1)
                dve.wait_ge(dve_chain, chain[0])

            def norm(src, dst, done):
                for i in range(NT):
                    last = dve.bn_stats(stats[:, i, :], src[:, i, :])
                link(last)
                for i in range(NT):
                    last = dve.bn_aggr(mean_var[:, i, :], stats[:, i, :])
                link(last)
                dve.tensor_scalar(var_eps[:], mean_var[:, :, 1], GNN_EPS, None, ALU.add).then_inc(var_ready, 1)
                dve.wait_ge(std_ready, done)
                link(dve.reciprocal(rstd[:], std[:]))
                for i in range(NT):
                    last = dve.tensor_scalar(dst[:, i, :], src[:, i, :], mean_var[:, i, 0:1], rstd[:, i:i + 1],
                                             ALU.subtract, ALU.mult)
                    if i % GT == GT - 1:
                        last.then_inc(xn_ready, 1)

            dve.wait_ge(x_in, 16)
            norm(x, xn, 1)
            for g in range(NG):
                dve.wait_ge(y_full, g + 1)
                dve.tensor_copy(y[:, GT * g:GT * g + GT, :], misc[g % 2][:]).then_inc(y_ready, 1)

            def product(u):
                g, c, operand = UNITS[u]
                n = product_no[u]
                if operand:
                    dve.wait_ge(strip_copied, operand_no[u] + 1)
                    strip = copies[:, operand_no[u] % COPY_RING, :]
                else:
                    dve.wait_ge(strip_full, u + 1)
                    strip = strips[u % STRIP_RING][:]
                if n >= 2:
                    dve.wait_ge(product_done, n - 1)
                dve.tensor_tensor_reduce(
                    out=junk[:, n % 2, :], in0=strip, in1=adj[:, c, GW * g:GW * g + GW], scale=1.0, scalar=0.0,
                    op0=ALU.mult, op1=ALU.add, accum_out=edge_parts[:, c, g:g + 1]).then_inc(product_done, 1)

            for u, (g, c, _) in enumerate(UNITS):
                if u in product_no:
                    product(u)
                if u in GROUP_END:
                    gg = GROUP_END.index(u)
                    dve.wait_ge(h_full, gg + 1)
                    dve.tensor_tensor(t["x1"][:, GT * gg:GT * gg + GT, :], misc[gg % 2][:],
                                      x[:, GT * gg:GT * gg + GT, :], ALU.add).then_inc(h_used, 1)
            dve.wait_ge(product_done, len(PRODUCTS))
            dve.wait_ge(h_used, NG)
            link(dve.reduce_sum(edge[:], edge_parts[:], AX))
            for i in range(NT):
                last = dve.scalar_tensor_tensor(out=t["x1"][:, i, :], in0=w3[:], scalar=edge[:, i:i + 1],
                                                in1=t["x1"][:, i, :], op0=ALU.mult, op1=ALU.add)
            link(last)
            norm(t["x1"], xn, 2)

        @block.scalar
        def _(act):
            act.wait_ge(var_ready, 1)
            act.activation(std[:], var_eps[:], ACT.Sqrt).then_inc(std_ready, 1)
            for g in range(NG):
                act.wait_ge(xnT_full, g + 1)
                act.activation(xnT[:, GW * g:GW * g + GW], acc[g % 2][:], ACT.Copy).then_inc(xnT_ready, 1)
            act.wait_ge(w_in, 48)
            for u, (g, c, operand) in enumerate(UNITS):
                if operand:
                    n = operand_no[u]
                    act.wait_ge(strip_full, u + 1)
                    if n >= COPY_RING:
                        act.wait_ge(acc_step, n - COPY_RING + 1)
                        before = [product_no[v] for v in PRODUCTS
                                  if UNITS[v][2] and operand_no[v] <= n - COPY_RING]
                        if before:
                            act.wait_ge(product_done, max(before) + 1)
                    act.activation(copies[:, n % COPY_RING, :], strips[u % STRIP_RING][:],
                                   ACT.Copy).then_inc(strip_copied, 1)
                    if c == NT - 1:
                        act.wait_ge(acc_step, n + 1)
                        if g:
                            act.wait_ge(h_full, g)
                        act.activation(accT[:], acc[g % 2][:], ACT.Identity, bias=bias[:]).then_inc(acc_copied, 1)
            act.wait_ge(var_ready, 2)
            act.activation(std[:], var_eps[:], ACT.Sqrt).then_inc(std_ready, 1)

        @block.tensor
        def _(pe):
            pe.wait_ge(consts, 4)
            for g in range(NG):
                pe.wait_ge(xn_ready, g + 1)
                if g >= 2:
                    pe.wait_ge(xnT_ready, g - 1)
                for j in range(GT):
                    last = pe.transpose(acc[g % 2][:, P * j:P * j + P], xn[:, GT * g + j, :], t["ident"][:])
                last.then_inc(xnT_full, 1)
            pe.wait_ge(w_in, 48)
            for g in range(NG):
                pe.wait_ge(xnT_ready, g + 1)
                if g >= 2:
                    pe.wait_ge(y_ready, g - 1)
                for j in range(GT):
                    i = GT * g + j
                    last = pe.matmul(misc[g % 2][:, j, :], xnT[:, P * i:P * i + P], w12[:, 1, :],
                                     start=True, stop=True)
                last.then_inc(y_full, 1)
            pe.wait_ge(y_ready, NG)

            def transposes(u):
                g, c, _ = UNITS[u]
                if u >= STRIP_RING:
                    v = u - STRIP_RING
                    if UNITS[v][2]:
                        pe.wait_ge(strip_copied, operand_no[v] + 1)
                    else:
                        pe.wait_ge(product_done, product_no[v] + 1)
                for j in range(GT):
                    last = pe.transpose(strips[u % STRIP_RING][:, P * j:P * j + P],
                                        adj[:, GT * g + j, P * c:P * c + P], t["ident"][:])
                last.then_inc(strip_full, 1)

            def products(u):
                g, c, operand = UNITS[u]
                if operand:
                    n = operand_no[u]
                    if c == 0:
                        if g >= 2:
                            pe.wait_ge(acc_copied, g - 1)
                        pe.matmul(acc[g % 2][:], w12[:, 0, :], xnT[:, GW * g:GW * g + GW], start=True, stop=False)
                    pe.wait_ge(strip_copied, n + 1)
                    pe.matmul(acc[g % 2][:], y[:, c, :], copies[:, n % COPY_RING, :], start=False,
                              stop=(c == NT - 1)).then_inc(acc_step, 1)
                    if c == NT - 1:
                        pe.wait_ge(acc_copied, g + 1)
                        if g >= 2:
                            pe.wait_ge(h_used, g - 1)
                        for j in range(GT):
                            last = pe.transpose(misc[g % 2][:, j, :], accT[:, P * j:P * j + P], t["ident"][:])
                        last.then_inc(h_full, 1)

            AHEAD = 2
            for u in range(len(UNITS) + AHEAD):
                if u < len(UNITS):
                    g, c, operand = UNITS[u]
                    if operand and c == 0:
                        pe.wait_ge(adj_in[g], 16 * GT)
                    transposes(u)
                if u >= AHEAD:
                    products(u - AHEAD)



def project(nc, a, t, k_scratch, q_scratch, sx_scratch):
    with ExitStack() as ctx:
        def sb(name, shape, dt=F32):
            return ctx.enter_context(nc.sbuf_tensor(name, shape, dt))

        def sem(name):
            return ctx.enter_context(nc.semaphore(name))

        hl_w = sb("hl_w_in", [P, H])
        hl_wT = sb("hl_wT", [P, P])
        hl_b = sb("hl_b", [P, 1])
        kv_w = sb("kv_w", [D, 2, P])
        kv_wT = sb("kv_wT", [P, 2, P])
        q_w = sb("q_w", [P, NH, D])
        q_wT = sb("q_wT", [P, P])
        xnT = sb("xnT2", [P, S])
        sxT = t["sxT"]
        hi = sb("hi", [P, 3, GW], F32R)
        lo = sb("lo", [P, 3, GW], F32R)
        pt = [ctx.enter_context(nc.psum_tensor(f"pt{i}", [P, GW], F32)) for i in range(2)]
        pw = ctx.enter_context(nc.psum_tensor("pw", [P, 4, P], F32))
        pq = [ctx.enter_context(nc.psum_tensor(f"pq{i}", [P, GW], F32)) for i in range(3)]

        w_in = sem("project_w_in")
        wT_full, wT_ready, zeroed = sem("wT_full"), sem("wT_ready"), sem("zeroed")
        x_full, x_ready = sem("x_full"), sem("x_ready")
        sx_full, sx_ready = sem("sx_full"), sem("sx_ready")
        part_full, hi_ready, lo_ready, part_out = sem("part_full"), sem("hi_ready"), sem("lo_ready"), sem("part_out")
        hi_out = [sem(f"hi_out{i}") for i in range(3)]
        sx_out, late_w_in = sem("sx_out"), sem("late_w_in")
        v_full, v_ready = sem("v_full"), sem("v_ready")
        block = ctx.enter_context(nc.Block())

        PARTS = [("k", 0, g) for g in range(NG)] + [("q", n, g) for n in range(NH) for g in range(NG)]
        xnT_v = t["xn"]

        @block.sync
        def _(sp):
            sp.dma_start(hl_w[:], a["ffn_hl_w"].rearrange("n d h -> (n d) h")).then_inc(w_in, 16)
            sp.dma_start(hl_b[:], a["ffn_hl_b"].rearrange("n (d o) -> (n d) o", o=1)).then_inc(w_in, 16)
            sp.dma_start(kv_w[:, 0, :].rearrange("o (n d) -> o n d", n=NH),
                         a["ffn_wk"].rearrange("n o d -> o n d")).then_inc(w_in, 16)
            sp.dma_start(kv_w[:, 1, :].rearrange("o (n d) -> o n d", n=NH),
                         a["ffn_wv"].rearrange("n o d -> o n d")).then_inc(w_in, 16)
            sp.dma_start(q_w[:], a["ffn_wq"].rearrange("n e o d -> (e o) n d")).then_inc(w_in, 16)
            sp.dma_start(t["gate_w"][:], a["ffn_gate_w"].rearrange("n e f -> (n e) f")).then_inc(late_w_in, 16)
            sp.dma_start(t["fgate_w"][:], a["ffn_fgate_w"]).then_inc(late_w_in, 16)
            for name in ("ln_g", "ln_b", "fnorm_g", "fnorm_b"):
                sp.dma_start(t[name][:], a["ffn_" + name].partition_broadcast(P)).then_inc(late_w_in, 16)
            sp.wait_ge(zeroed, 2)
            for n in range(NH):
                rows = slice(D * n, D * n + D)
                sp.dma_start(t["gate_b"][D * n:D * n + NE, :],
                             a["ffn_gate_b"][n].rearrange("(e o) -> e o", o=1)).then_inc(late_w_in, 16)
                for k, layer in enumerate(("fc1", "fc2")):
                    sp.dma_start(t["fc_w"][:, k, rows], a[f"ffn_{layer}_w"]).then_inc(late_w_in, 16)
                    sp.dma_start(t["fc_b"][rows, k:k + 1],
                                 a[f"ffn_{layer}_b"].rearrange("(d o) -> d o", o=1)).then_inc(late_w_in, 16)
            sp.wait_ge(sx_ready, NG)
            sp.dma_start(sx_scratch.rearrange("n d s -> (n d) s"), sxT[:]).then_inc(sx_out, 16)
            for i, (what, n, g) in enumerate(PARTS):
                cols = slice(GW * g, GW * g + GW)
                for part, ready, src in ((0, hi_ready, hi), (1, lo_ready, lo)):
                    if what == "k":
                        dst = k_scratch[part].rearrange("n o s -> (n o) s")[:, cols]
                    else:
                        dst = q_scratch[part, n].rearrange("e o s -> (e o) s")[:, cols]
                    sp.wait_ge(ready, i + 1)
                    sp.dma_start(dst, src[:, i % 3, :].bitcast(F32)).then_inc(hi_out[i % 3], 16)
            sp.wait_ge(sx_out, 16)
            sp.wait_ge(late_w_in, 16 * (6 + 5 * NH))
            for i in range(3):
                sp.wait_ge(hi_out[i], 32 * len(range(i, len(PARTS), 3)))

        @block.tensor
        def _(pe):
            pe.wait_ge(w_in, 80)
            pe.transpose(pw[:, 0, :], hl_w[:], t["ident"][:])
            pe.transpose(pw[:, 1, 0:D], kv_w[:, 0, :], t["ident"][0:D, 0:D])
            pe.transpose(pw[:, 2, 0:D], kv_w[:, 1, :], t["ident"][0:D, 0:D])
            pe.transpose(pw[:, 3, :], q_w[:].rearrange("p n d -> p (n d)"), t["ident"][:]).then_inc(wT_full, 1)
            for g in range(NG):
                if g >= 2:
                    pe.wait_ge(x_ready, g - 1)
                for j in range(GT):
                    last = pe.transpose(pt[g % 2][:, P * j:P * j + P], xnT_v[:, GT * g + j, :], t["ident"][:])
                last.then_inc(x_full, 1)
            pe.wait_ge(wT_ready, 1)
            for g in range(NG):
                pe.wait_ge(x_ready, max(g + 1, min(g + 3, NG)))
                if g >= 2:
                    pe.wait_ge(sx_ready, g - 1)
                pe.matmul(pt[g % 2][:], hl_wT[:], xnT[:, GW * g:GW * g + GW], start=True, stop=True).then_inc(sx_full, 1)
            for i, (what, n, g) in enumerate(PARTS):
                pe.wait_ge(sx_ready, g + 1 if i < NG else NG)
                if i >= 3:
                    pe.wait_ge(lo_ready, i - 2)
                cols = slice(GW * g, GW * g + GW)
                if what == "k":
                    last = pe.matmul(pq[i % 3][:], kv_wT[:, 0, :], sxT[:, cols], start=True, stop=True)
                else:
                    rows = slice(D * n, D * n + D)
                    last = pe.matmul(pq[i % 3][:], q_wT[rows, :], sxT[rows, cols], start=True, stop=True)
                last.then_inc(part_full, 1)
            for g in range(NG):
                if g >= 2:
                    pe.wait_ge(v_ready, g - 1)
                else:
                    pe.wait_ge(sx_ready, NG)
                for j in range(GT):
                    i = GT * g + j
                    last = pe.matmul(pt[g % 2][:, P * j:P * j + P], sxT[:, P * i:P * i + P], kv_wT[:, 1, :],
                                     start=True, stop=True)
                last.then_inc(v_full, 1)

        @block.scalar
        def _(act):
            for g in range(NG):
                act.wait_ge(x_full, g + 1)
                act.activation(xnT[:, GW * g:GW * g + GW], pt[g % 2][:], ACT.Copy).then_inc(x_ready, 1)
            for g in range(NG):
                act.wait_ge(sx_full, g + 1)
                act.activation(sxT[:, GW * g:GW * g + GW], pt[g % 2][:], ACT.Identity, bias=hl_b[:]).then_inc(sx_ready, 1)
            for i in range(len(PARTS)):
                act.wait_ge(part_full, i + 1)
                if i >= 3:
                    act.wait_ge(hi_out[i % 3], 32 * (i // 3))
                act.activation(hi[:, i % 3, :], pq[i % 3][:], ACT.Copy).then_inc(hi_ready, 1)

        @block.vector
        def _(dve):
            dve.memset(kv_wT[:], 0.0).then_inc(zeroed, 1)
            dve.memset(t["gate_b"][:], 0.0).then_inc(zeroed, 1)
            dve.wait_ge(zeroed, 1)
            dve.wait_ge(wT_full, 1)
            dve.tensor_copy(hl_wT[:], pw[:, 0, :])
            for k in range(2):
                for n in range(NH):
                    rows = slice(D * n, D * n + D)
                    dve.tensor_copy(kv_wT[rows, k, rows], pw[rows, 1 + k, 0:D])
            dve.tensor_copy(q_wT[:], pw[:, 3, :]).then_inc(wT_ready, 1)
            for i in range(len(PARTS)):
                dve.wait_ge(hi_ready, i + 1)
                if i >= 3:
                    dve.wait_ge(hi_out[i % 3], 32 * (i // 3))
                dve.tensor_tensor(lo[:, i % 3, :], pq[i % 3][:], hi[:, i % 3, :].bitcast(F32),
                                  ALU.subtract).then_inc(lo_ready, 1)
            for g in range(NG):
                dve.wait_ge(v_full, g + 1)
                dve.tensor_copy(t["v_all"][:, :, GT * g:GT * g + GT, :].rearrange("p n t o -> p t n o"),
                                pt[g % 2][:].rearrange("p (t n o) -> p t n o", t=GT, n=NH)).then_inc(v_ready, 1)


def attend(nc, t, k_scratch, q_scratch, sx_scratch):
    with ExitStack() as ctx:
        def sb(name, shape, dt=F32):
            return ctx.enter_context(nc.sbuf_tensor(name, shape, dt))

        def sem(name):
            return ctx.enter_context(nc.semaphore(name))

        keys = sb("keys", [KR + 1, S], F32R)
        keys_max = sb("keys_max", [KR, S], F32R)
        queries = [sb(f"queries{g}", [KR + 1, NE, GW], F32R) for g in range(NG)]
        values = sb("values", [P, NT, D])
        ones = sb("ones", [P, D])
        features = sb("features", [P, GW])
        probs = sb("probs", [P, NP_RING, NE, GW])
        chunk_max = sb("chunk_max", [P, NE * GT, NG])
        row_max = sb("row_max", [P, NE * GT])
        neg_max = sb("neg_max", [P, D], F32R)
        neg_maxT = sb("neg_maxT", [P, D], F32R)
        inv_sum = sb("inv_sum", [P, GW])
        inv_masked = sb("inv_masked", [P, GW])
        scores = [ctx.enter_context(nc.psum_tensor(f"scores{i}", [P, 2, GW], F32)) for i in range(2)]
        chunk = [ctx.enter_context(nc.psum_tensor(f"chunk{i}", [P, GW], F32)) for i in range(2)]
        outT = ctx.enter_context(nc.psum_tensor("outT", [P, GW], F32))
        sums = ctx.enter_context(nc.psum_tensor("sums", [P, GW], F32))

        ones_ready = sem("ones_ready")
        keys_in = [sem(f"keys_in{c}") for c in range(NG)]
        values_in = [sem(f"values_in{c}") for c in range(NG)]
        queries_in = [sem(f"queries_in{g}") for g in range(NG)]
        keys_max_in, features_in = sem("keys_max_in"), sem("features_in")
        max_row_in = [sem(f"max_row_in{g}") for g in range(NG)]
        scores_full, scores_used = sem("scores_full"), sem("scores_used")
        probs_used = sem("probs_used")
        chunk_full, chunk_used = sem("chunk_full"), sem("chunk_used")
        row_max_ready, neg_ready, neg_maxT_ready = sem("row_max_ready"), sem("neg_ready"), sem("neg_maxT_ready")
        inv_ready, masked_ready, out_used = sem("inv_ready"), sem("masked_ready"), sem("out_used")
        block = ctx.enter_context(nc.Block())

        SCALE = float(D) ** 0.5

        def chunks_at(slot, last):
            first = LEAD + PER_SLOT * slot
            return range(first, min(first + PER_SLOT, NC) if last else first + PER_SLOT)

        def load_keys(sp, h, c):
            for r, part in enumerate((0, 1, 0)):
                sp.dma_start(keys[D * r:D * r + D, GW * c:GW * c + GW].bitcast(F32),
                             k_scratch[part, h, :, GW * c:GW * c + GW]).then_inc(keys_in[c], 16)

        def load_keys_max(sp, h):
            for r, part in enumerate((0, 1, 0)):
                sp.dma_start(keys_max[D * r:D * r + D, :].bitcast(F32), k_scratch[part, h]).then_inc(keys_max_in, 16)

        def load_queries(sp, h, g):
            for r, part in enumerate((0, 0, 1)):
                sp.dma_start(queries[g][D * r:D * r + D, :, :].bitcast(F32),
                             q_scratch[part, h].rearrange("e o s -> o e s")[:, :, GW * g:GW * g + GW])\
                    .then_inc(queries_in[g], 16)

        def load_values(sp, h, c):
            sp.dma_start(values[:, GT * c:GT * c + GT, :],
                         t["v_all"][:, h, GT * c:GT * c + GT, :]).then_inc(values_in[c], 16)

        def load_features(sp, h, g):
            for e in range(NE):
                sp.dma_start(features[D * e:D * e + D, :], sx_scratch[h, :, GW * g:GW * g + GW]).then_inc(features_in, 16)

        def place_max_row(sp, step, g):
            sp.wait_ge(neg_maxT_ready, step + 1)
            for quadrant in range(4):
                q0 = D * quadrant
                sp.dma_start(queries[g][KR:KR + 1, :, :].rearrange("r e (j f) -> r (e j) f", f=P)[:, :, q0:q0 + D].bitcast(F32),
                             neg_maxT[q0:q0 + NE * GT, :].bitcast(F32)).then_inc(max_row_in[g], 16)

        def sp_head(sp, h, last):
            events = []
            for g in range(NG):
                step_end = STEP_END[g]

                def next_queries(g=g, i=step_end):
                    sp.wait_ge(scores_full, h * (2 * NS) + 2 * (i + 1))
                    load_queries(sp, h + 1, g)
                if not last:
                    events.append((step_end + 0.5, next_queries))

                def feat(g=g):
                    sp.wait_ge(masked_ready, h * NG + g + 1)
                    if g + 1 < NG:
                        load_features(sp, h, g + 1)
                    else:
                        load_features(sp, h + 1, 0)
                if not (last and g == NG - 1):
                    events.append((step_end + 0.9, feat))
                if not last:
                    slot = STEP_START[NG - 1] + GT * g + GT - 1

                    def next_keys(c=g, i=slot):
                        sp.wait_ge(scores_full, h * (2 * NS) + 2 * (i + 1))
                        load_keys(sp, h + 1, c)

                    def next_values(c=g, i=slot):
                        sp.wait_ge(probs_used, h * NS + NP_RING + i + 1)
                        load_values(sp, h + 1, c)
                    events.append((slot + 0.4, next_keys))
                    events.append((slot + 1.6, next_values))
                for dh in (0, 1):
                    at = dh * NC + CHUNK_END[g]
                    if at >= LEAD and at < LEAD + NC and not (last and dh):
                        def row(dh=dh, g=g):
                            place_max_row(sp, (h + dh) * NG + g, g)
                        events.append(((at - LEAD) // PER_SLOT + 0.7, row))
            if not last:
                def next_keys_max():
                    sp.wait_ge(chunk_full, (h + 1) * NC)
                    load_keys_max(sp, h + 1)
                events.append(((NC - 1 - LEAD) // PER_SLOT + 0.3, next_keys_max))
            for _, do in sorted(events, key=lambda x: x[0]):
                do()

        @block.sync
        def _(sp):
            load_queries(sp, 0, 0)
            load_keys_max(sp, 0)
            for c in range(NG):
                load_keys(sp, 0, c)
                load_values(sp, 0, c)
                if c:
                    load_queries(sp, 0, c)
            load_features(sp, 0, 0)
            for g in range(NG):
                if CHUNK_END[g] < LEAD:
                    place_max_row(sp, g, g)
            with sp.Fori(0, NH - 1) as h:
                sp_head(sp, h, False)
            sp_head(sp, NH - 1, True)

        def pe_chunk(pe, h, i):
            g, c, e, j = CHUNKS[i % NC]
            head = h + i // NC
            if i % NC == 0:
                pe.wait_ge(keys_max_in, head * 48 + 48)
            if (e, j, c) == (0, 0, 0):
                pe.wait_ge(queries_in[g], head * 48 + 48)
            pe.wait_ge(chunk_used, h * NC + i + 1)
            n = chunk_width(g, c, j)
            bank = chunk[i % 2]
            if c == g:
                pe.matmul(bank[:, n - P:n], t["ident_bf"][:], t["mask_qk"][:], start=True, stop=False,
                          skip_group_check=True)
            last = pe.matmul(bank[:, 0:n], queries[g][0:KR, e, P * j:P * j + P], keys_max[:, GW * c:GW * c + n],
                             start=(c < g), stop=True, skip_group_check=(c == g))
            last.then_inc(chunk_full, 1)

        def pe_scores(pe, h, i):
            g, k = SLOTS[i]
            shift = slot_shift(g, k)
            if i == STEP_START[g]:
                pe.wait_ge(max_row_in[g], h * 64 + 64)
                pe.wait_ge(keys_in[g], h * 48 + 48)
            for half in range(2):
                pe.wait_ge(scores_used, h * (2 * NS) + 2 * i + half + 1)
                for e2 in range(2):
                    e = 2 * half + e2
                    if k >= GT * g:
                        pe.matmul(scores[half][:, e2, 0:P], t["ident_bf"][:], t["mask_kq"][:], start=True,
                                  stop=False, skip_group_check=True)
                    last = pe.matmul(scores[half][:, e2, 0:GW - shift], keys[:, P * k:P * k + P],
                                     queries[g][:, e, shift:GW], start=(k < GT * g), stop=True,
                                     skip_group_check=(k >= GT * g))
                last.then_inc(scores_full, 1)

        def pe_values(pe, h, i):
            g, k = SLOTS[i]
            shift = slot_shift(g, k)
            pe.wait_ge(scores_used, h * (2 * NS) + 2 * i + 4)
            if i == STEP_START[g]:
                pe.wait_ge(values_in[g], h * 16 + 16)
                pe.wait_ge(out_used, h * NG + g + 1)
            first, stop = k == 0, i == STEP_END[g]
            for stationary, bank in ((values[:, k, :], outT), (ones[:], sums)):
                for e in range(NE):
                    last = pe.matmul(bank[D * e:D * e + D, shift:GW], stationary,
                                     probs[:, i % NP_RING, e, 0:GW - shift], start=first, stop=stop)
            last.then_inc(probs_used, 1)

        def pe_head(pe, h, last):
            for i in range(NS):
                pe_scores(pe, h, i)
                for n in chunks_at(i, last):
                    pe_chunk(pe, h, n)
                if i:
                    pe_values(pe, h, i - 1)
            pe_values(pe, h, NS - 1)

        @block.tensor
        def _(pe):
            pe.wait_ge(ones_ready, 3)
            for i in range(LEAD):
                pe_chunk(pe, 0, i)
            with pe.Fori(0, NH - 1) as h:
                pe_head(pe, h, False)
            pe_head(pe, NH - 1, True)

        def act_head(act, h):
            for i, (g, k) in enumerate(SLOTS):
                n = GW - slot_shift(g, k)
                act.wait_ge(probs_used, h * NS + i + 1)
                for half in range(2):
                    act.wait_ge(scores_full, h * (2 * NS) + 2 * i + half + 1)
                    act.activation(probs[:, i % NP_RING, 2 * half:2 * half + 2, 0:n], scores[half][:, :, 0:n], ACT.Exp,
                                   scale=SCALE).then_inc(scores_used, 1)

        @block.scalar
        def _(act):
            act.sem_inc(scores_used, 2)
            with act.Fori(0, NH - 1) as h:
                act_head(act, h)
            act_head(act, NH - 1)

        def dve_chunk(dve, h, i):
            g, c, e, j = CHUNKS[i % NC]
            n = chunk_width(g, c, j)
            step = (h + i // NC) * NG + g
            first = CHUNK_END[g - 1] + 1 if g else 0
            if i % NC == first and not (isinstance(step, int) and step == 0):
                dve.wait_ge(row_max_ready, step)
            dve.wait_ge(chunk_full, h * NC + i + 1)
            dve.reduce_max(chunk_max[:, GT * e + j, c:c + 1], chunk[i % 2][:, 0:n], AX).then_inc(chunk_used, 1)
            if i % NC == CHUNK_END[g]:
                dve.wait_ge(chunk_used, h * NC + i + 3)
                if not (isinstance(step, int) and step == 0):
                    dve.wait_ge(neg_ready, step)
                dve.reduce_max(row_max[:], chunk_max[:, :, 0:g + 1], AX).then_inc(row_max_ready, 1)
                dve.wait_ge(row_max_ready, step + 1)
                if not (isinstance(step, int) and step == 0):
                    dve.wait_ge(neg_maxT_ready, step)
                dve.tensor_scalar(neg_max[:, 0:NE * GT], row_max[:], -1.0, None, ALU.mult).then_inc(neg_ready, 1)
                dve.wait_ge(neg_ready, step + 1)
                g0, h0 = ((g - 1) % NG, h + i // NC - (1 if g == 0 else 0))
                if not (isinstance(step, int) and step == 0):
                    dve.wait_ge(max_row_in[g0], h0 * 64 + 64)
                dve.transpose(neg_maxT[:].bitcast(F32), neg_max[:].bitcast(F32)).then_inc(neg_maxT_ready, 1)

        def dve_step_end(dve, h, g):
            step = h * NG + g
            dve.wait_ge(probs_used, h * NS + NP_RING + STEP_END[g] + 1)
            dve.wait_ge(out_used, step + 1)
            dve.reciprocal(inv_sum[:], sums[:]).then_inc(inv_ready, 1)
            dve.wait_ge(inv_ready, step + 1)
            dve.wait_ge(features_in, h * (64 * NG) + 64 * (g + 1))
            dve.scalar_tensor_tensor(out=inv_masked[:], in0=features[:], scalar=0.0, in1=inv_sum[:],
                                     op0=ALU.not_equal, op1=ALU.mult).then_inc(masked_ready, 1)
            dve.wait_ge(masked_ready, step + 1)
            dve.tensor_tensor(t["heads_out"][:, h, GW * g:GW * g + GW] if isinstance(h, int)
                              else t["heads_out"][:, bass.ds(h, 1), GW * g:GW * g + GW].rearrange("p a s -> p (a s)"),
                              outT[:], inv_masked[:], ALU.mult).then_inc(out_used, 1)

        def dve_head(dve, h, last):
            for i in range(NS):
                for n in chunks_at(i, last):
                    dve_chunk(dve, h, n)
                if i - 1 in STEP_END:
                    dve_step_end(dve, h, STEP_END.index(i - 1))
            dve_step_end(dve, h, NG - 1)

        @block.vector
        def _(dve):
            dve.sem_inc(chunk_used, 2)
            dve.sem_inc(out_used, 1)
            dve.memset(neg_max[:].bitcast(F32), 0.0).then_inc(ones_ready, 1)
            dve.memset(ones[:], 1.0).then_inc(ones_ready, 1)
            dve.wait_ge(ones_ready, 2)
            for i in range(LEAD):
                dve_chunk(dve, 0, i)
            with dve.Fori(0, NH - 1) as h:
                dve_head(dve, h, False)
            dve_head(dve, NH - 1, True)

        @block.gpsimd
        def _(pool):
            pool.sem_inc(probs_used, NP_RING)
            pool.memset(keys[KR:KR + 1, :].bitcast(F32), 1.0).then_inc(ones_ready, 1)


def finish(nc, a, t, out):
    JN = GT * NH

    with ExitStack() as ctx:
        def sb(name, shape, dt=F32):
            return ctx.enter_context(nc.sbuf_tensor(name, shape, dt))

        def sem(name):
            return ctx.enter_context(nc.semaphore(name))

        gate_wT = sb("gate_wT", [P, NH, D])
        fc_wT = sb("fc_wT", [P, 2, P])
        fgate_wT = sb("fgate_wT", [P, NH])
        logitsT = sb("logitsT", [P, NG, GW])
        small = {n: sb(n, [P, NG, JN]) for n in ("gate_max", "gate_sum", "gate_inv", "sum1", "var1", "vare1",
                                                 "std1", "rstd1", "sum2", "var2", "vare2", "std2", "rstd2")}
        tiny = {n: sb(n, [P, NG, GT]) for n in ("out_max", "out_sum", "out_inv")}
        gate = {n: sb(n, [P, NG, JN, NE]) for n in ("gate_shift", "gate_exp", "gate_share")}
        ogate = {n: sb(n, [P, NG, GT, NH]) for n in ("out_shift", "out_exp", "out_share")}
        shared = sb("shared", [P, 2, NH * NE, D])
        mixed = sb("mixed", [P, NG, JN, D])
        resid = sb("resid", [P, NG, JN, D])
        centred = sb("centred", [P, NG, JN, D])
        square = sb("square", [P, NG, JN, D])
        normed = sb("normed", [P, NG, JN, D])
        scaled = sb("scaled", [P, NG, JN, D])
        fx = sb("fx", [P, NG, JN, D])
        fxT = sb("fxT", [P, NG, GW])
        nonzero = sb("nonzero", [P, NG, GW])
        hidden = sb("hidden", [P, NG, GW])
        hidden_m = sb("hidden_m", [P, NG, GW])
        fc_out = sb("fc_out", [P, NG, GW])
        banks = [ctx.enter_context(nc.psum_tensor(f"bank{i}", [P, GW], F32)) for i in range(8)]

        names = ("wT_full2 wT_ready2 zeroed2 logits_full logits_ready tok_full shift_ready gexp_ready gsum_ready "
                 "ginv_ready share_ready heads_full heads_used mixed_ready feat_full resid_ready sum1_ready "
                 "centred1_ready square1_ready var1_ready vare1_ready std1_ready rstd1_ready normed1_ready "
                 "scaled1_ready fx_ready fxT_full fxT_ready nonzero_ready fc1_full hidden_ready masked_ready2 "
                 "fc2_full fc2_masked fc_out_ready back_full sum2_ready centred2_ready square2_ready var2_ready "
                 "vare2_ready std2_ready rstd2_ready normed2_ready scaled2_ready fout_ready foutT_full foutT_ready "
                 "olog_full omax_ready oshift_ready oexp_ready osum_ready oinv_ready oshare_ready gated_ready "
                 "result_ready result_out gmax_ready").split()
        s = {n: sem(n) for n in names}
        block = ctx.enter_context(nc.Block())

        def spread(ap, n):
            return ap.unsqueeze(2).to_broadcast([P, ap.shape[1], n])

        def each(vec):
            return vec.unsqueeze(1).to_broadcast([P, JN, D])

        def pairs(bank):
            return bank[:].rearrange("p (k d) -> p k d", d=D)

        @block.tensor
        def _(pe):
            ident = t["ident"][:]
            pe.transpose(banks[0][:, 0:NH * NE], t["gate_w"][:], t["ident"][0:NH * NE, 0:NH * NE])
            pe.transpose(banks[0][:, 128:128 + D], t["fc_w"][:, 0, :], t["ident"][0:D, 0:D])
            pe.transpose(banks[0][:, 256:256 + D], t["fc_w"][:, 1, :], t["ident"][0:D, 0:D])
            pe.transpose(banks[0][:, 384:384 + NH], t["fgate_w"][:], t["ident"][0:NH, 0:NH]).then_inc(s["wT_full2"], 1)
            pe.wait_ge(s["wT_ready2"], 1)
            for g in range(NG):
                for n in range(NH):
                    last = pe.matmul(banks[g][D * n:D * n + D, :], gate_wT[:, n, :],
                                     t["heads_out"][:, n, GW * g:GW * g + GW], start=True, stop=True)
                last.then_inc(s["logits_full"], 1)
            for g in range(NG):
                pe.wait_ge(s["logits_ready"], g + 1)
                for j in range(GT):
                    last = pe.transpose(banks[4 + g][:, P * j:P * j + P], logitsT[:, g, P * j:P * j + P], ident)
                last.then_inc(s["tok_full"], 1)
            for u in range(NT):
                pe.wait_ge(s["heads_used"], u - 3) if u >= 4 else pe.wait_ge(s["logits_ready"], u + 1)
                for n in range(NH):
                    last = pe.transpose(banks[u % 4][:, P * n:P * n + P], t["heads_out"][:, n, P * u:P * u + P], ident)
                last.then_inc(s["heads_full"], 1)
            for g in range(NG):
                pe.wait_ge(s["shift_ready"], g + 1)
                for j in range(GT):
                    i = GT * g + j
                    last = pe.transpose(banks[4 + g][:, P * j:P * j + P], t["sxT"][:, P * i:P * i + P], ident)
                last.then_inc(s["feat_full"], 1)
            for g in range(NG):
                pe.wait_ge(s["fx_ready"], g + 1)
                for j in range(GT):
                    last = pe.transpose(banks[g][:, P * j:P * j + P],
                                        fx[:, g, NH * j:NH * j + NH, :].rearrange("p n d -> p (n d)"), ident)
                last.then_inc(s["fxT_full"], 1)
            for g in range(NG):
                pe.wait_ge(s["fxT_ready"], g + 1)
                pe.matmul(banks[4 + g][:], fc_wT[:, 0, :], fxT[:, g, :], start=True, stop=True).then_inc(s["fc1_full"], 1)
            for g in range(NG):
                pe.wait_ge(s["masked_ready2"], g + 1)
                pe.matmul(banks[g][:], fc_wT[:, 1, :], hidden_m[:, g, :], start=True, stop=True).then_inc(s["fc2_full"], 1)
            for g in range(NG):
                pe.wait_ge(s["fc_out_ready"], g + 1)
                for j in range(GT):
                    last = pe.transpose(banks[4 + g][:, P * j:P * j + P], fc_out[:, g, P * j:P * j + P], ident)
                last.then_inc(s["back_full"], 1)
            for g in range(NG):
                pe.wait_ge(s["fout_ready"], g + 1)
                for j in range(GT):
                    last = pe.transpose(banks[g][:, P * j:P * j + P],
                                        fx[:, g, NH * j:NH * j + NH, :].rearrange("p n d -> p (n d)"), ident)
                last.then_inc(s["foutT_full"], 1)
            for g in range(NG):
                pe.wait_ge(s["foutT_ready"], g + 1)
                for j in range(GT):
                    last = pe.matmul(banks[4 + g][:, NH * j:NH * j + NH], hidden[:, g, P * j:P * j + P], fgate_wT[:],
                                     start=True, stop=True)
                last.then_inc(s["olog_full"], 1)

        @block.scalar
        def _(act):
            def stage(waits, done, do):
                for g in range(NG):
                    for w in waits:
                        act.wait_ge(s[w], g + 1)
                    do(g).then_inc(s[done], 1)

            stage(["logits_full"], "logits_ready",
                  lambda g: act.activation(logitsT[:, g, :], banks[g][:], ACT.Identity, bias=t["gate_b"][:]))
            stage(["shift_ready"], "gexp_ready",
                  lambda g: act.activation(gate["gate_exp"][:, g], gate["gate_shift"][:, g], ACT.Exp))
            stage(["centred1_ready"], "square1_ready",
                  lambda g: act.activation(square[:, g], centred[:, g], ACT.Square))
            stage(["vare1_ready"], "std1_ready",
                  lambda g: act.activation(small["std1"][:, g], small["vare1"][:, g], ACT.Sqrt))
            stage(["fxT_full"], "fxT_ready", lambda g: act.activation(fxT[:, g, :], banks[g][:], ACT.Copy))
            stage(["fc1_full"], "hidden_ready",
                  lambda g: act.activation(hidden[:, g, :], banks[4 + g][:], ACT.Relu, bias=t["fc_b"][:, 0:1]))
            stage(["centred2_ready", "var1_ready"], "square2_ready",
                  lambda g: act.activation(square[:, g], centred[:, g], ACT.Square))
            stage(["vare2_ready"], "std2_ready",
                  lambda g: act.activation(small["std2"][:, g], small["vare2"][:, g], ACT.Sqrt))
            stage(["foutT_full", "masked_ready2"], "foutT_ready",
                  lambda g: act.activation(hidden[:, g, :], banks[g][:], ACT.Copy))
            stage(["oshift_ready"], "oexp_ready",
                  lambda g: act.activation(ogate["out_exp"][:, g], ogate["out_shift"][:, g], ACT.Exp))

        @block.vector
        def _(dve):
            def stage(waits, done, do):
                for g in range(NG):
                    for w in waits:
                        dve.wait_ge(s[w], g + 1)
                    do(g).then_inc(s[done], 1)

            def norm(k, source, bank0):
                stage([source[1]], f"sum{k}_ready", lambda g: dve.reduce_sum(small[f"sum{k}"][:, g], source[0](g), AX))
                stage([f"sum{k}_ready"], f"centred{k}_ready", lambda g: dve.scalar_tensor_tensor(
                    out=centred[:, g], in0=spread(small[f"sum{k}"][:, g], D), scalar=-1.0 / D, in1=source[0](g),
                    op0=ALU.mult, op1=ALU.add))
                stage([f"square{k}_ready"], f"var{k}_ready",
                      lambda g: dve.reduce_sum(small[f"var{k}"][:, g], square[:, g], AX))
                stage([f"var{k}_ready"], f"vare{k}_ready", lambda g: dve.tensor_scalar(
                    small[f"vare{k}"][:, g], small[f"var{k}"][:, g], 1.0 / D, FFN_EPS, ALU.mult, ALU.add))
                stage([f"std{k}_ready"], f"rstd{k}_ready",
                      lambda g: dve.reciprocal(small[f"rstd{k}"][:, g], small[f"std{k}"][:, g]))
                stage([f"rstd{k}_ready"] + (["scaled1_ready"] if k == 2 else []), f"normed{k}_ready",
                      lambda g: dve.tensor_tensor(normed[:, g], centred[:, g], spread(small[f"rstd{k}"][:, g], D), ALU.mult))

            dve.memset(gate_wT[:], 0.0).then_inc(s["zeroed2"], 1)
            dve.memset(fc_wT[:], 0.0).then_inc(s["zeroed2"], 1)
            dve.wait_ge(s["zeroed2"], 2)
            dve.wait_ge(s["wT_full2"], 1)
            dve.tensor_copy(gate_wT[:, :, 0:NE], banks[0][:, 0:NH * NE].rearrange("p (n e) -> p n e", n=NH))
            for k in range(2):
                for n in range(NH):
                    rows = slice(D * n, D * n + D)
                    dve.tensor_copy(fc_wT[rows, k, rows], banks[0][rows, 128 * (k + 1):128 * (k + 1) + D])
            dve.tensor_copy(fgate_wT[:], banks[0][:, 384:384 + NH]).then_inc(s["wT_ready2"], 1)

            def logits(g):
                return banks[4 + g][:].rearrange("p (k r) -> p k r", r=D)[:, :, 0:NE]
            stage(["tok_full"], "gmax_ready", lambda g: dve.reduce_max(small["gate_max"][:, g], logits(g), AX))
            stage(["gmax_ready"], "shift_ready", lambda g: dve.tensor_tensor(
                gate["gate_shift"][:, g], logits(g), spread(small["gate_max"][:, g], NE), ALU.subtract))
            stage(["gexp_ready"], "gsum_ready",
                  lambda g: dve.reduce_sum(small["gate_sum"][:, g], gate["gate_exp"][:, g], AX))
            stage(["gsum_ready"], "ginv_ready",
                  lambda g: dve.reciprocal(small["gate_inv"][:, g], small["gate_sum"][:, g]))
            stage(["ginv_ready"], "share_ready", lambda g: dve.tensor_tensor(
                gate["gate_share"][:, g], gate["gate_exp"][:, g], spread(small["gate_inv"][:, g], NE), ALU.mult))
            for u in range(NT):
                g, j = u // GT, u % GT
                dve.wait_ge(s["heads_full"], u + 1)
                dve.wait_ge(s["share_ready"], g + 1)
                if u >= 2:
                    dve.wait_ge(s["mixed_ready"], u - 1)
                share = gate["gate_share"][:, g, NH * j:NH * j + NH, :].rearrange("p n e -> p (n e)")
                dve.tensor_tensor(shared[:, u % 2], banks[u % 4][:].rearrange("p (k d) -> p k d", d=D),
                                  spread(share, D), ALU.mult).then_inc(s["heads_used"], 1)
                dve.wait_ge(s["heads_used"], u + 1)
                dve.reduce_sum(mixed[:, g, NH * j:NH * j + NH, :],
                               shared[:, u % 2].rearrange("p (n e) d -> p n d e", n=NH), AX).then_inc(s["mixed_ready"], 1)
            for g in range(NG):
                dve.wait_ge(s["feat_full"], g + 1)
                dve.wait_ge(s["mixed_ready"], GT * g + GT)
                dve.tensor_tensor(resid[:, g], pairs(banks[4 + g]), mixed[:, g], ALU.add).then_inc(s["resid_ready"], 1)
            norm(1, (lambda g: resid[:, g], "resid_ready"), None)
            stage(["fxT_ready"], "nonzero_ready",
                  lambda g: dve.tensor_scalar(nonzero[:, g, :], fxT[:, g, :], 0.0, None, ALU.not_equal))
            stage(["hidden_ready", "nonzero_ready"], "masked_ready2",
                  lambda g: dve.tensor_tensor(hidden_m[:, g, :], hidden[:, g, :], nonzero[:, g, :], ALU.mult))
            stage(["fc2_full"], "fc2_masked", lambda g: dve.scalar_tensor_tensor(
                out=logitsT[:, g, :], in0=banks[g][:], scalar=t["fc_b"][:, 1:2], in1=nonzero[:, g, :],
                op0=ALU.add, op1=ALU.mult))
            stage(["fc2_masked"], "fc_out_ready",
                  lambda g: dve.tensor_tensor(fc_out[:, g, :], logitsT[:, g, :], fxT[:, g, :], ALU.add))
            norm(2, (lambda g: pairs(banks[4 + g]), "back_full"), None)
            def ologits(g):
                return banks[4 + g][:, 0:GT * NH].rearrange("p (j n) -> p j n", n=NH)
            stage(["olog_full"], "omax_ready", lambda g: dve.reduce_max(tiny["out_max"][:, g], ologits(g), AX))
            stage(["omax_ready"], "oshift_ready", lambda g: dve.tensor_tensor(
                ogate["out_shift"][:, g], ologits(g), spread(tiny["out_max"][:, g], NH), ALU.subtract))
            stage(["oexp_ready"], "osum_ready", lambda g: dve.reduce_sum(tiny["out_sum"][:, g], ogate["out_exp"][:, g], AX))
            stage(["osum_ready"], "oinv_ready", lambda g: dve.reciprocal(tiny["out_inv"][:, g], tiny["out_sum"][:, g]))
            stage(["oinv_ready"], "oshare_ready", lambda g: dve.tensor_tensor(
                ogate["out_share"][:, g], ogate["out_exp"][:, g], spread(tiny["out_inv"][:, g], NH), ALU.mult))
            stage(["oshare_ready"], "gated_ready", lambda g: dve.tensor_tensor(
                resid[:, g], fx[:, g],
                spread(ogate["out_share"][:, g].rearrange("p j n -> p (j n)"), D), ALU.mult))

        @block.gpsimd
        def _(pool):
            def stage(waits, done, do):
                for g in range(NG):
                    for w in waits:
                        pool.wait_ge(s[w], g + 1)
                    do(g).then_inc(s[done], 1)

            for k, (scale, shift), last in ((1, ("ln_g", "ln_b"), "fx_ready"), (2, ("fnorm_g", "fnorm_b"), "fout_ready")):
                stage([f"normed{k}_ready"], f"scaled{k}_ready",
                      lambda g: pool.tensor_tensor(scaled[:, g], normed[:, g], each(t[scale][:]), ALU.mult))
                stage([f"scaled{k}_ready"] + (["fxT_full"] if k == 2 else []), last,
                      lambda g: pool.tensor_tensor(fx[:, g], scaled[:, g], each(t[shift][:]), ALU.add))
            stage(["gated_ready"], "result_ready", lambda g: pool.tensor_tensor(
                mixed[:, g], resid[:, g], t["x1"][:, GT * g:GT * g + GT, :].rearrange("p j (n d) -> p (j n) d", d=D),
                ALU.add))

        @block.sync
        def _(sp):
            rows = out.rearrange("(g j p) f -> g p j f", j=GT, p=P)
            for g in range(NG):
                sp.wait_ge(s["result_ready"], g + 1)
                sp.dma_start(rows[g], mixed[:, g].rearrange("p (j n) d -> p j (n d)", j=GT)).then_inc(s["result_out"], 16)
            sp.wait_ge(s["result_out"], 16 * NG)


_INS = ['x', 'adj', 'L0_gnn_weight', 'L0_gnn_bias', 'L0_ffn_hl_w', 'L0_ffn_hl_b', 'L0_ffn_wq', 'L0_ffn_wk', 'L0_ffn_wv', 'L0_ffn_gate_w', 'L0_ffn_gate_b', 'L0_ffn_ln_g', 'L0_ffn_ln_b', 'L0_ffn_fc1_w', 'L0_ffn_fc1_b', 'L0_ffn_fc2_w', 'L0_ffn_fc2_b', 'L0_ffn_fnorm_g', 'L0_ffn_fnorm_b', 'L0_ffn_fgate_w']


def kernel(**inputs):
    import numpy as _np
    import concourse.bacc as _bacc
    from concourse import mybir as _mybir
    from concourse.bass_utils import run_bass_kernel_spmd as _run

    nc = _bacc.Bacc("TRN2", target_bir_lowering=False, num_devices=1)
    arrays, args = {}, {}
    for name in _INS:
        a = _np.ascontiguousarray(inputs[name])
        arrays[f"in_{name}_dram"] = a
        args[name.replace("L0_", "")] = nc.dram_tensor(f"in_{name}_dram", a.shape, _mybir.dt.from_np(a.dtype), kind="ExternalInput").ap()
    out = nc.dram_tensor("out_0_dram", (2048, 128), _mybir.dt.float32, kind="ExternalOutput").ap()
    build(nc, args, out)
    r = _run(nc, [arrays], core_ids=[0])
    return r.results[0]["out_0_dram"]
```

```python
from contextlib import ExitStack

import concourse.bass as bass
from concourse import mybir

F32 = mybir.dt.float32
F32R = mybir.dt.float32r
BF16 = mybir.dt.bfloat16
ALU = mybir.AluOpType
ACT = mybir.ActivationFunctionType
AX = mybir.AxisListType.X

P = 128
S = 2048
H = 128
NH = 4
NE = 4
D = 32
NT = S // P
NG = 4
GT = NT // NG
GW = S // NG
GNN_EPS = 1e-5
FFN_EPS = 1e-8
NEG = -1e30
BIG = 3e38
KR = 3 * D

SLOTS = [(g, t) for g in range(NG) for t in range(GT * (g + 1))]
NS = len(SLOTS)
STEP_END = [max(i for i, (g, _) in enumerate(SLOTS) if g == gg) for gg in range(NG)]
STEP_START = [min(i for i, (g, _) in enumerate(SLOTS) if g == gg) for gg in range(NG)]
CHUNKS = [(g, c, e, j) for g in range(NG) for c in range(g + 1) for e in range(NE) for j in range(GT)]
NC = len(CHUNKS)
CHUNK_END = [max(i for i, ch in enumerate(CHUNKS) if ch[0] == gg) for gg in range(NG)]
CHUNK_START = [min(i for i, ch in enumerate(CHUNKS) if ch[0] == gg) for gg in range(NG)]
SCORE_RING, CHUNK_RING = 3, 3
NP_RING = 5
NPAIR = NS // 2
PAIR_LAG = 3


def chunk_width(g, c, j):
    return (j + 1) * P if c == g else GW


def slot_shift(g, t):
    return max(0, t - GT * g) * P


def slot_width(i):
    return GW - slot_shift(*SLOTS[i])


def bank_of(n, ring):
    return n % NC % ring


def turns_since(n, ring):
    return min(d for d in range(1, 2 * ring) if bank_of(n - d, ring) == bank_of(n, ring))


SW = 2
def plan_head():
    LEAD_SLOTS = 3
    pieces = []
    for i in range(NS + PAIR_LAG + 1):
        if i < NS:
            scores = [(("scores", i, e), i, SW * (slot_width(i) + (240 if slot_shift(*SLOTS[i]) or SLOTS[i][1] == GT * SLOTS[i][0] else 0)))
                      for e in range(NE)]
        else:
            scores = []
        pieces += scores[:3]
        if 1 <= i <= NS:
            pieces.append((("values", i - 1), i, 4 * slot_width(i - 1) + 190))
        pieces += scores[3:]
        done = i - PAIR_LAG - 1
        if done >= 0 and done % 2 == 0:
            pieces.append((("sums", done // 2), i, 4 * slot_width(done) + 190))
    cost = [chunk_width(g, c, j) + CHUNK_FIXED for g, c, _, j in CHUNKS]
    pace = sum(cost) / sum(width for _, _, width in pieces)
    for lead in range(CHUNK_END[0] + 1, NC):
        steps, n, behind = [], lead, 0.0
        slot_at = {}
        for piece, i, width in pieces:
            steps.append(piece)
            behind += width * pace
            while n < NC + lead and (behind > cost[n % NC] / 2 or piece is pieces[-1][0]):
                steps.append(("chunk", n))
                slot_at[n] = i
                behind -= cost[n % NC]
                n += 1
        if all(slot_at.get(CHUNK_END[g], 0) <= STEP_START[g] - LEAD_SLOTS for g in range(1, NG)):
            return lead, steps, slot_at
    raise ValueError("no lead is enough")


CHUNK_FIXED = 120
LEAD, HEAD_STEPS, CHUNK_SLOT = plan_head()


def build(nc, a, out):
    k_scratch = nc.dram_tensor("k_scratch", (2, NH, D, S), F32, kind="Internal").ap()
    q_scratch = nc.dram_tensor("q_scratch", (2, NH, NE, D, S), F32, kind="Internal").ap()
    sx_scratch = nc.dram_tensor("sx_scratch", (NH, D, S), F32, kind="Internal").ap()
    sum_scratch = nc.dram_tensor("sum_scratch", (NH, NE, S), F32, kind="Internal").ap()
    with ExitStack() as ctx:
        def sb(name, shape, dt=F32):
            return ctx.enter_context(nc.sbuf_tensor(name, shape, dt))

        t = {
            "ident": sb("ident", [P, P]),
            "mask_add": sb("mask_add", [P, GW]),
            "ident_bf": sb("ident_bf", [P, P], BF16),
            "mask_kq": sb("mask_kq", [P, P], BF16),
            "x1": sb("x1", [P, NT, H]),
            "xn": sb("xn", [P, NT, H]),
        }
        graph(nc, a, t)
        t["sxT"] = sb("sxT", [P, S])
        t["gate_w"] = sb("gate_w", [NH * NE, P])
        t["gate_b"] = sb("gate_b", [P, NH * NE])
        t["fc_w"] = sb("fc_w", [D, 2, P])
        t["fc_b"] = sb("fc_b", [P, 2])
        t["fgate_w"] = sb("fgate_w", [NH, P])
        for name in ("ln_g", "ln_b", "fnorm_g", "fnorm_b"):
            t[name] = sb(name, [P, D])
        t["v_all"] = sb("v_all", [P, NH, NT, D])
        t["heads_out"] = sb("heads_out", [P, NH, S])
        project(nc, a, t, k_scratch, q_scratch, sx_scratch)
        attend(nc, t, k_scratch, q_scratch, sx_scratch, sum_scratch)
        finish(nc, a, t, sum_scratch, out)


def graph(nc, a, t):
    UNITS, GROUP_END = [], []
    for g in range(NG):
        for c in range(NT):
            UNITS.append((g, c, True))
            if c // GT == g:
                UNITS += [(g2, c, False) for g2 in range(g)]
        GROUP_END.append(len(UNITS) - 1)
    STRIP_RING, COPY_RING = 4, 6
    operands = [u for u, x in enumerate(UNITS) if x[2]]
    operand_no = {u: n for n, u in enumerate(operands)}
    PRODUCTS = [u for u, (g, c, op) in enumerate(UNITS) if not op or c // GT <= g]
    product_no = {u: n for n, u in enumerate(PRODUCTS)}

    with ExitStack() as ctx:
        def sb(name, shape, dt=F32):
            return ctx.enter_context(nc.sbuf_tensor(name, shape, dt))

        def sem(name):
            return ctx.enter_context(nc.semaphore(name))

        adj = sb("adj", [P, NT, S])
        x = sb("x_in", [P, NT, H])
        xn = t["xn"]
        xnT = sb("xnT", [P, S])
        y = sb("y", [P, NT, H])
        copies = sb("copies", [P, COPY_RING, GW])
        junk = sb("junk", [P, 2, GW])
        accT = sb("accT", [P, GW])
        w12 = sb("w12", [P, 2, H])
        w3 = sb("w3", [P, H])
        bias = sb("bias", [P, 1])
        stats = sb("stats", [P, NT, 6])
        mean_var = sb("mean_var", [P, NT, 2])
        var_eps = sb("var_eps", [P, NT])
        std = sb("std", [P, NT])
        rstd = sb("rstd", [P, NT])
        edge_parts = sb("edge_parts", [P, NT, NG])
        edge = sb("edge", [P, NT])
        strips = [ctx.enter_context(nc.psum_tensor(f"strip{i}", [P, GW], F32)) for i in range(STRIP_RING)]
        acc = [ctx.enter_context(nc.psum_tensor(f"acc{i}", [P, GW], F32)) for i in range(2)]
        misc = [ctx.enter_context(nc.psum_tensor(f"misc{i}", [P, GT, P], F32)) for i in range(2)]

        x_in, w_in = sem("x_in_sem"), sem("w_in")
        adj_in = [sem(f"adj_in{g}") for g in range(NG)]
        consts, const_steps = sem("consts"), sem("const_steps")
        dve_chain = sem("dve_chain")
        var_ready, std_ready, xn_ready = sem("var_ready"), sem("std_ready"), sem("xn_ready")
        xnT_full, xnT_ready = sem("xnT_full"), sem("xnT_ready")
        y_full, y_ready = sem("y_full"), sem("y_ready")
        strip_full, strip_copied = sem("strip_full"), sem("strip_copied")
        strip_used, product_done = sem("strip_used"), sem("product_done")
        acc_step, acc_copied = sem("acc_step"), sem("acc_copied")
        h_full, h_used = sem("h_full"), sem("h_used")
        x1_stats = sem("x1_stats")
        block = ctx.enter_context(nc.Block())

        adj_v = a["adj"].rearrange("(i p) j -> i p j", p=P)

        @block.sync
        def _(sp):
            sp.dma_start(x[:], a["x"].rearrange("(i p) d -> p i d", p=P)).then_inc(x_in, 16)
            sp.dma_start(w12[:], a["gnn_weight"][0:2 * H, :].rearrange("(k p) d -> p k d", p=P)).then_inc(w_in, 16)
            sp.dma_start(w3[:], a["gnn_weight"][2 * H, :].partition_broadcast(P)).then_inc(w_in, 16)
            sp.dma_start(bias[:], a["gnn_bias"].rearrange("(p o) -> p o", o=1)).then_inc(w_in, 16)
            for i in range(NT):
                sp.dma_start(adj[:, i, :], adj_v[i]).then_inc(adj_in[i // GT], 16)

        @block.gpsimd
        def _(pool):
            pool.memset(t["ident"][:], 0.0).then_inc(const_steps, 1)
            pool.memset(t["mask_add"][:], 0.0).then_inc(const_steps, 1)
            pool.memset(t["ident_bf"][:], 0.0).then_inc(const_steps, 1)
            pool.memset(t["mask_kq"][:], 0.0).then_inc(const_steps, 1)
            pool.wait_ge(const_steps, 4)
            for m in (t["ident"], t["ident_bf"]):
                pool.affine_select(out=m[:], in_=m[:], compare_op=ALU.not_equal, fill=1.0, base=0,
                                   pattern=[[-1, P]], channel_multiplier=1).then_inc(consts, 1)
            pool.affine_select(out=t["mask_add"][:, GW - P:GW], in_=t["mask_add"][:, GW - P:GW], compare_op=ALU.is_ge,
                               fill=NEG, base=0, pattern=[[-1, P]], channel_multiplier=1).then_inc(consts, 1)
            pool.affine_select(out=t["mask_kq"][:], in_=t["mask_kq"][:], compare_op=ALU.is_ge, fill=NEG, base=0,
                               pattern=[[1, P]], channel_multiplier=-1).then_inc(consts, 1)

        @block.vector
        def _(dve):
            chain = [0]

            def link(ins):
                chain[0] += 1
                ins.then_inc(dve_chain, 1)
                dve.wait_ge(dve_chain, chain[0])

            def norm(src, dst, done):
                for i in range(NT):
                    last = dve.bn_stats(stats[:, i, :], src[:, i, :])
                link(last)
                for i in range(NT):
                    last = dve.bn_aggr(mean_var[:, i, :], stats[:, i, :])
                link(last)
                dve.tensor_scalar(var_eps[:], mean_var[:, :, 1], GNN_EPS, None, ALU.add).then_inc(var_ready, 1)
                dve.wait_ge(std_ready, done)
                link(dve.reciprocal(rstd[:], std[:]))
                for i in range(NT):
                    last = dve.tensor_scalar(dst[:, i, :], src[:, i, :], mean_var[:, i, 0:1], rstd[:, i:i + 1],
                                             ALU.subtract, ALU.mult)
                    if i % GT == GT - 1:
                        last.then_inc(xn_ready, 1)

            dve.wait_ge(x_in, 16)
            norm(x, xn, 1)
            for g in range(NG):
                dve.wait_ge(y_full, g + 1)
                dve.tensor_copy(y[:, GT * g:GT * g + GT, :], misc[g % 2][:]).then_inc(y_ready, 1)

            def product(u):
                g, c, operand = UNITS[u]
                n = product_no[u]
                if operand:
                    dve.wait_ge(strip_copied, operand_no[u] + 1)
                    strip = copies[:, operand_no[u] % COPY_RING, :]
                else:
                    dve.wait_ge(strip_full, u + 1)
                    strip = strips[u % STRIP_RING][:]
                if n >= 2:
                    dve.wait_ge(product_done, n - 1)
                dve.tensor_tensor_reduce(
                    out=junk[:, n % 2, :], in0=strip, in1=adj[:, c, GW * g:GW * g + GW], scale=1.0, scalar=0.0,
                    op0=ALU.mult, op1=ALU.add, accum_out=edge_parts[:, c, g:g + 1]).then_inc(product_done, 1)

            for u, (g, c, _) in enumerate(UNITS):
                if u in product_no:
                    product(u)
                if u in GROUP_END:
                    gg = GROUP_END.index(u)
                    dve.wait_ge(h_full, gg + 1)
                    dve.tensor_tensor(t["x1"][:, GT * gg:GT * gg + GT, :], misc[gg % 2][:],
                                      x[:, GT * gg:GT * gg + GT, :], ALU.add).then_inc(h_used, 1)
            dve.wait_ge(product_done, len(PRODUCTS))
            dve.wait_ge(h_used, NG)
            link(dve.reduce_sum(edge[:], edge_parts[:], AX))
            for i in range(NT):
                last = dve.scalar_tensor_tensor(out=t["x1"][:, i, :], in0=w3[:], scalar=edge[:, i:i + 1],
                                                in1=t["x1"][:, i, :], op0=ALU.mult, op1=ALU.add)
            link(last)
            norm(t["x1"], xn, 2)

        @block.scalar
        def _(act):
            act.wait_ge(var_ready, 1)
            act.activation(std[:], var_eps[:], ACT.Sqrt).then_inc(std_ready, 1)
            for g in range(NG):
                act.wait_ge(xnT_full, g + 1)
                act.activation(xnT[:, GW * g:GW * g + GW], acc[g % 2][:], ACT.Copy).then_inc(xnT_ready, 1)
            act.wait_ge(w_in, 48)
            for u, (g, c, operand) in enumerate(UNITS):
                if operand:
                    n = operand_no[u]
                    act.wait_ge(strip_full, u + 1)
                    if n >= COPY_RING:
                        act.wait_ge(acc_step, n - COPY_RING + 1)
                        before = [product_no[v] for v in PRODUCTS
                                  if UNITS[v][2] and operand_no[v] <= n - COPY_RING]
                        if before:
                            act.wait_ge(product_done, max(before) + 1)
                    act.activation(copies[:, n % COPY_RING, :], strips[u % STRIP_RING][:],
                                   ACT.Copy).then_inc(strip_copied, 1)
                    if c == NT - 1:
                        act.wait_ge(acc_step, n + 1)
                        if g:
                            act.wait_ge(h_full, g)
                        act.activation(accT[:], acc[g % 2][:], ACT.Identity, bias=bias[:]).then_inc(acc_copied, 1)
            act.wait_ge(var_ready, 2)
            act.activation(std[:], var_eps[:], ACT.Sqrt).then_inc(std_ready, 1)

        @block.tensor
        def _(pe):
            pe.wait_ge(consts, 4)
            for g in range(NG):
                pe.wait_ge(xn_ready, g + 1)
                if g >= 2:
                    pe.wait_ge(xnT_ready, g - 1)
                for j in range(GT):
                    last = pe.transpose(acc[g % 2][:, P * j:P * j + P], xn[:, GT * g + j, :], t["ident"][:])
                last.then_inc(xnT_full, 1)
            pe.wait_ge(w_in, 48)
            for g in range(NG):
                pe.wait_ge(xnT_ready, g + 1)
                if g >= 2:
                    pe.wait_ge(y_ready, g - 1)
                for j in range(GT):
                    i = GT * g + j
                    last = pe.matmul(misc[g % 2][:, j, :], xnT[:, P * i:P * i + P], w12[:, 1, :],
                                     start=True, stop=True)
                last.then_inc(y_full, 1)
            pe.wait_ge(y_ready, NG)

            def transposes(u):
                g, c, _ = UNITS[u]
                if u >= STRIP_RING:
                    v = u - STRIP_RING
                    if UNITS[v][2]:
                        pe.wait_ge(strip_copied, operand_no[v] + 1)
                    else:
                        pe.wait_ge(product_done, product_no[v] + 1)
                for j in range(GT):
                    last = pe.transpose(strips[u % STRIP_RING][:, P * j:P * j + P],
                                        adj[:, GT * g + j, P * c:P * c + P], t["ident"][:])
                last.then_inc(strip_full, 1)

            def products(u):
                g, c, operand = UNITS[u]
                if operand:
                    n = operand_no[u]
                    if c == 0:
                        if g >= 2:
                            pe.wait_ge(acc_copied, g - 1)
                        pe.matmul(acc[g % 2][:], w12[:, 0, :], xnT[:, GW * g:GW * g + GW], start=True, stop=False)
                    pe.wait_ge(strip_copied, n + 1)
                    pe.matmul(acc[g % 2][:], y[:, c, :], copies[:, n % COPY_RING, :], start=False,
                              stop=(c == NT - 1)).then_inc(acc_step, 1)
                    if c == NT - 1:
                        pe.wait_ge(acc_copied, g + 1)
                        if g >= 2:
                            pe.wait_ge(h_used, g - 1)
                        for j in range(GT):
                            last = pe.transpose(misc[g % 2][:, j, :], accT[:, P * j:P * j + P], t["ident"][:])
                        last.then_inc(h_full, 1)

            AHEAD = 2
            for u in range(len(UNITS) + AHEAD):
                if u < len(UNITS):
                    g, c, operand = UNITS[u]
                    if operand and c == 0:
                        pe.wait_ge(adj_in[g], 16 * GT)
                    transposes(u)
                if u >= AHEAD:
                    products(u - AHEAD)



def project(nc, a, t, k_scratch, q_scratch, sx_scratch):
    with ExitStack() as ctx:
        def sb(name, shape, dt=F32):
            return ctx.enter_context(nc.sbuf_tensor(name, shape, dt))

        def sem(name):
            return ctx.enter_context(nc.semaphore(name))

        hl_w = sb("hl_w_in", [P, H])
        hl_wT = sb("hl_wT", [P, P])
        hl_b = sb("hl_b", [P, 1])
        kv_w = sb("kv_w", [D, 2, P])
        kv_wT = sb("kv_wT", [P, 2, P])
        q_w = sb("q_w", [P, NH, D])
        q_wT = sb("q_wT", [P, P])
        xnT = sb("xnT2", [P, S])
        sxT = t["sxT"]
        hi = sb("hi", [P, 3, GW], F32R)
        lo = sb("lo", [P, 3, GW], F32R)
        pt = [ctx.enter_context(nc.psum_tensor(f"pt{i}", [P, GW], F32)) for i in range(2)]
        pw = ctx.enter_context(nc.psum_tensor("pw", [P, 4, P], F32))
        pq = [ctx.enter_context(nc.psum_tensor(f"pq{i}", [P, GW], F32)) for i in range(3)]

        w_in = sem("project_w_in")
        wT_full, wT_ready, zeroed = sem("wT_full"), sem("wT_ready"), sem("zeroed")
        x_full, x_ready = sem("x_full"), sem("x_ready")
        sx_full, sx_ready = sem("sx_full"), sem("sx_ready")
        part_full, hi_ready, lo_ready, part_out = sem("part_full"), sem("hi_ready"), sem("lo_ready"), sem("part_out")
        hi_out = [sem(f"hi_out{i}") for i in range(3)]
        sx_out, late_w_in = sem("sx_out"), sem("late_w_in")
        v_full, v_ready = sem("v_full"), sem("v_ready")
        block = ctx.enter_context(nc.Block())

        PARTS = [("k", 0, g) for g in range(NG)] + [("q", n, g) for n in range(NH) for g in range(NG)]
        xnT_v = t["xn"]

        @block.sync
        def _(sp):
            sp.dma_start(hl_w[:], a["ffn_hl_w"].rearrange("n d h -> (n d) h")).then_inc(w_in, 16)
            sp.dma_start(hl_b[:], a["ffn_hl_b"].rearrange("n (d o) -> (n d) o", o=1)).then_inc(w_in, 16)
            sp.dma_start(kv_w[:, 0, :].rearrange("o (n d) -> o n d", n=NH),
                         a["ffn_wk"].rearrange("n o d -> o n d")).then_inc(w_in, 16)
            sp.dma_start(kv_w[:, 1, :].rearrange("o (n d) -> o n d", n=NH),
                         a["ffn_wv"].rearrange("n o d -> o n d")).then_inc(w_in, 16)
            sp.dma_start(q_w[:], a["ffn_wq"].rearrange("n e o d -> (e o) n d")).then_inc(w_in, 16)
            sp.dma_start(t["gate_w"][:], a["ffn_gate_w"].rearrange("n e f -> (n e) f")).then_inc(late_w_in, 16)
            sp.dma_start(t["fgate_w"][:], a["ffn_fgate_w"]).then_inc(late_w_in, 16)
            for name in ("ln_g", "ln_b", "fnorm_g", "fnorm_b"):
                sp.dma_start(t[name][:], a["ffn_" + name].partition_broadcast(P)).then_inc(late_w_in, 16)
            sp.dma_start(t["gate_b"][:], a["ffn_gate_b"].rearrange("n e -> (n e)").partition_broadcast(P))\
                .then_inc(late_w_in, 16)
            for n in range(NH):
                rows = slice(D * n, D * n + D)
                for k, layer in enumerate(("fc1", "fc2")):
                    sp.dma_start(t["fc_w"][:, k, rows], a[f"ffn_{layer}_w"]).then_inc(late_w_in, 16)
                    sp.dma_start(t["fc_b"][rows, k:k + 1],
                                 a[f"ffn_{layer}_b"].rearrange("(d o) -> d o", o=1)).then_inc(late_w_in, 16)
            sp.wait_ge(sx_ready, NG)
            sp.dma_start(sx_scratch.rearrange("n d s -> (n d) s"), sxT[:]).then_inc(sx_out, 16)
            for i, (what, n, g) in enumerate(PARTS):
                cols = slice(GW * g, GW * g + GW)
                for part, ready, src in ((0, hi_ready, hi), (1, lo_ready, lo)):
                    if what == "k":
                        dst = k_scratch[part].rearrange("n o s -> (n o) s")[:, cols]
                    else:
                        dst = q_scratch[part, n].rearrange("e o s -> (e o) s")[:, cols]
                    sp.wait_ge(ready, i + 1)
                    sp.dma_start(dst, src[:, i % 3, :].bitcast(F32)).then_inc(hi_out[i % 3], 16)
            sp.wait_ge(sx_out, 16)
            sp.wait_ge(late_w_in, 16 * (7 + 4 * NH))
            for i in range(3):
                sp.wait_ge(hi_out[i], 32 * len(range(i, len(PARTS), 3)))

        @block.tensor
        def _(pe):
            pe.wait_ge(w_in, 80)
            pe.transpose(pw[:, 0, :], hl_w[:], t["ident"][:])
            pe.transpose(pw[:, 1, 0:D], kv_w[:, 0, :], t["ident"][0:D, 0:D])
            pe.transpose(pw[:, 2, 0:D], kv_w[:, 1, :], t["ident"][0:D, 0:D])
            pe.transpose(pw[:, 3, :], q_w[:].rearrange("p n d -> p (n d)"), t["ident"][:]).then_inc(wT_full, 1)
            for g in range(NG):
                if g >= 2:
                    pe.wait_ge(x_ready, g - 1)
                for j in range(GT):
                    last = pe.transpose(pt[g % 2][:, P * j:P * j + P], xnT_v[:, GT * g + j, :], t["ident"][:])
                last.then_inc(x_full, 1)
            pe.wait_ge(wT_ready, 1)
            for g in range(NG):
                pe.wait_ge(x_ready, max(g + 1, min(g + 3, NG)))
                if g >= 2:
                    pe.wait_ge(sx_ready, g - 1)
                pe.matmul(pt[g % 2][:], hl_wT[:], xnT[:, GW * g:GW * g + GW], start=True, stop=True).then_inc(sx_full, 1)
            for i, (what, n, g) in enumerate(PARTS):
                pe.wait_ge(sx_ready, g + 1 if i < NG else NG)
                if i >= 3:
                    pe.wait_ge(lo_ready, i - 2)
                cols = slice(GW * g, GW * g + GW)
                if what == "k":
                    last = pe.matmul(pq[i % 3][:], kv_wT[:, 0, :], sxT[:, cols], start=True, stop=True)
                else:
                    rows = slice(D * n, D * n + D)
                    last = pe.matmul(pq[i % 3][:], q_wT[rows, :], sxT[rows, cols], start=True, stop=True)
                last.then_inc(part_full, 1)
            for g in range(NG):
                if g >= 2:
                    pe.wait_ge(v_ready, g - 1)
                else:
                    pe.wait_ge(sx_ready, NG)
                for j in range(GT):
                    i = GT * g + j
                    last = pe.matmul(pt[g % 2][:, P * j:P * j + P], sxT[:, P * i:P * i + P], kv_wT[:, 1, :],
                                     start=True, stop=True)
                last.then_inc(v_full, 1)

        @block.scalar
        def _(act):
            for g in range(NG):
                act.wait_ge(x_full, g + 1)
                act.activation(xnT[:, GW * g:GW * g + GW], pt[g % 2][:], ACT.Copy).then_inc(x_ready, 1)
            for g in range(NG):
                act.wait_ge(sx_full, g + 1)
                act.activation(sxT[:, GW * g:GW * g + GW], pt[g % 2][:], ACT.Identity, bias=hl_b[:]).then_inc(sx_ready, 1)
            for i in range(len(PARTS)):
                act.wait_ge(part_full, i + 1)
                if i >= 3:
                    act.wait_ge(hi_out[i % 3], 32 * (i // 3))
                act.activation(hi[:, i % 3, :], pq[i % 3][:], ACT.Copy).then_inc(hi_ready, 1)

        @block.vector
        def _(dve):
            dve.memset(kv_wT[:], 0.0).then_inc(zeroed, 1)
            dve.wait_ge(zeroed, 1)
            dve.wait_ge(wT_full, 1)
            dve.tensor_copy(hl_wT[:], pw[:, 0, :])
            for k in range(2):
                for n in range(NH):
                    rows = slice(D * n, D * n + D)
                    dve.tensor_copy(kv_wT[rows, k, rows], pw[rows, 1 + k, 0:D])
            dve.tensor_copy(q_wT[:], pw[:, 3, :]).then_inc(wT_ready, 1)
            for i in range(len(PARTS)):
                dve.wait_ge(hi_ready, i + 1)
                if i >= 3:
                    dve.wait_ge(hi_out[i % 3], 32 * (i // 3))
                dve.tensor_tensor(lo[:, i % 3, :], pq[i % 3][:], hi[:, i % 3, :].bitcast(F32),
                                  ALU.subtract).then_inc(lo_ready, 1)
            for g in range(NG):
                dve.wait_ge(v_full, g + 1)
                dve.tensor_copy(t["v_all"][:, :, GT * g:GT * g + GT, :].rearrange("p n t o -> p t n o"),
                                pt[g % 2][:].rearrange("p (t n o) -> p t n o", t=GT, n=NH)).then_inc(v_ready, 1)


def attend(nc, t, k_scratch, q_scratch, sx_scratch, sum_scratch):
    with ExitStack() as ctx:
        def sb(name, shape, dt=F32):
            return ctx.enter_context(nc.sbuf_tensor(name, shape, dt))

        def sem(name):
            return ctx.enter_context(nc.semaphore(name))

        keys = sb("keys", [KR + 1, S], F32R)
        keys_max = sb("keys_max", [KR, S], F32R)
        queries = [sb(f"queries{g}", [KR + 1, NE, GW], F32R) for g in range(NG)]
        values = sb("values", [P, NT, D])
        ones = sb("ones", [P, D])
        features = sb("features", [P, GW])
        probs = sb("probs", [P, NP_RING, NE, GW])
        masked_chunk = sb("masked_chunk", [P, 2, GW])
        chunk_max = sb("chunk_max", [P, NE * GT, NG])
        row_max = sb("row_max", [P, NE * GT])
        neg_max = sb("neg_max", [P, D], F32R)
        neg_maxT = sb("neg_maxT", [P, D], F32R)
        pair_probs = sb("pair_probs", [P, 2, NE, GW])
        sums_row = sb("sums_row", [P, 2, GW])
        scores = [ctx.enter_context(nc.psum_tensor(f"scores{i}", [P, GW], F32)) for i in range(SCORE_RING)]
        chunk = [ctx.enter_context(nc.psum_tensor(f"chunk{i}", [P, GW], F32)) for i in range(CHUNK_RING)]
        outT = ctx.enter_context(nc.psum_tensor("outT", [P, GW], F32))
        sums = ctx.enter_context(nc.psum_tensor("sums", [P, GW], F32))

        ones_ready, key_ones_ready = sem("ones_ready"), sem("key_ones_ready")
        keys_in = [sem(f"keys_in{c}") for c in range(NG)]
        values_in = [sem(f"values_in{c}") for c in range(NG)]
        queries_in = [sem(f"queries_in{g}") for g in range(NG)]
        keys_max_in = [sem(f"keys_max_in{c}") for c in range(NG)]
        features_in = sem("features_in")
        max_row_in = [sem(f"max_row_in{g}") for g in range(NG)]
        scores_full, scores_used = sem("scores_full"), sem("scores_used")
        probs_used = sem("probs_used")
        chunk_full, chunk_used, diagonal_seen = sem("chunk_full"), sem("chunk_used"), sem("diagonal_seen")
        row_max_ready, neg_ready, neg_maxT_ready = sem("row_max_ready"), sem("neg_ready"), sem("neg_maxT_ready")
        pair_ready, pair_summed = sem("pair_ready"), sem("pair_summed")
        out_used, sums_used = sem("out_used"), sem("sums_used")
        sums_out = [sem(f"sums_out{i}") for i in range(2)]
        block = ctx.enter_context(nc.Block())

        SCALE = float(D) ** 0.5
        PAIR_CREDIT = 3

        def load_keys(sp, h, c):
            for r, part in enumerate((0, 1, 0)):
                sp.dma_start(keys[D * r:D * r + D, GW * c:GW * c + GW].bitcast(F32),
                             k_scratch[part, h, :, GW * c:GW * c + GW]).then_inc(keys_in[c], 16)

        def load_keys_max(sp, h, c):
            for r, part in enumerate((0, 1, 0)):
                sp.dma_start(keys_max[D * r:D * r + D, GW * c:GW * c + GW].bitcast(F32),
                             k_scratch[part, h, :, GW * c:GW * c + GW]).then_inc(keys_max_in[c], 16)

        def load_queries(sp, h, g):
            for r, part in enumerate((0, 0, 1)):
                sp.dma_start(queries[g][D * r:D * r + D, :, :].bitcast(F32),
                             q_scratch[part, h].rearrange("e o s -> o e s")[:, :, GW * g:GW * g + GW])\
                    .then_inc(queries_in[g], 16)

        def load_values(sp, h, c):
            sp.dma_start(values[:, GT * c:GT * c + GT, :],
                         t["v_all"][:, h, GT * c:GT * c + GT, :]).then_inc(values_in[c], 16)

        def load_features(sp, h, g):
            for e in range(NE):
                sp.dma_start(features[D * e:D * e + D, :], sx_scratch[h, :, GW * g:GW * g + GW]).then_inc(features_in, 16)

        def place_max_row(sp, step, g):
            sp.wait_ge(neg_maxT_ready, step + 1)
            for quadrant in range(4):
                q0 = D * quadrant
                sp.dma_start(queries[g][KR:KR + 1, :, :].rearrange("r e (j f) -> r (e j) f", f=P)[:, :, q0:q0 + D].bitcast(F32),
                             neg_maxT[q0:q0 + NE * GT, :].bitcast(F32)).then_inc(max_row_in[g], 16)

        def sp_head(sp, h, last):
            events = []
            for g in range(NG):
                step_end = STEP_END[g]

                def next_queries(g=g, i=step_end):
                    sp.wait_ge(scores_full, (h * NS + i + 1) * NE)
                    load_queries(sp, h + 1, g)
                if not last:
                    events.append((step_end + 0.5, next_queries))

                def feat(g=g):
                    sp.wait_ge(out_used, h * NG + g + 2)
                    if g + 1 < NG:
                        load_features(sp, h, g + 1)
                    else:
                        load_features(sp, h + 1, 0)
                if not (last and g == NG - 1):
                    events.append((step_end + 0.9, feat))

                def sums_to_dram(g=g):
                    sp.wait_ge(sums_used, h * NG + g + 2)
                    sp.dma_start(sum_scratch[h, :, GW * g:GW * g + GW],
                                 sums_row[0:D * (NE - 1) + 1:D, g % 2, :]).then_inc(sums_out[g % 2], 16)
                events.append((step_end + PAIR_LAG + 1.0, sums_to_dram))
                if not last:
                    slot = STEP_START[NG - 1] + GT * g + GT - 1

                    def next_keys(c=g, i=slot):
                        sp.wait_ge(scores_full, (h * NS + i + 1) * NE)
                        load_keys(sp, h + 1, c)

                    def next_values(c=g, i=slot):
                        sp.wait_ge(probs_used, h * NS + NP_RING + i + 1)
                        load_values(sp, h + 1, c)
                    events.append((slot + 0.4, next_keys))
                    events.append((slot + 1.6, next_values))
                for dh in (0, 1):
                    at = dh * NC + CHUNK_END[g]
                    if at >= LEAD and at < LEAD + NC and not (last and dh):
                        def row(dh=dh, g=g):
                            place_max_row(sp, (h + dh) * NG + g, g)
                        events.append((CHUNK_SLOT[at] + 0.7, row))
                if not last:
                    reader = max(n for n, ch in enumerate(CHUNKS) if ch[1] == g)

                    def next_keys_max(c=g, n=reader):
                        sp.wait_ge(chunk_full, h * NC + n + 1)
                        load_keys_max(sp, h + 1, c)
                    events.append((CHUNK_SLOT[reader] + 0.3, next_keys_max))
            for _, do in sorted(events, key=lambda x: x[0]):
                do()

        @block.sync
        def _(sp):
            for i in range(2):
                sp.sem_inc(sums_out[i], 16)
            load_queries(sp, 0, 0)
            for c in range(NG):
                load_keys_max(sp, 0, c)
            for c in range(NG):
                load_keys(sp, 0, c)
                load_values(sp, 0, c)
                if c:
                    load_queries(sp, 0, c)
            load_features(sp, 0, 0)
            for g in range(NG):
                if CHUNK_END[g] < LEAD:
                    place_max_row(sp, g, g)
            with sp.Fori(0, NH - 1) as h:
                sp_head(sp, h, False)
            sp_head(sp, NH - 1, True)
            for i in range(2):
                sp.wait_ge(sums_out[i], 16 + 8 * NH * NG)

        def pe_chunk(pe, h, i):
            g, c, e, j = CHUNKS[i % NC]
            head = h + i // NC
            if (e, j, c) == (0, 0, 0):
                pe.wait_ge(queries_in[g], head * 48 + 48)
            if (e, j, c) == (0, 0, g):
                pe.wait_ge(keys_max_in[c], head * 48 + 48)
            pe.wait_ge(chunk_used, h * NC + i + 1 + CHUNK_RING - turns_since(i, CHUNK_RING))
            n = chunk_width(g, c, j)
            pe.matmul(chunk[bank_of(i, CHUNK_RING)][:, 0:n], queries[g][0:KR, e, P * j:P * j + P], keys_max[:, GW * c:GW * c + n],
                      start=True, stop=True).then_inc(chunk_full, 1)

        def pe_scores(pe, h, i, e):
            g, k = SLOTS[i]
            shift = slot_shift(g, k)
            if i == STEP_START[g] and e == 0:
                pe.wait_ge(max_row_in[g], h * 64 + 64)
                pe.wait_ge(keys_in[g], h * 48 + 48)
            n = NE * i + e
            pe.wait_ge(scores_used, (h * NS + i) * NE + e + 1 + SCORE_RING - turns_since(n, SCORE_RING))
            diagonal = k >= GT * g
            if diagonal:
                pe.matmul(scores[bank_of(n, SCORE_RING)][:, 0:P], t["ident_bf"][:], t["mask_kq"][:], start=True, stop=False,
                          skip_group_check=True)
            pe.matmul(scores[bank_of(n, SCORE_RING)][:, 0:GW - shift], keys[:, P * k:P * k + P], queries[g][:, e, shift:GW],
                      start=not diagonal, stop=True, skip_group_check=diagonal).then_inc(scores_full, 1)

        def pe_values(pe, h, i):
            g, k = SLOTS[i]
            shift = slot_shift(g, k)
            pe.wait_ge(scores_used, (h * NS + i + 1) * NE + SCORE_RING)
            if i == STEP_START[g]:
                pe.wait_ge(values_in[g], h * 16 + 16)
                pe.wait_ge(out_used, h * NG + g + 1)
            for e in range(NE):
                last = pe.matmul(outT[D * e:D * e + D, shift:GW], values[:, k, :],
                                 probs[:, i % NP_RING, e, 0:GW - shift], start=(k == 0), stop=(i == STEP_END[g]))
            last.then_inc(probs_used, 1)

        def pe_sums(pe, h, pair):
            i = 2 * pair
            g, k = SLOTS[i]
            shift, shift2 = slot_shift(g, k), slot_shift(g, k + 1)
            pe.wait_ge(pair_ready, h * NPAIR + pair + 1)
            if i == STEP_START[g]:
                pe.wait_ge(sums_used, h * NG + g + 1)
            if shift2 > shift:
                for e in range(NE):
                    pe.matmul(sums[D * e:D * e + D, shift:shift2], ones[:],
                              probs[:, i % NP_RING, e, 0:shift2 - shift], start=(k == 0), stop=False)
            for e in range(NE):
                last = pe.matmul(sums[D * e:D * e + D, shift2:GW], ones[:], pair_probs[:, pair % 2, e, 0:GW - shift2],
                                 start=(k == 0 and shift2 == shift), stop=(i + 1 == STEP_END[g]))
            last.then_inc(pair_summed, 1)

        def pe_head(pe, h, last):
            for what, n, *expert in HEAD_STEPS:
                if what == "scores":
                    pe_scores(pe, h, n, expert[0])
                elif what == "values":
                    pe_values(pe, h, n)
                elif what == "sums":
                    pe_sums(pe, h, n)
                elif not (last and n >= NC):
                    pe_chunk(pe, h, n)

        @block.tensor
        def _(pe):
            pe.wait_ge(ones_ready, 2)
            pe.wait_ge(key_ones_ready, 1)
            for i in range(LEAD):
                pe_chunk(pe, 0, i)
            with pe.Fori(0, NH - 1) as h:
                pe_head(pe, h, False)
            pe_head(pe, NH - 1, True)

        def act_sums(act, h, g):
            act.wait_ge(pair_summed, h * NPAIR + PAIR_CREDIT + STEP_END[g] // 2 + 1)
            act.wait_ge(sums_out[g % 2], h * (8 * NG) + g // 2 * 16 + 16)
            act.activation(sums_row[:, g % 2, :], sums[:], ACT.Copy).then_inc(sums_used, 1)

        def act_head(act, h):
            for i in range(NS + 1):
                if i < NS:
                    g, k = SLOTS[i]
                    n = GW - slot_shift(g, k)
                    act.wait_ge(probs_used, h * NS + i + 1)
                    act.wait_ge(pair_summed, h * NPAIR + PAIR_CREDIT + (i - NP_RING) // 2 + 1)
                    for e in range(NE):
                        act.wait_ge(scores_full, (h * NS + i) * NE + e + 1)
                        act.activation(probs[:, i % NP_RING, e, 0:n], scores[bank_of(NE * i + e, SCORE_RING)][:, 0:n],
                                       ACT.Exp, scale=SCALE).then_inc(scores_used, 1)
                for g in range(NG):
                    if i == min(STEP_END[g] + PAIR_LAG + 1, NS):
                        act_sums(act, h, g)

        @block.scalar
        def _(act):
            act.sem_inc(scores_used, SCORE_RING)
            act.sem_inc(sums_used, 1)
            with act.Fori(0, NH - 1) as h:
                act_head(act, h)
            act_head(act, NH - 1)

        def dve_chunk(dve, h, i):
            g, c, e, j = CHUNKS[i % NC]
            n = chunk_width(g, c, j)
            step = (h + i // NC) * NG + g
            first = CHUNK_END[g - 1] + 1 if g else 0
            if i % NC == first and not (isinstance(step, int) and step == 0):
                dve.wait_ge(row_max_ready, step)
            dve.wait_ge(chunk_full, h * NC + i + 1)
            if c < g:
                dve.reduce_max(chunk_max[:, GT * e + j, c:c + 1], chunk[bank_of(i, CHUNK_RING)][:, 0:n], AX).then_inc(chunk_used, 1)
            else:
                dve.wait_ge(chunk_used, h * NC + i - 1 + CHUNK_RING)
                dve.sem_inc(diagonal_seen, 1)
                dve.tensor_tensor_reduce(
                    out=masked_chunk[:, i % 2, 0:n], in0=chunk[bank_of(i, CHUNK_RING)][:, 0:n], in1=t["mask_add"][:, GW - n:GW], scale=1.0,
                    scalar=-BIG, op0=ALU.add, op1=ALU.max, accum_out=chunk_max[:, GT * e + j, c:c + 1]).then_inc(chunk_used, 1)
            if i % NC == CHUNK_END[g]:
                dve.wait_ge(chunk_used, h * NC + i + 1 + CHUNK_RING)
                if not (isinstance(step, int) and step == 0):
                    dve.wait_ge(neg_ready, step)
                dve.reduce_max(row_max[:], chunk_max[:, :, 0:g + 1], AX).then_inc(row_max_ready, 1)
                dve.wait_ge(row_max_ready, step + 1)
                if not (isinstance(step, int) and step == 0):
                    dve.wait_ge(neg_maxT_ready, step)
                dve.tensor_scalar(neg_max[:, 0:NE * GT], row_max[:], -1.0, None, ALU.mult).then_inc(neg_ready, 1)
                dve.wait_ge(neg_ready, step + 1)
                g0, h0 = ((g - 1) % NG, h + i // NC - (1 if g == 0 else 0))
                if not (isinstance(step, int) and step == 0):
                    dve.wait_ge(max_row_in[g0], h0 * 64 + 64)
                dve.transpose(neg_maxT[:].bitcast(F32), neg_max[:].bitcast(F32)).then_inc(neg_maxT_ready, 1)

        def dve_step_end(dve, h, g):
            dve.wait_ge(probs_used, h * NS + NP_RING + STEP_END[g] + 1)
            dve.wait_ge(features_in, h * (64 * NG) + 64 * (g + 1))
            cols = slice(GW * g, GW * g + GW)
            place = (t["heads_out"][:, h, cols] if isinstance(h, int) else
                     t["heads_out"][:, bass.ds(h, 1), cols].rearrange("p a s -> p (a s)"))
            dve.scalar_tensor_tensor(out=place, in0=features[:], scalar=0.0, in1=outT[:],
                                     op0=ALU.not_equal, op1=ALU.mult).then_inc(out_used, 1)

        def dve_head(dve, h, last):
            for what, n, *_ in HEAD_STEPS:
                if what == "chunk" and not (last and n >= NC):
                    dve_chunk(dve, h, n)
                elif what == "values" and n in STEP_END:
                    dve_step_end(dve, h, STEP_END.index(n))

        @block.vector
        def _(dve):
            dve.sem_inc(chunk_used, CHUNK_RING)
            dve.sem_inc(out_used, 1)
            dve.memset(neg_max[:].bitcast(F32), 0.0).then_inc(ones_ready, 1)
            dve.memset(ones[:], 1.0).then_inc(ones_ready, 1)
            dve.wait_ge(ones_ready, 2)
            for i in range(LEAD):
                dve_chunk(dve, 0, i)
            with dve.Fori(0, NH - 1) as h:
                dve_head(dve, h, False)
            dve_head(dve, NH - 1, True)

        def pool_head(pool, h):
            for pair in range(NPAIR):
                i = 2 * pair
                g, k = SLOTS[i]
                apart = slot_shift(g, k + 1) - slot_shift(g, k)
                n = GW - slot_shift(g, k + 1)
                pool.wait_ge(scores_used, (h * NS + i + 2) * NE + SCORE_RING)
                pool.wait_ge(pair_summed, h * NPAIR + PAIR_CREDIT + pair - 1)
                pool.tensor_tensor(pair_probs[:, pair % 2, :, 0:n], probs[:, i % NP_RING, :, apart:apart + n],
                                   probs[:, (i + 1) % NP_RING, :, 0:n], ALU.add).then_inc(pair_ready, 1)

        @block.gpsimd
        def _(pool):
            pool.sem_inc(probs_used, NP_RING)
            pool.sem_inc(pair_summed, PAIR_CREDIT)
            pool.memset(keys[KR:KR + 1, :].bitcast(F32), 1.0).then_inc(key_ones_ready, 1)
            with pool.Fori(0, NH - 1) as h:
                pool_head(pool, h)
            pool_head(pool, NH - 1)


def finish(nc, a, t, sum_scratch, out):
    JN = GT * NH

    with ExitStack() as ctx:
        def sb(name, shape, dt=F32):
            return ctx.enter_context(nc.sbuf_tensor(name, shape, dt))

        def sem(name):
            return ctx.enter_context(nc.semaphore(name))

        gate_wT = sb("gate_wT", [P, NH, D])
        sums_in = sb("sums_in", [NH * NE, S])
        inv_sums = sb("inv_sums", [P, NG, JN, NE])
        logit_parts = sb("logit_parts", [P, NG, JN, NE, NE])
        fc_wT = sb("fc_wT", [P, 2, P])
        fgate_wT = sb("fgate_wT", [P, NH])
        logitsT = sb("logitsT", [P, NG, GW])
        small = {n: sb(n, [P, NG, JN]) for n in ("gate_max", "gate_sum", "gate_inv", "sum1", "var1", "vare1",
                                                 "std1", "rstd1", "sum2", "var2", "vare2", "std2", "rstd2")}
        tiny = {n: sb(n, [P, NG, GT]) for n in ("out_max", "out_sum", "out_inv")}
        gate = {n: sb(n, [P, NG, JN, NE]) for n in ("gate_logit0", "gate_logit", "gate_share0", "gate_shift", "gate_exp", "gate_share")}
        ogate = {n: sb(n, [P, NG, GT, NH]) for n in ("out_shift", "out_exp", "out_share")}
        shared = sb("shared", [P, 2, NH * NE, D])
        mixed = sb("mixed", [P, NG, JN, D])
        resid = sb("resid", [P, NG, JN, D])
        centred = sb("centred", [P, NG, JN, D])
        square = sb("square", [P, NG, JN, D])
        normed = sb("normed", [P, NG, JN, D])
        scaled = sb("scaled", [P, NG, JN, D])
        fx = sb("fx", [P, NG, JN, D])
        fxT = sb("fxT", [P, NG, GW])
        nonzero = sb("nonzero", [P, NG, GW])
        hidden = sb("hidden", [P, NG, GW])
        hidden_m = sb("hidden_m", [P, NG, GW])
        fc_out = sb("fc_out", [P, NG, GW])
        banks = [ctx.enter_context(nc.psum_tensor(f"bank{i}", [P, GW], F32)) for i in range(8)]

        names = ("wT_full2 wT_ready2 zeroed2 logits_full logits_ready tok_full shift_ready gexp_ready gsum_ready "
                 "ginv_ready share_ready heads_full heads_used mixed_ready feat_full resid_ready sum1_ready "
                 "centred1_ready square1_ready var1_ready vare1_ready std1_ready rstd1_ready normed1_ready "
                 "scaled1_ready fx_ready fxT_full fxT_ready nonzero_ready fc1_full hidden_ready masked_ready2 "
                 "fc2_full fc2_masked fc_out_ready back_full sum2_ready centred2_ready square2_ready var2_ready "
                 "vare2_ready std2_ready rstd2_ready normed2_ready scaled2_ready fout_ready foutT_full foutT_ready "
                 "olog_full omax_ready oshift_ready oexp_ready osum_ready oinv_ready oshare_ready gated_ready "
                 "result_ready result_out gmax_ready sums_in_sem sums_full inv_ready parts_ready logit0_ready logit_ready "
                 "share0_ready").split()
        s = {n: sem(n) for n in names}
        block = ctx.enter_context(nc.Block())

        def spread(ap, n):
            return ap.unsqueeze(2).to_broadcast([P, ap.shape[1], n])

        def each(vec):
            return vec.unsqueeze(1).to_broadcast([P, JN, D])

        def pairs(bank):
            return bank[:].rearrange("p (k d) -> p k d", d=D)

        @block.tensor
        def _(pe):
            ident = t["ident"][:]
            pe.transpose(banks[0][:, 0:NH * NE], t["gate_w"][:], t["ident"][0:NH * NE, 0:NH * NE])
            pe.transpose(banks[0][:, 128:128 + D], t["fc_w"][:, 0, :], t["ident"][0:D, 0:D])
            pe.transpose(banks[0][:, 256:256 + D], t["fc_w"][:, 1, :], t["ident"][0:D, 0:D])
            pe.transpose(banks[0][:, 384:384 + NH], t["fgate_w"][:], t["ident"][0:NH, 0:NH]).then_inc(s["wT_full2"], 1)
            pe.wait_ge(s["wT_ready2"], 1)
            pe.wait_ge(s["sums_in_sem"], 16)
            for i in range(NT):
                last = pe.transpose(banks[7][:, NH * NE * i:NH * NE * i + NH * NE], sums_in[:, P * i:P * i + P],
                                    t["ident"][0:NH * NE, 0:NH * NE])
            last.then_inc(s["sums_full"], 1)
            for g in range(NG):
                for n in range(NH):
                    last = pe.matmul(banks[g][D * n:D * n + D, :], gate_wT[:, n, :],
                                     t["heads_out"][:, n, GW * g:GW * g + GW], start=True, stop=True)
                last.then_inc(s["logits_full"], 1)
            for g in range(NG):
                pe.wait_ge(s["logits_ready"], g + 1)
                if g == 3:
                    pe.wait_ge(s["inv_ready"], 1)
                for j in range(GT):
                    last = pe.transpose(banks[4 + g][:, P * j:P * j + P], logitsT[:, g, P * j:P * j + P], ident)
                last.then_inc(s["tok_full"], 1)
            for u in range(NT):
                pe.wait_ge(s["heads_used"], u - 3) if u >= 4 else pe.wait_ge(s["logits_ready"], u + 1)
                for n in range(NH):
                    last = pe.transpose(banks[u % 4][:, P * n:P * n + P], t["heads_out"][:, n, P * u:P * u + P], ident)
                last.then_inc(s["heads_full"], 1)
            for g in range(NG):
                pe.wait_ge(s["shift_ready"], g + 1)
                for j in range(GT):
                    i = GT * g + j
                    last = pe.transpose(banks[4 + g][:, P * j:P * j + P], t["sxT"][:, P * i:P * i + P], ident)
                last.then_inc(s["feat_full"], 1)
            for g in range(NG):
                pe.wait_ge(s["fx_ready"], g + 1)
                for j in range(GT):
                    last = pe.transpose(banks[g][:, P * j:P * j + P],
                                        fx[:, g, NH * j:NH * j + NH, :].rearrange("p n d -> p (n d)"), ident)
                last.then_inc(s["fxT_full"], 1)
            for g in range(NG):
                pe.wait_ge(s["fxT_ready"], g + 1)
                pe.matmul(banks[4 + g][:], fc_wT[:, 0, :], fxT[:, g, :], start=True, stop=True).then_inc(s["fc1_full"], 1)
            for g in range(NG):
                pe.wait_ge(s["masked_ready2"], g + 1)
                pe.matmul(banks[g][:], fc_wT[:, 1, :], hidden_m[:, g, :], start=True, stop=True).then_inc(s["fc2_full"], 1)
            for g in range(NG):
                pe.wait_ge(s["fc_out_ready"], g + 1)
                for j in range(GT):
                    last = pe.transpose(banks[4 + g][:, P * j:P * j + P], fc_out[:, g, P * j:P * j + P], ident)
                last.then_inc(s["back_full"], 1)
            for g in range(NG):
                pe.wait_ge(s["fout_ready"], g + 1)
                for j in range(GT):
                    last = pe.transpose(banks[g][:, P * j:P * j + P],
                                        fx[:, g, NH * j:NH * j + NH, :].rearrange("p n d -> p (n d)"), ident)
                last.then_inc(s["foutT_full"], 1)
            for g in range(NG):
                pe.wait_ge(s["foutT_ready"], g + 1)
                for j in range(GT):
                    last = pe.matmul(banks[4 + g][:, NH * j:NH * j + NH], hidden[:, g, P * j:P * j + P], fgate_wT[:],
                                     start=True, stop=True)
                last.then_inc(s["olog_full"], 1)

        @block.scalar
        def _(act):
            def stage(waits, done, do):
                for g in range(NG):
                    for w in waits:
                        act.wait_ge(s[w], g + 1)
                    do(g).then_inc(s[done], 1)

            stage(["logits_full"], "logits_ready",
                  lambda g: act.activation(logitsT[:, g, :], banks[g][:], ACT.Copy))
            stage(["shift_ready"], "gexp_ready",
                  lambda g: act.activation(gate["gate_exp"][:, g], gate["gate_shift"][:, g], ACT.Exp))
            stage(["centred1_ready"], "square1_ready",
                  lambda g: act.activation(square[:, g], centred[:, g], ACT.Square))
            stage(["vare1_ready"], "std1_ready",
                  lambda g: act.activation(small["std1"][:, g], small["vare1"][:, g], ACT.Sqrt))
            stage(["fxT_full"], "fxT_ready", lambda g: act.activation(fxT[:, g, :], banks[g][:], ACT.Copy))
            stage(["fc1_full"], "hidden_ready",
                  lambda g: act.activation(hidden[:, g, :], banks[4 + g][:], ACT.Relu, bias=t["fc_b"][:, 0:1]))
            stage(["centred2_ready", "var1_ready"], "square2_ready",
                  lambda g: act.activation(square[:, g], centred[:, g], ACT.Square))
            stage(["vare2_ready"], "std2_ready",
                  lambda g: act.activation(small["std2"][:, g], small["vare2"][:, g], ACT.Sqrt))
            stage(["foutT_full", "masked_ready2"], "foutT_ready",
                  lambda g: act.activation(hidden[:, g, :], banks[g][:], ACT.Copy))
            stage(["oshift_ready"], "oexp_ready",
                  lambda g: act.activation(ogate["out_exp"][:, g], ogate["out_shift"][:, g], ACT.Exp))

        @block.vector
        def _(dve):
            def stage(waits, done, do):
                for g in range(NG):
                    for w in waits:
                        dve.wait_ge(s[w], g + 1)
                    do(g).then_inc(s[done], 1)

            def norm(k, source, bank0):
                stage([source[1]], f"sum{k}_ready", lambda g: dve.reduce_sum(small[f"sum{k}"][:, g], source[0](g), AX))
                stage([f"sum{k}_ready"], f"centred{k}_ready", lambda g: dve.scalar_tensor_tensor(
                    out=centred[:, g], in0=spread(small[f"sum{k}"][:, g], D), scalar=-1.0 / D, in1=source[0](g),
                    op0=ALU.mult, op1=ALU.add))
                stage([f"square{k}_ready"], f"var{k}_ready",
                      lambda g: dve.reduce_sum(small[f"var{k}"][:, g], square[:, g], AX))
                stage([f"var{k}_ready"], f"vare{k}_ready", lambda g: dve.tensor_scalar(
                    small[f"vare{k}"][:, g], small[f"var{k}"][:, g], 1.0 / D, FFN_EPS, ALU.mult, ALU.add))
                stage([f"std{k}_ready"], f"rstd{k}_ready",
                      lambda g: dve.reciprocal(small[f"rstd{k}"][:, g], small[f"std{k}"][:, g]))
                stage([f"rstd{k}_ready"] + (["scaled1_ready"] if k == 2 else []), f"normed{k}_ready",
                      lambda g: dve.tensor_tensor(normed[:, g], centred[:, g], spread(small[f"rstd{k}"][:, g], D), ALU.mult))

            dve.memset(gate_wT[:], 0.0).then_inc(s["zeroed2"], 1)
            dve.memset(fc_wT[:], 0.0).then_inc(s["zeroed2"], 1)
            dve.wait_ge(s["zeroed2"], 2)
            dve.wait_ge(s["wT_full2"], 1)
            for e in range(NE):
                rows = slice(D * e, D * e + D)
                dve.tensor_copy(gate_wT[rows, :, e:NE * NE:NE],
                                banks[0][rows, 0:NH * NE].rearrange("p (n l) -> p n l", n=NH))
            for k in range(2):
                for n in range(NH):
                    rows = slice(D * n, D * n + D)
                    dve.tensor_copy(fc_wT[rows, k, rows], banks[0][rows, 128 * (k + 1):128 * (k + 1) + D])
            dve.tensor_copy(fgate_wT[:], banks[0][:, 384:384 + NH]).then_inc(s["wT_ready2"], 1)

            dve.wait_ge(s["sums_full"], 1)
            dve.reciprocal(inv_sums[:].rearrange("p g k e -> p (g k e)"),
                           banks[7][:, 0:NT * NH * NE]).then_inc(s["inv_ready"], 1)
            dve.wait_ge(s["inv_ready"], 1)

            def parts(g):
                return banks[4 + g][:].rearrange("p (k r) -> p k r", r=D)[:, :, 0:NE * NE]\
                    .rearrange("p k (l e) -> p k l e", e=NE)
            stage(["tok_full"], "parts_ready", lambda g: dve.tensor_tensor(
                logit_parts[:, g], parts(g), inv_sums[:, g].unsqueeze(2).to_broadcast([P, JN, NE, NE]), ALU.mult))
            stage(["parts_ready"], "logit0_ready",
                  lambda g: dve.reduce_sum(gate["gate_logit0"][:, g], logit_parts[:, g], AX))
            stage(["logit0_ready"], "logit_ready", lambda g: dve.tensor_tensor(
                gate["gate_logit"][:, g].rearrange("p (j n) e -> p j (n e)", n=NH),
                gate["gate_logit0"][:, g].rearrange("p (j n) e -> p j (n e)", n=NH),
                t["gate_b"][:].unsqueeze(1).to_broadcast([P, GT, NH * NE]), ALU.add))
            stage(["logit_ready"], "gmax_ready",
                  lambda g: dve.reduce_max(small["gate_max"][:, g], gate["gate_logit"][:, g], AX))
            stage(["gmax_ready"], "shift_ready", lambda g: dve.tensor_tensor(
                gate["gate_shift"][:, g], gate["gate_logit"][:, g], spread(small["gate_max"][:, g], NE), ALU.subtract))
            stage(["gexp_ready"], "gsum_ready",
                  lambda g: dve.reduce_sum(small["gate_sum"][:, g], gate["gate_exp"][:, g], AX))
            stage(["gsum_ready"], "ginv_ready",
                  lambda g: dve.reciprocal(small["gate_inv"][:, g], small["gate_sum"][:, g]))
            stage(["ginv_ready"], "share0_ready", lambda g: dve.tensor_tensor(
                gate["gate_share0"][:, g], gate["gate_exp"][:, g], spread(small["gate_inv"][:, g], NE), ALU.mult))
            stage(["share0_ready"], "share_ready", lambda g: dve.tensor_tensor(
                gate["gate_share"][:, g], gate["gate_share0"][:, g], inv_sums[:, g], ALU.mult))
            for u in range(NT):
                g, j = u // GT, u % GT
                dve.wait_ge(s["heads_full"], u + 1)
                dve.wait_ge(s["share_ready"], g + 1)
                if u >= 2:
                    dve.wait_ge(s["mixed_ready"], u - 1)
                share = gate["gate_share"][:, g, NH * j:NH * j + NH, :].rearrange("p n e -> p (n e)")
                dve.tensor_tensor(shared[:, u % 2], banks[u % 4][:].rearrange("p (k d) -> p k d", d=D),
                                  spread(share, D), ALU.mult).then_inc(s["heads_used"], 1)
                dve.wait_ge(s["heads_used"], u + 1)
                dve.reduce_sum(mixed[:, g, NH * j:NH * j + NH, :],
                               shared[:, u % 2].rearrange("p (n e) d -> p n d e", n=NH), AX).then_inc(s["mixed_ready"], 1)
            for g in range(NG):
                dve.wait_ge(s["feat_full"], g + 1)
                dve.wait_ge(s["mixed_ready"], GT * g + GT)
                dve.tensor_tensor(resid[:, g], pairs(banks[4 + g]), mixed[:, g], ALU.add).then_inc(s["resid_ready"], 1)
            norm(1, (lambda g: resid[:, g], "resid_ready"), None)
            stage(["fxT_ready"], "nonzero_ready",
                  lambda g: dve.tensor_scalar(nonzero[:, g, :], fxT[:, g, :], 0.0, None, ALU.not_equal))
            stage(["hidden_ready", "nonzero_ready"], "masked_ready2",
                  lambda g: dve.tensor_tensor(hidden_m[:, g, :], hidden[:, g, :], nonzero[:, g, :], ALU.mult))
            stage(["fc2_full"], "fc2_masked", lambda g: dve.scalar_tensor_tensor(
                out=logitsT[:, g, :], in0=banks[g][:], scalar=t["fc_b"][:, 1:2], in1=nonzero[:, g, :],
                op0=ALU.add, op1=ALU.mult))
            stage(["fc2_masked"], "fc_out_ready",
                  lambda g: dve.tensor_tensor(fc_out[:, g, :], logitsT[:, g, :], fxT[:, g, :], ALU.add))
            norm(2, (lambda g: pairs(banks[4 + g]), "back_full"), None)
            def ologits(g):
                return banks[4 + g][:, 0:GT * NH].rearrange("p (j n) -> p j n", n=NH)
            stage(["olog_full"], "omax_ready", lambda g: dve.reduce_max(tiny["out_max"][:, g], ologits(g), AX))
            stage(["omax_ready"], "oshift_ready", lambda g: dve.tensor_tensor(
                ogate["out_shift"][:, g], ologits(g), spread(tiny["out_max"][:, g], NH), ALU.subtract))
            stage(["oexp_ready"], "osum_ready", lambda g: dve.reduce_sum(tiny["out_sum"][:, g], ogate["out_exp"][:, g], AX))
            stage(["osum_ready"], "oinv_ready", lambda g: dve.reciprocal(tiny["out_inv"][:, g], tiny["out_sum"][:, g]))
            stage(["oinv_ready"], "oshare_ready", lambda g: dve.tensor_tensor(
                ogate["out_share"][:, g], ogate["out_exp"][:, g], spread(tiny["out_inv"][:, g], NH), ALU.mult))
            stage(["oshare_ready"], "gated_ready", lambda g: dve.tensor_tensor(
                resid[:, g], fx[:, g],
                spread(ogate["out_share"][:, g].rearrange("p j n -> p (j n)"), D), ALU.mult))

        @block.gpsimd
        def _(pool):
            def stage(waits, done, do):
                for g in range(NG):
                    for w in waits:
                        pool.wait_ge(s[w], g + 1)
                    do(g).then_inc(s[done], 1)

            for k, (scale, shift), last in ((1, ("ln_g", "ln_b"), "fx_ready"), (2, ("fnorm_g", "fnorm_b"), "fout_ready")):
                stage([f"normed{k}_ready"], f"scaled{k}_ready",
                      lambda g: pool.tensor_tensor(scaled[:, g], normed[:, g], each(t[scale][:]), ALU.mult))
                stage([f"scaled{k}_ready"] + (["fxT_full"] if k == 2 else []), last,
                      lambda g: pool.tensor_tensor(fx[:, g], scaled[:, g], each(t[shift][:]), ALU.add))
            stage(["gated_ready"], "result_ready", lambda g: pool.tensor_tensor(
                mixed[:, g], resid[:, g], t["x1"][:, GT * g:GT * g + GT, :].rearrange("p j (n d) -> p (j n) d", d=D),
                ALU.add))

        @block.sync
        def _(sp):
            sp.dma_start(sums_in[:], sum_scratch.rearrange("n e s -> (n e) s")).then_inc(s["sums_in_sem"], 16)
            rows = out.rearrange("(g j p) f -> g p j f", j=GT, p=P)
            for g in range(NG):
                sp.wait_ge(s["result_ready"], g + 1)
                sp.dma_start(rows[g], mixed[:, g].rearrange("p (j n) d -> p j (n d)", j=GT)).then_inc(s["result_out"], 16)
            sp.wait_ge(s["result_out"], 16 * NG)


_INS = ['x', 'adj', 'L0_gnn_weight', 'L0_gnn_bias', 'L0_ffn_hl_w', 'L0_ffn_hl_b', 'L0_ffn_wq', 'L0_ffn_wk', 'L0_ffn_wv', 'L0_ffn_gate_w', 'L0_ffn_gate_b', 'L0_ffn_ln_g', 'L0_ffn_ln_b', 'L0_ffn_fc1_w', 'L0_ffn_fc1_b', 'L0_ffn_fc2_w', 'L0_ffn_fc2_b', 'L0_ffn_fnorm_g', 'L0_ffn_fnorm_b', 'L0_ffn_fgate_w']


def kernel(**inputs):
    import numpy as _np
    import concourse.bacc as _bacc
    from concourse import mybir as _mybir
    from concourse.bass_utils import run_bass_kernel_spmd as _run

    nc = _bacc.Bacc("TRN2", target_bir_lowering=False, num_devices=1)
    arrays, args = {}, {}
    for name in _INS:
        a = _np.ascontiguousarray(inputs[name])
        arrays[f"in_{name}_dram"] = a
        args[name.replace("L0_", "")] = nc.dram_tensor(f"in_{name}_dram", a.shape, _mybir.dt.from_np(a.dtype), kind="ExternalInput").ap()
    out = nc.dram_tensor("out_0_dram", (2048, 128), _mybir.dt.float32, kind="ExternalOutput").ap()
    build(nc, args, out)
    r = _run(nc, [arrays], core_ids=[0])
    return r.results[0]["out_0_dram"]
```

```python
from contextlib import ExitStack

import concourse.bass as bass
from concourse import mybir

F32 = mybir.dt.float32
F32R = mybir.dt.float32r
BF16 = mybir.dt.bfloat16
ALU = mybir.AluOpType
ACT = mybir.ActivationFunctionType
AX = mybir.AxisListType.X

P = 128
S = 2048
H = 128
NH = 4
NE = 4
D = 32
NT = S // P
NG = 4
GT = NT // NG
GW = S // NG
GNN_EPS = 1e-5
FFN_EPS = 1e-8
NEG = -1e30
BIG = 3e38
NORMS = ("ln_g", "ln_b", "fnorm_g", "fnorm_b")
KR = 3 * D

SLOTS = [(g, t) for g in range(NG) for t in range(GT * (g + 1))]
NS = len(SLOTS)
STEP_END = [max(i for i, (g, _) in enumerate(SLOTS) if g == gg) for gg in range(NG)]
STEP_START = [min(i for i, (g, _) in enumerate(SLOTS) if g == gg) for gg in range(NG)]
CHUNKS = [(g, c, e, j) for g in range(NG) for c in range(g + 1) for e in range(NE) for j in range(GT)]
NC = len(CHUNKS)
CHUNK_END = [max(i for i, ch in enumerate(CHUNKS) if ch[0] == gg) for gg in range(NG)]
SCORE_RING, CHUNK_RING = 3, 3
NP_RING = 5
NPAIR = NS // 2
PART_RING = 5
PAIR_LAG = 3


def chunk_width(g, c, j):
    return (j + 1) * P if c == g else GW


def slot_shift(g, t):
    return max(0, t - GT * g) * P


def is_diagonal(i):
    g, k = SLOTS[i]
    return k >= GT * g


def slot_width(i):
    return GW - slot_shift(*SLOTS[i])


def shares_bank(i):
    return NE * slot_width(i) <= GW


def bank_of(n, ring):
    return n % NC % ring


def turns_since(n, ring):
    return min(d for d in range(1, 2 * ring) if bank_of(n - d, ring) == bank_of(n, ring))


def plan_head():
    LEAD_SLOTS = 3
    FIXED, MASK, CHUNK_FIXED, SCORES_WEIGHT = 190, 240, 120, 2
    pieces = []
    for i in range(NS + PAIR_LAG + 1):
        scores = []
        if i < NS:
            cost = SCORES_WEIGHT * (slot_width(i) + (MASK if is_diagonal(i) else 0))
            scores = [(("scores", i, e), i, cost) for e in range(NE)]
            if shares_bank(i):
                scores = [(("scores", i, 0), i, SCORES_WEIGHT * (GW + MASK))]
        pieces += scores[:NE - 1]
        if 1 <= i <= NS:
            pieces.append((("values", i - 1), i, 4 * slot_width(i - 1) + FIXED))
        pieces += scores[NE - 1:]
        done = i - PAIR_LAG - 1
        if done >= 0 and done % 2 == 0:
            pieces.append((("sums", done // 2), i, 4 * slot_width(done) + FIXED))
    chunk_cost = [chunk_width(g, c, j) + CHUNK_FIXED for g, c, _, j in CHUNKS]
    pace = sum(chunk_cost) / sum(cost for _, _, cost in pieces)
    for lead in range(CHUNK_END[0] + 1, NC):
        steps, chunk_slot, n, behind = [], {}, lead, 0.0
        for place, (piece, i, cost) in enumerate(pieces):
            steps.append(piece)
            behind += cost * pace
            while n < NC + lead and (behind > chunk_cost[n % NC] / 2 or place == len(pieces) - 1):
                steps.append(("chunk", n))
                chunk_slot[n] = i
                behind -= chunk_cost[n % NC]
                n += 1
        if all(chunk_slot.get(CHUNK_END[g], 0) <= STEP_START[g] - LEAD_SLOTS for g in range(1, NG)):
            return lead, steps, chunk_slot
    raise ValueError("no lead is enough")


LEAD, HEAD_STEPS, CHUNK_SLOT = plan_head()


def build(nc, a, out):
    k_scratch = nc.dram_tensor("k_scratch", (2, NH, D, S), F32, kind="Internal").ap()
    q_scratch = nc.dram_tensor("q_scratch", (2, NH, NE, D, S), F32, kind="Internal").ap()
    sx_scratch = nc.dram_tensor("sx_scratch", (NH, D, S), F32, kind="Internal").ap()
    sum_scratch = nc.dram_tensor("sum_scratch", (NH, NE, S), F32, kind="Internal").ap()
    with ExitStack() as ctx:
        def sb(name, shape, dt=F32):
            return ctx.enter_context(nc.sbuf_tensor(name, shape, dt))

        t = {
            "ident": sb("ident", [P, P]),
            "mask_add": sb("mask_add", [P, GW]),
            "ident_bf": sb("ident_bf", [P, P], BF16),
            "mask_kq": sb("mask_kq", [P, P], BF16),
            "x1": sb("x1", [P, NT, H]),
            "xn": sb("xn", [P, NT, H]),
        }
        t["xnT"] = sb("xnT", [P, S])
        t["hl_wT"] = sb("hl_wT", [P, P])
        t["hl_b"] = sb("hl_b", [P, 1])
        t["kv_wT"] = sb("kv_wT", [P, 2, P])
        t["q_wT"] = sb("q_wT", [P, P])
        t["gate_wT"] = sb("gate_wT", [P, NH, D])
        t["fc_wT"] = sb("fc_wT", [P, 2, P])
        t["fgate_wT"] = sb("fgate_wT", [P, NH])
        t["gate_w"] = sb("gate_w", [NH * NE, P])
        t["gate_b"] = sb("gate_b", [P, NH * NE])
        t["fc_w"] = sb("fc_w", [D, 2, P])
        t["fc_b"] = sb("fc_b", [P, 2])
        t["fgate_w"] = sb("fgate_w", [NH, P])
        for name in ("fnorm_g", "fnorm_b"):
            t[name] = sb(name, [P, D])
        for name in NORMS:
            t[name + "_col"] = sb(name + "_col", [P, 1])
        graph(nc, a, t)
        t["sxT"] = sb("sxT", [P, S])
        t["v_all"] = sb("v_all", [P, NH, NT, D])
        t["heads_out"] = sb("heads_out", [P, NH, S])
        t["sums_row"] = sb("sums_row", [P, 2, GW])
        t["sums_out"] = [ctx.enter_context(nc.semaphore(f"sums_out{i}")) for i in range(2)]
        with ExitStack() as operands:
            def operand(name, shape):
                return operands.enter_context(nc.sbuf_tensor(name, shape, F32R))

            def arrival(name):
                return [operands.enter_context(nc.semaphore(f"{name}{g}")) for g in range(NG)]

            t["keys_max"] = operand("keys_max", [KR, S])
            t["queries"] = [operand(f"queries{g}", [KR + 1, NE, GW]) for g in range(NG)]
            t["queries_in"], t["keys_max_in"] = arrival("queries_in"), arrival("keys_max_in")
            t["hi"], t["lo"] = operand("hi", [P, PART_RING, GW]), operand("lo", [P, PART_RING, GW])
            t["part_out"] = [operands.enter_context(nc.semaphore(f"part_out{i}")) for i in range(PART_RING)]
            project(nc, a, t, k_scratch, q_scratch, sx_scratch)
            attend(nc, t, k_scratch, q_scratch, sx_scratch, sum_scratch)
        finish(nc, a, t, sum_scratch, out)


def graph(nc, a, t):
    UNITS = [(g, c) for g in range(NG) for c in range(NT)]
    SHELLS = []
    for g in range(NG):
        SHELLS += [(g, c) for c in range(g, NG)] + [(r, g) for r in range(g + 1, NG)]
    STRIP_RING, COPY_RING = 4, 6
    LATE_WEIGHTS = 16 * (10 + 8 * NH)
    AHEAD = 2

    with ExitStack() as ctx:
        def sb(name, shape, dt=F32):
            return ctx.enter_context(nc.sbuf_tensor(name, shape, dt))

        def sem(name):
            return ctx.enter_context(nc.semaphore(name))

        adj = sb("adj", [P, NT, S])
        x = sb("x_in", [P, NT, H])
        xn = t["xn"]
        xnT = t["xnT"]
        hl_w = sb("hl_w_in", [P, H])
        kv_w = sb("kv_w", [D, 2, P])
        q_w = sb("q_w", [P, NH, D])
        y = sb("y", [P, NT, H])
        copies = sb("copies", [P, COPY_RING, GW])
        junk = sb("junk", [P, 2, GW])
        accT = sb("accT", [P, GW])
        w12 = sb("w12", [P, 2, H])
        w3 = sb("w3", [P, H])
        bias = sb("bias", [P, 1])
        stats = sb("stats", [P, NT, 6])
        mean_var = sb("mean_var", [P, NT, 2])
        var_eps = sb("var_eps", [P, NT])
        std = sb("std", [P, NT])
        rstd = sb("rstd", [P, NT])
        edge_parts = sb("edge_parts", [P, NT, NG])
        edge = sb("edge", [P, NT])
        strips = [ctx.enter_context(nc.psum_tensor(f"strip{i}", [P, GW], F32)) for i in range(STRIP_RING)]
        acc = [ctx.enter_context(nc.psum_tensor(f"acc{i}", [P, GW], F32)) for i in range(2)]
        misc = [ctx.enter_context(nc.psum_tensor(f"misc{i}", [P, GT, P], F32)) for i in range(2)]

        x_in, w_in = [sem(f"x_in{g}") for g in range(NG)], sem("w_in")
        first_in = [sem(f"first_in{c}") for c in range(NG)]
        right_in = [None] + [sem(f"right_in{g}") for g in range(1, NG)]
        below_in = [sem(f"below_in{c}") for c in range(NG - 1)]

        def block_in(g, c):
            if g == 0:
                return first_in[c], 16
            return (right_in[g], 16 * (NG - g)) if c >= g else (below_in[c], 16 * (NG - 1 - c))
        consts, const_steps = sem("consts"), sem("const_steps")
        dve_chain = sem("dve_chain")
        var_ready, std_ready, xn_ready = sem("var_ready"), sem("std_ready"), sem("xn_ready")
        xnT_full, xnT_ready = sem("xnT_full"), sem("xnT_ready")
        y_full, y_ready = sem("y_full"), sem("y_ready")
        strip_full, strip_copied = sem("strip_full"), sem("strip_copied")
        strip_used, product_done = sem("strip_used"), sem("product_done")
        acc_step, acc_copied = sem("acc_step"), sem("acc_copied")
        h_full, h_used = sem("h_full"), sem("h_used")
        late_w_in, wT_full = sem("late_w_in"), sem("wT_full")
        block = ctx.enter_context(nc.Block())

        adj_v = a["adj"].rearrange("(i p) j -> p i j", p=P)

        @block.sync
        def _(sp):
            for g in range(NG):
                sp.dma_start(x[:, GT * g:GT * g + GT, :],
                             a["x"].rearrange("(i p) d -> p i d", p=P)[:, GT * g:GT * g + GT, :]).then_inc(x_in[g], 16)
            sp.dma_start(w12[:], a["gnn_weight"][0:2 * H, :].rearrange("(k p) d -> p k d", p=P)).then_inc(w_in, 16)
            sp.dma_start(w3[:], a["gnn_weight"][2 * H, :].partition_broadcast(P)).then_inc(w_in, 16)
            sp.dma_start(bias[:], a["gnn_bias"].rearrange("(p o) -> p o", o=1)).then_inc(w_in, 16)
            for g, c in SHELLS:
                rows, cols = slice(GT * g, GT * g + GT), slice(GW * c, GW * c + GW)
                sp.dma_start(adj[:, rows, cols], adj_v[:, rows, cols]).then_inc(block_in(g, c)[0], 16)
            sp.dma_start(hl_w[:], a["ffn_hl_w"].rearrange("n d h -> (n d) h")).then_inc(late_w_in, 16)
            sp.dma_start(t["hl_b"][:], a["ffn_hl_b"].rearrange("n (d o) -> (n d) o", o=1)).then_inc(late_w_in, 16)
            sp.dma_start(kv_w[:, 0, :].rearrange("o (n d) -> o n d", n=NH),
                         a["ffn_wk"].rearrange("n o d -> o n d")).then_inc(late_w_in, 16)
            sp.dma_start(kv_w[:, 1, :].rearrange("o (n d) -> o n d", n=NH),
                         a["ffn_wv"].rearrange("n o d -> o n d")).then_inc(late_w_in, 16)
            sp.dma_start(q_w[:], a["ffn_wq"].rearrange("n e o d -> (e o) n d")).then_inc(late_w_in, 16)
            sp.dma_start(t["gate_w"][:], a["ffn_gate_w"].rearrange("n e f -> (n e) f")).then_inc(late_w_in, 16)
            sp.dma_start(t["fgate_w"][:], a["ffn_fgate_w"]).then_inc(late_w_in, 16)
            for name in ("fnorm_g", "fnorm_b"):
                sp.dma_start(t[name][:], a["ffn_" + name].partition_broadcast(P)).then_inc(late_w_in, 16)
            sp.dma_start(t["gate_b"][:], a["ffn_gate_b"].rearrange("n e -> (n e)").partition_broadcast(P))\
                .then_inc(late_w_in, 16)
            for n in range(NH):
                rows = slice(D * n, D * n + D)
                for name in NORMS:
                    sp.dma_start(t[name + "_col"][rows, :],
                                 a["ffn_" + name].rearrange("(d o) -> d o", o=1)).then_inc(late_w_in, 16)
                for k, layer in enumerate(("fc1", "fc2")):
                    sp.dma_start(t["fc_w"][:, k, rows], a[f"ffn_{layer}_w"]).then_inc(late_w_in, 16)
                    sp.dma_start(t["fc_b"][rows, k:k + 1],
                                 a[f"ffn_{layer}_b"].rearrange("(d o) -> d o", o=1)).then_inc(late_w_in, 16)

        @block.gpsimd
        def _(pool):
            pool.memset(t["ident"][:], 0.0).then_inc(const_steps, 1)
            for name in ("kv_wT", "gate_wT", "fc_wT"):
                pool.memset(t[name][:], 0.0).then_inc(consts, 1)
            pool.memset(t["mask_add"][:], 0.0).then_inc(const_steps, 1)
            pool.memset(t["ident_bf"][:], 0.0).then_inc(const_steps, 1)
            pool.memset(t["mask_kq"][:], 0.0).then_inc(const_steps, 1)
            pool.wait_ge(const_steps, 4)
            for m in (t["ident"], t["ident_bf"]):
                pool.affine_select(out=m[:], in_=m[:], compare_op=ALU.not_equal, fill=1.0, base=0,
                                   pattern=[[-1, P]], channel_multiplier=1).then_inc(consts, 1)
            pool.affine_select(out=t["mask_add"][:, GW - P:GW], in_=t["mask_add"][:, GW - P:GW], compare_op=ALU.is_ge,
                               fill=NEG, base=0, pattern=[[-1, P]], channel_multiplier=1).then_inc(consts, 1)
            pool.affine_select(out=t["mask_kq"][:], in_=t["mask_kq"][:], compare_op=ALU.is_ge, fill=NEG, base=0,
                               pattern=[[1, P]], channel_multiplier=-1).then_inc(consts, 1)

        @block.vector
        def _(dve):
            chain = [0]

            def link(ins):
                chain[0] += 1
                ins.then_inc(dve_chain, 1)
                dve.wait_ge(dve_chain, chain[0])

            def stats_of(src, tiles):
                for i in tiles:
                    last = dve.bn_stats(stats[:, i, :], src[:, i, :])
                link(last)
                for i in tiles:
                    last = dve.bn_aggr(mean_var[:, i, :], stats[:, i, :])
                link(last)
                some = slice(tiles[0], tiles[-1] + 1)
                dve.tensor_scalar(var_eps[:, some], mean_var[:, some, 1], GNN_EPS, None, ALU.add).then_inc(var_ready, 1)

            def normalise(src, dst, tiles, done):
                dve.wait_ge(std_ready, done)
                some = slice(tiles[0], tiles[-1] + 1)
                link(dve.reciprocal(rstd[:, some], std[:, some]))
                for i in tiles:
                    last = dve.tensor_scalar(dst[:, i, :], src[:, i, :], mean_var[:, i, 0:1], rstd[:, i:i + 1],
                                             ALU.subtract, ALU.mult)
                    if i % GT == GT - 1:
                        last.then_inc(xn_ready, 1)

            for g in range(NG + 1):
                if g < NG:
                    dve.wait_ge(x_in[g], 16)
                    stats_of(x, range(GT * g, GT * g + GT))
                if g:
                    normalise(x, xn, range(GT * g - GT, GT * g), g)
            for g in range(NG):
                dve.wait_ge(y_full, g + 1)
                dve.tensor_copy(y[:, GT * g:GT * g + GT, :], misc[g % 2][:]).then_inc(y_ready, 1)

            def product(u):
                g, c = UNITS[u]
                if c // GT > g and c % GT == 0:
                    dve.wait_ge(*block_in(c // GT, g))
                dve.wait_ge(strip_copied, u + 1)
                if u >= 2:
                    dve.wait_ge(product_done, u - 1)
                dve.tensor_tensor_reduce(
                    out=junk[:, u % 2, :], in0=copies[:, u % COPY_RING, :], in1=adj[:, c, GW * g:GW * g + GW],
                    scale=1.0, scalar=0.0, op0=ALU.mult, op1=ALU.add,
                    accum_out=edge_parts[:, c, g:g + 1]).then_inc(product_done, 1)

            def add_x(g):
                dve.wait_ge(h_full, g + 1)
                dve.tensor_tensor(t["x1"][:, GT * g:GT * g + GT, :], misc[g % 2][:],
                                  x[:, GT * g:GT * g + GT, :], ALU.add).then_inc(h_used, 1)

            def add_edge(g):
                tiles = range(GT * g, GT * g + GT)
                dve.wait_ge(product_done, NT * (NG - 1) + tiles[-1] + 1)
                dve.wait_ge(h_used, g + 1)
                link(dve.reduce_sum(edge[:, tiles[0]:tiles[-1] + 1], edge_parts[:, tiles[0]:tiles[-1] + 1, :], AX))
                for i in tiles:
                    last = dve.scalar_tensor_tensor(out=t["x1"][:, i, :], in0=w3[:], scalar=edge[:, i:i + 1],
                                                    in1=t["x1"][:, i, :], op0=ALU.mult, op1=ALU.add)
                link(last)
                stats_of(t["x1"], tiles)

            for u, (g, c) in enumerate(UNITS):
                product(u)
                if c == GT and g:
                    add_x(g - 1)
                if g == NG - 1 and c % GT == GT - 1 and c < NT - 1:
                    add_edge(c // GT)
                    if c // GT:
                        normalise(t["x1"], xn, range(c + 1 - 2 * GT, c + 1 - GT), NG + c // GT)
            normalise(t["x1"], xn, range(NT - 2 * GT, NT - GT), 2 * NG - 1)
            add_x(NG - 1)
            add_edge(NG - 1)
            normalise(t["x1"], xn, range(NT - GT, NT), 2 * NG)

        @block.scalar
        def _(act):
            for g in range(NG):
                rows = slice(GT * g, GT * g + GT)
                act.wait_ge(var_ready, g + 1)
                act.activation(std[:, rows], var_eps[:, rows], ACT.Sqrt).then_inc(std_ready, 1)
            for g in range(NG):
                act.wait_ge(xnT_full, g + 1)
                act.activation(xnT[:, GW * g:GW * g + GW], acc[g % 2][:], ACT.Copy).then_inc(xnT_ready, 1)
            act.wait_ge(w_in, 48)

            def copy_acc(g):
                act.wait_ge(acc_step, NT * (g + 1))
                if g:
                    act.wait_ge(h_full, g)
                act.activation(accT[:], acc[g % 2][:], ACT.Identity, bias=bias[:]).then_inc(acc_copied, 1)

            for u, (g, c) in enumerate(UNITS):
                act.wait_ge(strip_full, u + 1)
                if u >= COPY_RING:
                    act.wait_ge(acc_step, u - COPY_RING + 1)
                    act.wait_ge(product_done, u - COPY_RING + 1)
                act.activation(copies[:, u % COPY_RING, :], strips[u % STRIP_RING][:], ACT.Copy).then_inc(strip_copied, 1)
                if g and c == AHEAD - 1:
                    copy_acc(g - 1)
                if g == NG - 1 and c % GT == GT - 2 and c > GT:
                    rows = slice(c + 2 - 2 * GT, c + 2 - GT)
                    act.wait_ge(var_ready, NG + c // GT)
                    act.activation(std[:, rows], var_eps[:, rows], ACT.Sqrt).then_inc(std_ready, 1)
            copy_acc(NG - 1)
            act.wait_ge(wT_full, 1)
            act.wait_ge(consts, 7)
            pw = acc[(NG - 2) % 2]
            act.activation(t["hl_wT"][:], pw[:, 0:P], ACT.Copy)
            for k in range(2):
                for n in range(NH):
                    rows = slice(D * n, D * n + D)
                    act.activation(t["kv_wT"][rows, k, rows], pw[rows, P * (1 + k):P * (1 + k) + D], ACT.Copy)
            act.activation(t["q_wT"][:], pw[:, 3 * P:4 * P], ACT.Copy)
            act.wait_ge(wT_full, 2)
            pw = misc[(NG - 2) % 2]
            for e in range(NE):
                rows = slice(D * e, D * e + D)
                act.activation(t["gate_wT"][rows, :, e:NE * NE:NE],
                               pw[rows, 0, 0:NH * NE].rearrange("p (n l) -> p n l", n=NH), ACT.Copy)
            for k in range(2):
                for n in range(NH):
                    rows = slice(D * n, D * n + D)
                    act.activation(t["fc_wT"][rows, k, rows], pw[rows, k + 1, 0:D], ACT.Copy)
            act.activation(t["fgate_wT"][:], pw[:, 3, 0:NH], ACT.Copy)
            act.wait_ge(var_ready, 2 * NG)
            act.activation(std[:, NT - GT:NT], var_eps[:, NT - GT:NT], ACT.Sqrt).then_inc(std_ready, 1)
            for g in range(NG):
                act.wait_ge(xnT_full, NG + g + 1)
                act.activation(xnT[:, GW * g:GW * g + GW], strips[g][:], ACT.Copy).then_inc(xnT_ready, 1)

        @block.tensor
        def _(pe):
            pe.wait_ge(consts, 7)
            for g in range(NG):
                pe.wait_ge(xn_ready, g + 1)
                if g >= 2:
                    pe.wait_ge(xnT_ready, g - 1)
                for j in range(GT):
                    last = pe.transpose(acc[g % 2][:, P * j:P * j + P], xn[:, GT * g + j, :], t["ident"][:])
                last.then_inc(xnT_full, 1)
            pe.wait_ge(w_in, 48)
            for g in range(NG):
                pe.wait_ge(xnT_ready, g + 1)
                if g >= 2:
                    pe.wait_ge(y_ready, g - 1)
                for j in range(GT):
                    i = GT * g + j
                    last = pe.matmul(misc[g % 2][:, j, :], xnT[:, P * i:P * i + P], w12[:, 1, :],
                                     start=True, stop=True)
                last.then_inc(y_full, 1)
            pe.wait_ge(y_ready, NG)

            def transposes(u):
                g, c = UNITS[u]
                if c % GT == 0:
                    pe.wait_ge(*block_in(g, c // GT))
                if u >= STRIP_RING:
                    pe.wait_ge(strip_copied, u - STRIP_RING + 1)
                for j in range(GT):
                    last = pe.transpose(strips[u % STRIP_RING][:, P * j:P * j + P],
                                        adj[:, GT * g + j, P * c:P * c + P], t["ident"][:])
                last.then_inc(strip_full, 1)

            def transpose_acc(g):
                pe.wait_ge(acc_copied, g + 1)
                if g >= 2:
                    pe.wait_ge(h_used, g - 1)
                for j in range(GT):
                    last = pe.transpose(misc[g % 2][:, j, :], accT[:, P * j:P * j + P], t["ident"][:])
                last.then_inc(h_full, 1)

            def product(u):
                g, c = UNITS[u]
                if c == 0:
                    if g >= 2:
                        pe.wait_ge(acc_copied, g - 1)
                    pe.matmul(acc[g % 2][:], w12[:, 0, :], xnT[:, GW * g:GW * g + GW], start=True, stop=False)
                pe.wait_ge(strip_copied, u + 1)
                pe.matmul(acc[g % 2][:], y[:, c, :], copies[:, u % COPY_RING, :], start=False,
                          stop=(c == NT - 1)).then_inc(acc_step, 1)
                if g and c == AHEAD:
                    transpose_acc(g - 1)

            for u in range(len(UNITS) + AHEAD):
                if u < len(UNITS):
                    transposes(u)
                if u >= AHEAD:
                    product(u - AHEAD)
            transpose_acc(NG - 1)
            pe.wait_ge(late_w_in, LATE_WEIGHTS)
            pe.wait_ge(acc_copied, NG - 1)
            pw = acc[(NG - 2) % 2]
            pe.transpose(pw[:, 0:P], hl_w[:], t["ident"][:])
            pe.transpose(pw[:, P:P + D], kv_w[:, 0, :], t["ident"][0:D, 0:D])
            pe.transpose(pw[:, 2 * P:2 * P + D], kv_w[:, 1, :], t["ident"][0:D, 0:D])
            pe.transpose(pw[:, 3 * P:4 * P], q_w[:].rearrange("p n d -> p (n d)"), t["ident"][:]).then_inc(wT_full, 1)
            pe.wait_ge(h_used, NG - 1)
            pw = misc[(NG - 2) % 2]
            pe.transpose(pw[:, 0, 0:NH * NE], t["gate_w"][:], t["ident"][0:NH * NE, 0:NH * NE])
            pe.transpose(pw[:, 1, 0:D], t["fc_w"][:, 0, :], t["ident"][0:D, 0:D])
            pe.transpose(pw[:, 2, 0:D], t["fc_w"][:, 1, :], t["ident"][0:D, 0:D])
            pe.transpose(pw[:, 3, 0:NH], t["fgate_w"][:], t["ident"][0:NH, 0:NH]).then_inc(wT_full, 1)
            for g in range(NG):
                pe.wait_ge(xn_ready, NG + g + 1)
                if g == 0:
                    pe.wait_ge(strip_copied, NT * NG)
                for j in range(GT):
                    last = pe.transpose(strips[g][:, P * j:P * j + P], xn[:, GT * g + j, :], t["ident"][:])
                last.then_inc(xnT_full, 1)


def load_keys_max(sp, t, k_scratch, h, c):
    for r, part in enumerate((0, 1, 0)):
        sp.dma_start(t["keys_max"][D * r:D * r + D, GW * c:GW * c + GW].bitcast(F32),
                     k_scratch[part, h, :, GW * c:GW * c + GW]).then_inc(t["keys_max_in"][c], 16)


def load_queries(sp, t, q_scratch, h, g):
    for r, part in enumerate((0, 0, 1)):
        sp.dma_start(t["queries"][g][D * r:D * r + D, :, :].bitcast(F32),
                     q_scratch[part, h].rearrange("e o s -> o e s")[:, :, GW * g:GW * g + GW])\
            .then_inc(t["queries_in"][g], 16)


PARTS = [("k", 0, g) for g in range(NG)] + [("q", n, g) for n in range(NH) for g in range(NG)]


def project(nc, a, t, k_scratch, q_scratch, sx_scratch):
    with ExitStack() as ctx:
        def sb(name, shape, dt=F32):
            return ctx.enter_context(nc.sbuf_tensor(name, shape, dt))

        def sem(name):
            return ctx.enter_context(nc.semaphore(name))

        hl_wT, kv_wT, q_wT, xnT = t["hl_wT"], t["kv_wT"], t["q_wT"], t["xnT"]
        sxT = t["sxT"]
        hi, lo = t["hi"], t["lo"]
        pt = [ctx.enter_context(nc.psum_tensor(f"pt{i}", [P, GW], F32)) for i in range(2)]
        pq = [ctx.enter_context(nc.psum_tensor(f"pq{i}", [P, GW], F32)) for i in range(3)]

        sx_full, sx_ready = sem("sx_full"), sem("sx_ready")
        part_full, hi_ready, lo_ready = sem("part_full"), sem("hi_ready"), sem("lo_ready")
        part_out = t["part_out"]
        sx_out = sem("sx_out")
        v_full, v_ready = sem("v_full"), sem("v_ready")
        block = ctx.enter_context(nc.Block())


        @block.sync
        def _(sp):
            sp.wait_ge(sx_ready, NG)
            sp.dma_start(sx_scratch.rearrange("n d s -> (n d) s"), sxT[:]).then_inc(sx_out, 16)
            for i, (what, n, g) in enumerate(PARTS):
                cols = slice(GW * g, GW * g + GW)
                for part, ready, src in ((0, hi_ready, hi), (1, lo_ready, lo)):
                    if what == "k":
                        dst = k_scratch[part].rearrange("n o s -> (n o) s")[:, cols]
                    else:
                        dst = q_scratch[part, n].rearrange("e o s -> (e o) s")[:, cols]
                    sp.wait_ge(ready, i + 1)
                    sp.dma_start(dst, src[:, i % PART_RING, :].bitcast(F32)).then_inc(part_out[i % PART_RING], 16)
                if i == 2 * NG + 1:
                    for n in range(NG + 1):
                        sp.wait_ge(part_out[n % PART_RING], 32 * (n // PART_RING + 1))
                    load_queries(sp, t, q_scratch, 0, 0)
                    load_keys_max(sp, t, k_scratch, 0, 0)
            sp.wait_ge(sx_out, 16)

        @block.tensor
        def _(pe):
            for g in range(NG):
                if g >= 2:
                    pe.wait_ge(sx_ready, g - 1)
                pe.matmul(pt[g % 2][:], hl_wT[:], xnT[:, GW * g:GW * g + GW], start=True, stop=True).then_inc(sx_full, 1)
            for i, (what, n, g) in enumerate(PARTS):
                pe.wait_ge(sx_ready, g + 1 if i < NG else NG)
                if i >= 3:
                    pe.wait_ge(lo_ready, i - 2)
                cols = slice(GW * g, GW * g + GW)
                if what == "k":
                    last = pe.matmul(pq[i % 3][:], kv_wT[:, 0, :], sxT[:, cols], start=True, stop=True)
                else:
                    rows = slice(D * n, D * n + D)
                    last = pe.matmul(pq[i % 3][:], q_wT[rows, :], sxT[rows, cols], start=True, stop=True)
                last.then_inc(part_full, 1)
            for g in range(NG):
                if g >= 2:
                    pe.wait_ge(v_ready, g - 1)
                else:
                    pe.wait_ge(sx_ready, NG)
                for j in range(GT):
                    i = GT * g + j
                    last = pe.matmul(pt[g % 2][:, P * j:P * j + P], sxT[:, P * i:P * i + P], kv_wT[:, 1, :],
                                     start=True, stop=True)
                last.then_inc(v_full, 1)

        @block.scalar
        def _(act):
            for g in range(NG):
                act.wait_ge(sx_full, g + 1)
                act.activation(sxT[:, GW * g:GW * g + GW], pt[g % 2][:], ACT.Identity, bias=t["hl_b"][:]).then_inc(sx_ready, 1)
            for i in range(len(PARTS)):
                act.wait_ge(part_full, i + 1)
                if i >= PART_RING:
                    act.wait_ge(part_out[i % PART_RING], 32 * (i // PART_RING))
                act.activation(hi[:, i % PART_RING, :], pq[i % 3][:], ACT.Copy).then_inc(hi_ready, 1)

        @block.vector
        def _(dve):
            for i in range(len(PARTS)):
                dve.wait_ge(hi_ready, i + 1)
                if i >= PART_RING:
                    dve.wait_ge(part_out[i % PART_RING], 32 * (i // PART_RING))
                dve.tensor_tensor(lo[:, i % PART_RING, :], pq[i % 3][:], hi[:, i % PART_RING, :].bitcast(F32),
                                  ALU.subtract).then_inc(lo_ready, 1)
            for g in range(NG):
                dve.wait_ge(v_full, g + 1)
                dve.tensor_copy(t["v_all"][:, :, GT * g:GT * g + GT, :].rearrange("p n t o -> p t n o"),
                                pt[g % 2][:].rearrange("p (t n o) -> p t n o", t=GT, n=NH)).then_inc(v_ready, 1)


def attend(nc, t, k_scratch, q_scratch, sx_scratch, sum_scratch):
    with ExitStack() as ctx:
        def sb(name, shape, dt=F32):
            return ctx.enter_context(nc.sbuf_tensor(name, shape, dt))

        def sem(name):
            return ctx.enter_context(nc.semaphore(name))

        keys = sb("keys", [KR + 1, S], F32R)
        keys_max, queries = t["keys_max"], t["queries"]
        values = sb("values", [P, NT, D])
        ones = sb("ones", [P, D])
        features = sb("features", [P, GW])
        probs = sb("probs", [P, NP_RING, NE, GW])
        masked_chunk = sb("masked_chunk", [P, 2, GW])
        chunk_max = sb("chunk_max", [P, NE * GT, NG])
        row_max = sb("row_max", [P, NE * GT])
        neg_max = sb("neg_max", [P, D], F32R)
        neg_maxT = sb("neg_maxT", [P, D], F32R)
        pair_probs = [t["xn"][:].rearrange("p i d -> p (i d)").rearrange("p (e s) -> p e s", e=NE),
                      t["xnT"][:].rearrange("p (e s) -> p e s", e=NE)]
        sums_row, sums_out = t["sums_row"], t["sums_out"]
        scores = [ctx.enter_context(nc.psum_tensor(f"scores{i}", [P, GW], F32)) for i in range(SCORE_RING)]
        chunk = [ctx.enter_context(nc.psum_tensor(f"chunk{i}", [P, GW], F32)) for i in range(CHUNK_RING)]
        outT = ctx.enter_context(nc.psum_tensor("outT", [P, GW], F32))
        sums = ctx.enter_context(nc.psum_tensor("sums", [P, GW], F32))

        ones_ready, key_ones_ready = sem("ones_ready"), sem("key_ones_ready")
        keys_in = [sem(f"keys_in{c}") for c in range(NG)]
        values_in = [sem(f"values_in{c}") for c in range(NG)]
        queries_in, keys_max_in = t["queries_in"], t["keys_max_in"]
        features_in = sem("features_in")
        max_row_in = [sem(f"max_row_in{g}") for g in range(NG)]
        scores_full, scores_used = sem("scores_full"), sem("scores_used")
        probs_used = sem("probs_used")
        chunk_full, chunk_used, diagonal_seen = sem("chunk_full"), sem("chunk_used"), sem("diagonal_seen")
        row_max_ready, neg_ready, neg_maxT_ready = sem("row_max_ready"), sem("neg_ready"), sem("neg_maxT_ready")
        pair_ready, pair_summed = sem("pair_ready"), sem("pair_summed")
        out_used, sums_used = sem("out_used"), sem("sums_used")
        block = ctx.enter_context(nc.Block())

        SCALE = float(D) ** 0.5
        PAIR_CREDIT = 3

        def load_keys(sp, h, c):
            for r, part in enumerate((0, 1, 0)):
                sp.dma_start(keys[D * r:D * r + D, GW * c:GW * c + GW].bitcast(F32),
                             k_scratch[part, h, :, GW * c:GW * c + GW]).then_inc(keys_in[c], 16)

        def load_values(sp, h, c):
            sp.dma_start(values[:, GT * c:GT * c + GT, :],
                         t["v_all"][:, h, GT * c:GT * c + GT, :]).then_inc(values_in[c], 16)

        def load_features(sp, h, g):
            for e in range(NE):
                sp.dma_start(features[D * e:D * e + D, :], sx_scratch[h, :, GW * g:GW * g + GW]).then_inc(features_in, 16)

        def place_max_row(sp, step, g):
            sp.wait_ge(neg_maxT_ready, step + 1)
            for quadrant in range(4):
                q0 = D * quadrant
                sp.dma_start(queries[g][KR:KR + 1, :, :].rearrange("r e (j f) -> r (e j) f", f=P)[:, :, q0:q0 + D].bitcast(F32),
                             neg_maxT[q0:q0 + NE * GT, :].bitcast(F32)).then_inc(max_row_in[g], 16)

        def sp_head(sp, h, last):
            events = []
            for g in range(NG):
                step_end = STEP_END[g]

                def next_queries(g=g, i=step_end):
                    sp.wait_ge(scores_full, (h * NS + i + 1) * NE)
                    load_queries(sp, t, q_scratch, h + 1, g)
                if not last:
                    events.append((step_end + 0.5, next_queries))

                def feat(g=g):
                    sp.wait_ge(out_used, h * NG + g + 2)
                    if g + 1 < NG:
                        load_features(sp, h, g + 1)
                    else:
                        load_features(sp, h + 1, 0)
                if not (last and g == NG - 1):
                    events.append((step_end + 0.9, feat))

                def sums_to_dram(g=g):
                    sp.wait_ge(sums_used, h * NG + g + 2)
                    sp.dma_start(sum_scratch[h, :, GW * g:GW * g + GW],
                                 sums_row[0:D * (NE - 1) + 1:D, g % 2, :]).then_inc(sums_out[g % 2], 16)
                events.append((step_end + PAIR_LAG + 1.0, sums_to_dram))
                if not last:
                    slot = STEP_START[NG - 1] + GT * g + GT - 1

                    def next_keys(c=g, i=slot):
                        sp.wait_ge(scores_full, (h * NS + i + 1) * NE)
                        load_keys(sp, h + 1, c)

                    def next_values(c=g, i=slot):
                        sp.wait_ge(probs_used, h * NS + NP_RING + i + 1)
                        load_values(sp, h + 1, c)
                    events.append((slot + 0.4, next_keys))
                    events.append((slot + 1.6, next_values))
                for dh in (0, 1):
                    at = dh * NC + CHUNK_END[g]
                    if at >= LEAD and at < LEAD + NC and not (last and dh):
                        def row(dh=dh, g=g):
                            place_max_row(sp, (h + dh) * NG + g, g)
                        events.append((CHUNK_SLOT[at] + 0.7, row))
                if not last:
                    reader = max(n for n, ch in enumerate(CHUNKS) if ch[1] == g)

                    def next_keys_max(c=g, n=reader):
                        sp.wait_ge(chunk_full, h * NC + n + 1)
                        load_keys_max(sp, t, k_scratch, h + 1, c)
                    events.append((CHUNK_SLOT[reader] + 0.3, next_keys_max))
            for _, do in sorted(events, key=lambda x: x[0]):
                do()

        @block.sync
        def _(sp):
            for i in range(2):
                sp.sem_inc(sums_out[i], 16)
            for n in range(2 * NG):
                sp.wait_ge(t["part_out"][n % PART_RING], 32 * (n // PART_RING + 1))
            for g in range(1, NG):
                load_queries(sp, t, q_scratch, 0, g)
                load_keys_max(sp, t, k_scratch, 0, g)
            for c in range(NG):
                load_keys(sp, 0, c)
                load_values(sp, 0, c)
            for i in range(PART_RING):
                sp.wait_ge(t["part_out"][i], 32 * len(range(i, len(PARTS), PART_RING)))
            load_features(sp, 0, 0)
            for g in range(NG):
                if CHUNK_END[g] < LEAD:
                    place_max_row(sp, g, g)
            with sp.Fori(0, NH - 1) as h:
                sp_head(sp, h, False)
            sp_head(sp, NH - 1, True)

        def pe_chunk(pe, h, i):
            g, c, e, j = CHUNKS[i % NC]
            head = h + i // NC
            if (e, j, c) == (0, 0, 0):
                pe.wait_ge(queries_in[g], head * 48 + 48)
            if (e, j, c) == (0, 0, g):
                pe.wait_ge(keys_max_in[c], head * 48 + 48)
            pe.wait_ge(chunk_used, h * NC + i + 1 + CHUNK_RING - turns_since(i, CHUNK_RING))
            n = chunk_width(g, c, j)
            pe.matmul(chunk[bank_of(i, CHUNK_RING)][:, 0:n], queries[g][0:KR, e, P * j:P * j + P], keys_max[:, GW * c:GW * c + n],
                      start=True, stop=True).then_inc(chunk_full, 1)

        def pe_scores(pe, h, i, e):
            g, k = SLOTS[i]
            shift = slot_shift(g, k)
            if i == STEP_START[g] and e == 0:
                pe.wait_ge(max_row_in[g], h * 64 + 64)
                pe.wait_ge(keys_in[g], h * 48 + 48)
            n = NE * i + e
            pe.wait_ge(scores_used, (h * NS + i) * NE + e + 1 + SCORE_RING - turns_since(n, SCORE_RING))
            if shares_bank(i):
                bank = scores[bank_of(n, SCORE_RING)][:].rearrange("p (e s) -> p e s", e=NE)
                pe.matmul(bank, t["ident_bf"][:], t["mask_kq"][:].unsqueeze(1).to_broadcast([P, NE, P]), start=True,
                          stop=False, skip_group_check=True)
                pe.matmul(bank, keys[:, P * k:P * k + P], queries[g][:, :, shift:GW], start=False, stop=True,
                          skip_group_check=True).then_inc(scores_full, NE)
                return
            diagonal = k >= GT * g
            if diagonal:
                pe.matmul(scores[bank_of(n, SCORE_RING)][:, 0:P], t["ident_bf"][:], t["mask_kq"][:], start=True, stop=False,
                          skip_group_check=True)
            pe.matmul(scores[bank_of(n, SCORE_RING)][:, 0:GW - shift], keys[:, P * k:P * k + P], queries[g][:, e, shift:GW],
                      start=not diagonal, stop=True, skip_group_check=diagonal).then_inc(scores_full, 1)

        def pe_values(pe, h, i):
            g, k = SLOTS[i]
            shift = slot_shift(g, k)
            pe.wait_ge(scores_used, (h * NS + i + 1) * NE + SCORE_RING)
            if i == STEP_START[g]:
                pe.wait_ge(values_in[g], h * 16 + 16)
                pe.wait_ge(out_used, h * NG + g + 1)
            for e in range(NE):
                last = pe.matmul(outT[D * e:D * e + D, shift:GW], values[:, k, :],
                                 probs[:, i % NP_RING, e, 0:GW - shift], start=(k == 0), stop=(i == STEP_END[g]))
            last.then_inc(probs_used, 1)

        def pe_sums(pe, h, pair):
            i = 2 * pair
            g, k = SLOTS[i]
            shift, shift2 = slot_shift(g, k), slot_shift(g, k + 1)
            pe.wait_ge(pair_ready, h * NPAIR + pair + 1)
            if i == STEP_START[g]:
                pe.wait_ge(sums_used, h * NG + g + 1)
            if shift2 > shift:
                for e in range(NE):
                    pe.matmul(sums[D * e:D * e + D, shift:shift2], ones[:],
                              probs[:, i % NP_RING, e, 0:shift2 - shift], start=(k == 0), stop=False)
            for e in range(NE):
                last = pe.matmul(sums[D * e:D * e + D, shift2:GW], ones[:], pair_probs[pair % 2][:, e, 0:GW - shift2],
                                 start=(k == 0 and shift2 == shift), stop=(i + 1 == STEP_END[g]))
            last.then_inc(pair_summed, 1)

        def pe_head(pe, h, last):
            for what, n, *expert in HEAD_STEPS:
                if what == "scores":
                    pe_scores(pe, h, n, expert[0])
                elif what == "values":
                    pe_values(pe, h, n)
                elif what == "sums":
                    pe_sums(pe, h, n)
                elif not (last and n >= NC):
                    pe_chunk(pe, h, n)

        @block.tensor
        def _(pe):
            for i in range(LEAD):
                pe_chunk(pe, 0, i)
            pe.wait_ge(ones_ready, 2)
            pe.wait_ge(key_ones_ready, 1)
            with pe.Fori(0, NH - 1) as h:
                pe_head(pe, h, False)
            pe_head(pe, NH - 1, True)

        def act_sums(act, h, g):
            act.wait_ge(pair_summed, h * NPAIR + PAIR_CREDIT + STEP_END[g] // 2 + 1)
            act.wait_ge(sums_out[g % 2], h * (8 * NG) + g // 2 * 16 + 16)
            act.activation(sums_row[:, g % 2, :], sums[:], ACT.Copy).then_inc(sums_used, 1)

        def act_head(act, h):
            for i in range(NS + 1):
                if i < NS:
                    g, k = SLOTS[i]
                    n = GW - slot_shift(g, k)
                    act.wait_ge(probs_used, h * NS + i + 1)
                    act.wait_ge(pair_summed, h * NPAIR + PAIR_CREDIT + (i - NP_RING) // 2 + 1)
                    if shares_bank(i):
                        act.wait_ge(scores_full, (h * NS + i + 1) * NE)
                        act.activation(probs[:, i % NP_RING, :, 0:n],
                                       scores[bank_of(NE * i, SCORE_RING)][:].rearrange("p (e s) -> p e s", e=NE),
                                       ACT.Exp, scale=SCALE).then_inc(scores_used, NE)
                    else:
                        for e in range(NE):
                            act.wait_ge(scores_full, (h * NS + i) * NE + e + 1)
                            act.activation(probs[:, i % NP_RING, e, 0:n], scores[bank_of(NE * i + e, SCORE_RING)][:, 0:n],
                                           ACT.Exp, scale=SCALE).then_inc(scores_used, 1)
                for g in range(NG):
                    if i == min(STEP_END[g] + PAIR_LAG + 1, NS):
                        act_sums(act, h, g)

        @block.scalar
        def _(act):
            act.sem_inc(scores_used, SCORE_RING)
            act.sem_inc(sums_used, 1)
            with act.Fori(0, NH - 1) as h:
                act_head(act, h)
            act_head(act, NH - 1)

        def dve_chunk(dve, h, i):
            g, c, e, j = CHUNKS[i % NC]
            n = chunk_width(g, c, j)
            step = (h + i // NC) * NG + g
            first = CHUNK_END[g - 1] + 1 if g else 0
            if i % NC == first and not (isinstance(step, int) and step == 0):
                dve.wait_ge(row_max_ready, step)
            dve.wait_ge(chunk_full, h * NC + i + 1)
            if c < g:
                dve.reduce_max(chunk_max[:, GT * e + j, c:c + 1], chunk[bank_of(i, CHUNK_RING)][:, 0:n], AX).then_inc(chunk_used, 1)
            else:
                dve.wait_ge(chunk_used, h * NC + i - 1 + CHUNK_RING)
                dve.sem_inc(diagonal_seen, 1)
                dve.tensor_tensor_reduce(
                    out=masked_chunk[:, i % 2, 0:n], in0=chunk[bank_of(i, CHUNK_RING)][:, 0:n], in1=t["mask_add"][:, GW - n:GW], scale=1.0,
                    scalar=-BIG, op0=ALU.add, op1=ALU.max, accum_out=chunk_max[:, GT * e + j, c:c + 1]).then_inc(chunk_used, 1)
            if i % NC == CHUNK_END[g]:
                dve.wait_ge(chunk_used, h * NC + i + 1 + CHUNK_RING)
                if not (isinstance(step, int) and step == 0):
                    dve.wait_ge(neg_ready, step)
                dve.reduce_max(row_max[:], chunk_max[:, :, 0:g + 1], AX).then_inc(row_max_ready, 1)
                dve.wait_ge(row_max_ready, step + 1)
                if not (isinstance(step, int) and step == 0):
                    dve.wait_ge(neg_maxT_ready, step)
                dve.tensor_scalar(neg_max[:, 0:NE * GT], row_max[:], -1.0, None, ALU.mult).then_inc(neg_ready, 1)
                dve.wait_ge(neg_ready, step + 1)
                g0, h0 = ((g - 1) % NG, h + i // NC - (1 if g == 0 else 0))
                if not (isinstance(step, int) and step == 0):
                    dve.wait_ge(max_row_in[g0], h0 * 64 + 64)
                dve.transpose(neg_maxT[:].bitcast(F32), neg_max[:].bitcast(F32)).then_inc(neg_maxT_ready, 1)

        def dve_step_end(dve, h, g):
            dve.wait_ge(probs_used, h * NS + NP_RING + STEP_END[g] + 1)
            dve.wait_ge(features_in, h * (64 * NG) + 64 * (g + 1))
            cols = slice(GW * g, GW * g + GW)
            place = (t["heads_out"][:, h, cols] if isinstance(h, int) else
                     t["heads_out"][:, bass.ds(h, 1), cols].rearrange("p a s -> p (a s)"))
            dve.scalar_tensor_tensor(out=place, in0=features[:], scalar=0.0, in1=outT[:],
                                     op0=ALU.not_equal, op1=ALU.mult).then_inc(out_used, 1)

        def dve_head(dve, h, last):
            for what, n, *_ in HEAD_STEPS:
                if what == "chunk" and not (last and n >= NC):
                    dve_chunk(dve, h, n)
                elif what == "values" and n in STEP_END:
                    dve_step_end(dve, h, STEP_END.index(n))

        @block.vector
        def _(dve):
            dve.sem_inc(chunk_used, CHUNK_RING)
            dve.sem_inc(out_used, 1)
            dve.memset(neg_max[:].bitcast(F32), 0.0).then_inc(ones_ready, 1)
            dve.memset(ones[:], 1.0).then_inc(ones_ready, 1)
            dve.wait_ge(ones_ready, 2)
            for i in range(LEAD):
                dve_chunk(dve, 0, i)
            with dve.Fori(0, NH - 1) as h:
                dve_head(dve, h, False)
            dve_head(dve, NH - 1, True)

        def pool_head(pool, h):
            for pair in range(NPAIR):
                i = 2 * pair
                g, k = SLOTS[i]
                apart = slot_shift(g, k + 1) - slot_shift(g, k)
                n = GW - slot_shift(g, k + 1)
                pool.wait_ge(scores_used, (h * NS + i + 2) * NE + SCORE_RING)
                pool.wait_ge(pair_summed, h * NPAIR + PAIR_CREDIT + pair - 1)
                pool.tensor_tensor(pair_probs[pair % 2][:, :, 0:n], probs[:, i % NP_RING, :, apart:apart + n],
                                   probs[:, (i + 1) % NP_RING, :, 0:n], ALU.add).then_inc(pair_ready, 1)

        @block.gpsimd
        def _(pool):
            pool.sem_inc(probs_used, NP_RING)
            pool.sem_inc(pair_summed, PAIR_CREDIT)
            pool.memset(keys[KR:KR + 1, :].bitcast(F32), 1.0).then_inc(key_ones_ready, 1)
            with pool.Fori(0, NH - 1) as h:
                pool_head(pool, h)
            pool_head(pool, NH - 1)


def finish(nc, a, t, sum_scratch, out):
    JN = GT * NH

    with ExitStack() as ctx:
        def sb(name, shape, dt=F32):
            return ctx.enter_context(nc.sbuf_tensor(name, shape, dt))

        def sem(name):
            return ctx.enter_context(nc.semaphore(name))

        gate_wT, fc_wT, fgate_wT = t["gate_wT"], t["fc_wT"], t["fgate_wT"]
        sums_in = sb("sums_in", [NH * NE, S])
        inv_sums = sb("inv_sums", [P, NG, JN, NE])
        logit_parts = sb("logit_parts", [P, NG, JN, NE, NE])
        logitsT = sb("logitsT", [P, NG, GW])
        small = {n: sb(n, [P, NG, JN]) for n in ("gate_max", "gate_sum", "gate_inv", "sum1", "var1", "vare1",
                                                 "std1", "rstd1", "sum2", "var2", "vare2", "std2", "rstd2")}
        tiny = {n: sb(n, [P, NG, GT]) for n in ("out_max", "out_sum", "out_inv")}
        gate = {n: sb(n, [P, NG, JN, NE]) for n in ("gate_logit0", "gate_logit", "gate_share0", "gate_shift", "gate_exp", "gate_share")}
        ogate = {n: sb(n, [P, NG, GT, NH]) for n in ("out_shift", "out_exp", "out_share")}
        shared = sb("shared", [P, GT, NH * NE, D])
        half_sums = sb("half_sums", [P, GT, NH, 2, D])
        mixed = sb("mixed", [P, NG, JN, D])
        resid = sb("resid", [P, NG, JN, D])
        centred = sb("centred", [P, NG, JN, D])
        square = sb("square", [P, NG, JN, D])
        normed = sb("normed", [P, NG, JN, D])
        scaled = t["xn"][:].rearrange("p (g j) h -> p g (j h)", g=NG).rearrange("p g (k d) -> p g k d", d=D)
        fx = sb("fx", [P, NG, JN, D])
        fxT = t["xnT"][:].rearrange("p (g s) -> p g s", g=NG)
        nonzero = sb("nonzero", [P, NG, GW])
        hidden = sb("hidden", [P, NG, GW])
        hidden_m = sb("hidden_m", [P, NG, GW])
        fc_out = hidden_m
        banks = [ctx.enter_context(nc.psum_tensor(f"bank{i}", [P, GW], F32)) for i in range(8)]

        names = ("logits_full logits_ready tok_full shift_ready gexp_ready gsum_ready "
                 "ginv_ready share_ready heads_full heads_used mixed_ready feat_full resid_ready sum1_ready "
                 "centred1_ready square1_ready var1_ready vare1_ready std1_ready rstd1_ready normed1_ready "
                 "fxT_full fxT_ready nonzero_ready fc1_full hidden_ready masked_ready2 "
                 "fc2_full fc2_masked fc_out_ready back_full sum2_ready centred2_ready square2_ready var2_ready "
                 "vare2_ready std2_ready rstd2_ready normed2_ready scaled2_ready fout_ready foutT_full foutT_ready "
                 "olog_full omax_ready oshift_ready oexp_ready osum_ready oinv_ready oshare_ready gated_ready "
                 "result_ready result_out gmax_ready sums_in_sem sums_full inv_ready parts_ready logit0_ready logit_ready "
                 "share0_ready halves_ready pool_mixed late_result_ready").split()
        s = {n: sem(n) for n in names}
        block = ctx.enter_context(nc.Block())

        def spread(ap, n):
            return ap.unsqueeze(2).to_broadcast([P, ap.shape[1], n])

        def each(vec):
            return vec.unsqueeze(1).to_broadcast([P, JN, D])

        def pairs(bank):
            return bank[:].rearrange("p (k d) -> p k d", d=D)

        def add_x1(engine, g):
            return engine.tensor_tensor(
                mixed[:, g], resid[:, g], t["x1"][:, GT * g:GT * g + GT, :].rearrange("p j (n d) -> p (j n) d", d=D), ALU.add)

        @block.tensor
        def _(pe):
            ident = t["ident"][:]
            for g in range(NG):
                for n in range(NH):
                    last = pe.matmul(banks[g][D * n:D * n + D, :], gate_wT[:, n, :],
                                     t["heads_out"][:, n, GW * g:GW * g + GW], start=True, stop=True)
                last.then_inc(s["logits_full"], 1)
            pe.wait_ge(s["sums_in_sem"], 16)
            for i in range(NT):
                last = pe.transpose(banks[7][:, NH * NE * i:NH * NE * i + NH * NE], sums_in[:, P * i:P * i + P],
                                    t["ident"][0:NH * NE, 0:NH * NE])
            last.then_inc(s["sums_full"], 1)
            for g in range(NG):
                pe.wait_ge(s["logits_ready"], g + 1)
                if g == 3:
                    pe.wait_ge(s["inv_ready"], 1)
                for j in range(GT):
                    last = pe.transpose(banks[4 + g][:, P * j:P * j + P], logitsT[:, g, P * j:P * j + P], ident)
                last.then_inc(s["tok_full"], 1)
            for u in range(NT):
                pe.wait_ge(s["heads_used"], u - 3) if u >= 4 else pe.wait_ge(s["logits_ready"], u + 1)
                for n in range(NH):
                    last = pe.transpose(banks[u % 4][:, P * n:P * n + P], t["heads_out"][:, n, P * u:P * u + P], ident)
                last.then_inc(s["heads_full"], 1)
            for g in range(NG):
                pe.wait_ge(s["shift_ready"], g + 1)
                for j in range(GT):
                    i = GT * g + j
                    last = pe.transpose(banks[4 + g][:, P * j:P * j + P], t["sxT"][:, P * i:P * i + P], ident)
                last.then_inc(s["feat_full"], 1)
            for g in range(NG):
                pe.wait_ge(s["normed1_ready"], g + 1)
                for j in range(GT):
                    last = pe.transpose(banks[g][:, P * j:P * j + P],
                                        normed[:, g, NH * j:NH * j + NH, :].rearrange("p n d -> p (n d)"), ident)
                last.then_inc(s["fxT_full"], 1)
            for g in range(NG):
                pe.wait_ge(s["fxT_ready"], g + 1)
                pe.matmul(banks[4 + g][:], fc_wT[:, 0, :], fxT[:, g, :], start=True, stop=True).then_inc(s["fc1_full"], 1)
            for g in range(NG):
                pe.wait_ge(s["masked_ready2"], g + 1)
                pe.matmul(banks[g][:], fc_wT[:, 1, :], hidden_m[:, g, :], start=True, stop=True).then_inc(s["fc2_full"], 1)
            for g in range(NG):
                pe.wait_ge(s["fc_out_ready"], g + 1)
                for j in range(GT):
                    last = pe.transpose(banks[4 + g][:, P * j:P * j + P], fc_out[:, g, P * j:P * j + P], ident)
                last.then_inc(s["back_full"], 1)
            for g in range(NG):
                pe.wait_ge(s["normed2_ready"], g + 1)
                for j in range(GT):
                    last = pe.transpose(banks[g][:, P * j:P * j + P],
                                        normed[:, g, NH * j:NH * j + NH, :].rearrange("p n d -> p (n d)"), ident)
                last.then_inc(s["foutT_full"], 1)
            for g in range(NG):
                pe.wait_ge(s["foutT_ready"], g + 1)
                for j in range(GT):
                    last = pe.matmul(banks[4 + g][:, NH * j:NH * j + NH], hidden[:, g, P * j:P * j + P], fgate_wT[:],
                                     start=True, stop=True)
                last.then_inc(s["olog_full"], 1)

        @block.scalar
        def _(act):
            def stage(waits, done, do):
                for g in range(NG):
                    for w in waits:
                        act.wait_ge(s[w], g + 1)
                    do(g).then_inc(s[done], 1)

            stage(["logits_full"], "logits_ready",
                  lambda g: act.activation(logitsT[:, g, :], banks[g][:], ACT.Copy))
            stage(["shift_ready"], "gexp_ready",
                  lambda g: act.activation(gate["gate_exp"][:, g], gate["gate_shift"][:, g], ACT.Exp))
            stage(["centred1_ready"], "square1_ready",
                  lambda g: act.activation(square[:, g], centred[:, g], ACT.Square))
            stage(["vare1_ready"], "std1_ready",
                  lambda g: act.activation(small["std1"][:, g], small["vare1"][:, g], ACT.Sqrt))
            stage(["fxT_full"], "fxT_ready", lambda g: act.activation(
                fxT[:, g, :], banks[g][:], ACT.Identity, bias=t["ln_b_col"][:], scale=t["ln_g_col"][:]))
            stage(["fc1_full"], "hidden_ready",
                  lambda g: act.activation(hidden[:, g, :], banks[4 + g][:], ACT.Relu, bias=t["fc_b"][:, 0:1]))
            stage(["centred2_ready", "var1_ready"], "square2_ready",
                  lambda g: act.activation(square[:, g], centred[:, g], ACT.Square))
            stage(["vare2_ready"], "std2_ready",
                  lambda g: act.activation(small["std2"][:, g], small["vare2"][:, g], ACT.Sqrt))
            stage(["foutT_full", "masked_ready2"], "foutT_ready",
                  lambda g: act.activation(hidden[:, g, :], banks[g][:], ACT.Identity, bias=t["fnorm_b_col"][:],
                                           scale=t["fnorm_g_col"][:]))
            stage(["oshift_ready"], "oexp_ready",
                  lambda g: act.activation(ogate["out_exp"][:, g], ogate["out_shift"][:, g], ACT.Exp))

        @block.vector
        def _(dve):
            def stage(waits, done, do):
                for g in range(NG):
                    for w in waits:
                        dve.wait_ge(s[w], g + 1)
                    do(g).then_inc(s[done], 1)

            def norm(k, source, source_ready, normed_free):
                stage([source_ready], f"sum{k}_ready", lambda g: dve.reduce_sum(small[f"sum{k}"][:, g], source(g), AX))
                stage([f"sum{k}_ready"], f"centred{k}_ready", lambda g: dve.scalar_tensor_tensor(
                    out=centred[:, g], in0=spread(small[f"sum{k}"][:, g], D), scalar=-1.0 / D, in1=source(g),
                    op0=ALU.mult, op1=ALU.add))
                stage([f"square{k}_ready"], f"var{k}_ready",
                      lambda g: dve.reduce_sum(small[f"var{k}"][:, g], square[:, g], AX))
                stage([f"var{k}_ready"], f"vare{k}_ready", lambda g: dve.tensor_scalar(
                    small[f"vare{k}"][:, g], small[f"var{k}"][:, g], 1.0 / D, FFN_EPS, ALU.mult, ALU.add))
                stage([f"std{k}_ready"], f"rstd{k}_ready",
                      lambda g: dve.reciprocal(small[f"rstd{k}"][:, g], small[f"std{k}"][:, g]))
                stage([f"rstd{k}_ready"] + normed_free, f"normed{k}_ready",
                      lambda g: dve.tensor_tensor(normed[:, g], centred[:, g], spread(small[f"rstd{k}"][:, g], D), ALU.mult))

            dve.wait_ge(s["sums_full"], 1)
            dve.reciprocal(inv_sums[:].rearrange("p g k e -> p (g k e)"),
                           banks[7][:, 0:NT * NH * NE]).then_inc(s["inv_ready"], 1)
            dve.wait_ge(s["inv_ready"], 1)

            def parts(g):
                return banks[4 + g][:].rearrange("p (k r) -> p k r", r=D)[:, :, 0:NE * NE]\
                    .rearrange("p k (l e) -> p k l e", e=NE)
            stage(["tok_full"], "parts_ready", lambda g: dve.tensor_tensor(
                logit_parts[:, g], parts(g), inv_sums[:, g].unsqueeze(2).to_broadcast([P, JN, NE, NE]), ALU.mult))
            stage(["parts_ready"], "logit0_ready",
                  lambda g: dve.reduce_sum(gate["gate_logit0"][:, g], logit_parts[:, g], AX))
            stage(["logit0_ready"], "logit_ready", lambda g: dve.tensor_tensor(
                gate["gate_logit"][:, g].rearrange("p (j n) e -> p j (n e)", n=NH),
                gate["gate_logit0"][:, g].rearrange("p (j n) e -> p j (n e)", n=NH),
                t["gate_b"][:].unsqueeze(1).to_broadcast([P, GT, NH * NE]), ALU.add))
            stage(["logit_ready"], "gmax_ready",
                  lambda g: dve.reduce_max(small["gate_max"][:, g], gate["gate_logit"][:, g], AX))
            stage(["gmax_ready"], "shift_ready", lambda g: dve.tensor_tensor(
                gate["gate_shift"][:, g], gate["gate_logit"][:, g], spread(small["gate_max"][:, g], NE), ALU.subtract))
            stage(["gexp_ready"], "gsum_ready",
                  lambda g: dve.reduce_sum(small["gate_sum"][:, g], gate["gate_exp"][:, g], AX))
            stage(["gsum_ready"], "ginv_ready",
                  lambda g: dve.reciprocal(small["gate_inv"][:, g], small["gate_sum"][:, g]))
            stage(["ginv_ready"], "share0_ready", lambda g: dve.tensor_tensor(
                gate["gate_share0"][:, g], gate["gate_exp"][:, g], spread(small["gate_inv"][:, g], NE), ALU.mult))
            stage(["share0_ready"], "share_ready", lambda g: dve.tensor_tensor(
                gate["gate_share"][:, g], gate["gate_share0"][:, g], inv_sums[:, g], ALU.mult))
            for u in range(NT):
                g, j = u // GT, u % GT
                dve.wait_ge(s["heads_full"], u + 1)
                dve.wait_ge(s["share_ready"], g + 1)
                if g:
                    if j < GT - 1:
                        dve.wait_ge(s["halves_ready"], (GT - 1) * (g - 1) + j + 1)
                    else:
                        dve.wait_ge(s["mixed_ready"], g)
                share = gate["gate_share"][:, g, NH * j:NH * j + NH, :].rearrange("p n e -> p (n e)")
                dve.tensor_tensor(shared[:, j], banks[u % 4][:].rearrange("p (k d) -> p k d", d=D),
                                  spread(share, D), ALU.mult).then_inc(s["heads_used"], 1)
                if j == GT - 1:
                    dve.wait_ge(s["heads_used"], u + 1)
                    dve.reduce_sum(mixed[:, g, NH * j:NH * j + NH, :],
                                   shared[:, j].rearrange("p (n e) d -> p n d e", n=NH), AX).then_inc(s["mixed_ready"], 1)
            for g in range(NG):
                dve.wait_ge(s["feat_full"], g + 1)
                dve.wait_ge(s["mixed_ready"], g + 1)
                dve.wait_ge(s["pool_mixed"], (GT - 1) * (g + 1))
                dve.tensor_tensor(resid[:, g], pairs(banks[4 + g]), mixed[:, g], ALU.add).then_inc(s["resid_ready"], 1)
            norm(1, lambda g: resid[:, g], "resid_ready", [])
            stage(["fxT_ready"], "nonzero_ready",
                  lambda g: dve.tensor_scalar(nonzero[:, g, :], fxT[:, g, :], 0.0, None, ALU.not_equal))
            stage(["hidden_ready", "nonzero_ready"], "masked_ready2",
                  lambda g: dve.tensor_tensor(hidden_m[:, g, :], hidden[:, g, :], nonzero[:, g, :], ALU.mult))
            stage(["fc2_full"], "fc2_masked", lambda g: dve.scalar_tensor_tensor(
                out=logitsT[:, g, :], in0=banks[g][:], scalar=t["fc_b"][:, 1:2], in1=nonzero[:, g, :],
                op0=ALU.add, op1=ALU.mult))
            stage(["fc2_masked"], "fc_out_ready",
                  lambda g: dve.tensor_tensor(fc_out[:, g, :], logitsT[:, g, :], fxT[:, g, :], ALU.add))
            norm(2, lambda g: pairs(banks[4 + g]), "back_full", ["fxT_full"])
            stage(["normed2_ready"], "scaled2_ready",
                  lambda g: dve.tensor_tensor(scaled[:, g], normed[:, g], each(t["fnorm_g"][:]), ALU.mult))
            stage(["scaled2_ready"], "fout_ready",
                  lambda g: dve.tensor_tensor(fx[:, g], scaled[:, g], each(t["fnorm_b"][:]), ALU.add))
            def ologits(g):
                return banks[4 + g][:, 0:GT * NH].rearrange("p (j n) -> p j n", n=NH)
            stage(["olog_full"], "omax_ready", lambda g: dve.reduce_max(tiny["out_max"][:, g], ologits(g), AX))
            stage(["omax_ready"], "oshift_ready", lambda g: dve.tensor_tensor(
                ogate["out_shift"][:, g], ologits(g), spread(tiny["out_max"][:, g], NH), ALU.subtract))
            stage(["oexp_ready"], "osum_ready", lambda g: dve.reduce_sum(tiny["out_sum"][:, g], ogate["out_exp"][:, g], AX))
            stage(["osum_ready"], "oinv_ready", lambda g: dve.reciprocal(tiny["out_inv"][:, g], tiny["out_sum"][:, g]))
            stage(["oinv_ready"], "oshare_ready", lambda g: dve.tensor_tensor(
                ogate["out_share"][:, g], ogate["out_exp"][:, g], spread(tiny["out_inv"][:, g], NH), ALU.mult))
            stage(["oshare_ready", "fout_ready"], "gated_ready", lambda g: dve.tensor_tensor(
                resid[:, g], fx[:, g],
                spread(ogate["out_share"][:, g].rearrange("p j n -> p (j n)"), D), ALU.mult))
            for g in range(2, NG):
                dve.wait_ge(s["gated_ready"], g + 1)
                add_x1(dve, g).then_inc(s["late_result_ready"], 1)

        @block.gpsimd
        def _(pool):
            for u in range(NT):
                g, j = u // GT, u % GT
                if j == GT - 1:
                    continue
                n = (GT - 1) * g + j
                pool.wait_ge(s["heads_used"], u + 1)
                if g:
                    pool.wait_ge(s["pool_mixed"], n - GT + 2)
                by_expert = shared[:, j].rearrange("p (n e) d -> p n e d", n=NH)
                pool.tensor_tensor(half_sums[:, j], by_expert[:, :, 0:2], by_expert[:, :, 2:4],
                                   ALU.add).then_inc(s["halves_ready"], 1)
                pool.wait_ge(s["halves_ready"], n + 1)
                pool.tensor_tensor(mixed[:, g, NH * j:NH * j + NH, :], half_sums[:, j, :, 0], half_sums[:, j, :, 1],
                                   ALU.add).then_inc(s["pool_mixed"], 1)
            for g in range(2):
                pool.wait_ge(s["gated_ready"], g + 1)
                add_x1(pool, g).then_inc(s["result_ready"], 1)

        @block.sync
        def _(sp):
            for i in range(2):
                sp.wait_ge(t["sums_out"][i], 16 + 8 * NH * NG)
            sp.dma_start(sums_in[:], sum_scratch.rearrange("n e s -> (n e) s")).then_inc(s["sums_in_sem"], 16)
            rows = out.rearrange("(g j p) f -> g p j f", j=GT, p=P)
            for g in range(NG):
                sp.wait_ge(*((s["result_ready"], g + 1) if g < 2 else (s["late_result_ready"], g - 1)))
                sp.dma_start(rows[g], mixed[:, g].rearrange("p (j n) d -> p j (n d)", j=GT)).then_inc(s["result_out"], 16)
            sp.wait_ge(s["result_out"], 16 * NG)


_INS = ['x', 'adj', 'L0_gnn_weight', 'L0_gnn_bias', 'L0_ffn_hl_w', 'L0_ffn_hl_b', 'L0_ffn_wq', 'L0_ffn_wk', 'L0_ffn_wv', 'L0_ffn_gate_w', 'L0_ffn_gate_b', 'L0_ffn_ln_g', 'L0_ffn_ln_b', 'L0_ffn_fc1_w', 'L0_ffn_fc1_b', 'L0_ffn_fc2_w', 'L0_ffn_fc2_b', 'L0_ffn_fnorm_g', 'L0_ffn_fnorm_b', 'L0_ffn_fgate_w']


def kernel(**inputs):
    import numpy as _np
    import concourse.bacc as _bacc
    from concourse import mybir as _mybir
    from concourse.bass_utils import run_bass_kernel_spmd as _run

    nc = _bacc.Bacc("TRN2", target_bir_lowering=False, num_devices=1)
    arrays, args = {}, {}
    for name in _INS:
        a = _np.ascontiguousarray(inputs[name])
        arrays[f"in_{name}_dram"] = a
        args[name.replace("L0_", "")] = nc.dram_tensor(f"in_{name}_dram", a.shape, _mybir.dt.from_np(a.dtype), kind="ExternalInput").ap()
    out = nc.dram_tensor("out_0_dram", (2048, 128), _mybir.dt.float32, kind="ExternalOutput").ap()
    build(nc, args, out)
    r = _run(nc, [arrays], core_ids=[0])
    return r.results[0]["out_0_dram"]
```
